# Optimizing a Trainium2 kernel written in Bass

```python
import numpy as np
import jax
import jax.numpy as jnp

def _softmax(x, axis=-1):
    return jax.nn.softmax(x, axis=axis)

def _gelu(x):
    return jax.nn.gelu(x, approximate=True)

def _silu(x):
    return jax.nn.silu(x)

def _sigmoid(x):
    return jax.nn.sigmoid(x)

def _layernorm(x, axis=-1, eps=1e-05):
    m = jnp.mean(x, axis=axis, keepdims=True)
    v = jnp.var(x, axis=axis, keepdims=True)
    return (x - m) / jnp.sqrt(v + eps)

def _scatter_add(tgt, idx, src, axis=0):
    return tgt.at[idx].add(src)

def _segment_sum(src, seg, n):
    return jax.ops.segment_sum(src, seg, n)
kernel_name = 'mk_macaron_d1_jaxref_r8_b83ca2'

def setup_inputs(seed: int=0):
    np.random.seed(seed)
    _w = jnp.asarray

    def _L0_attn_setup():
        import jax, jax.numpy as jnp
        import numpy as np
        MIN_TIMESCALE = 1.0
        MAX_TIMESCALE = 10000.0

        def llama_rope(x):
            B, S, N, H = x.shape
            half = H // 2
            fraction = 2.0 * jnp.arange(0, half, dtype=jnp.float32) / H
            timescale = MIN_TIMESCALE * (MAX_TIMESCALE / MIN_TIMESCALE) ** fraction
            position = jnp.arange(S, dtype=jnp.float32)[None, :, None, None]
            sinusoid = position / timescale[None, None, None, :]
            sin, cos = (jnp.sin(sinusoid), jnp.cos(sinusoid))
            xr = x.astype(jnp.float32).reshape(B, S, N, half, 2)
            x1, x2 = (xr[..., 0], xr[..., 1])
            r1 = x1 * cos - x2 * sin
            r2 = x2 * cos + x1 * sin
            out = jnp.stack((r1, r2), axis=-1).reshape(B, S, N, H)
            return out.astype(x.dtype)
        key = jax.random.key(seed)
        kx, kq, kk, kv, ko = jax.random.split(key, 5)
        B, S, D, N, H = (4, 256, 256, 16, 128)
        x = jax.random.normal(kx, (B, S, D), dtype=jnp.float32)
        wq = jax.random.normal(kq, (D, N, H), dtype=jnp.float32) / np.sqrt(D)
        wk = jax.random.normal(kk, (D, N, H), dtype=jnp.float32) / np.sqrt(D)
        wv = jax.random.normal(kv, (D, N, H), dtype=jnp.float32) / np.sqrt(D)
        wo = jax.random.normal(ko, (N, H, D), dtype=jnp.float32) / np.sqrt(N * H)
        return {'x': x, 'wq': wq, 'wk': wk, 'wv': wv, 'wo': wo}
    _L0_attn_in = _L0_attn_setup()

    def _L0_ffn_setup():
        import jax, jax.numpy as jnp
        import numpy as np
        NUM_EXPERTS = 8
        TOP_K = 2
        LORA_ALPHA = 2.0
        LORA_RANK = 16
        D_MODEL = 256
        D_HIDDEN = 704
        key = jax.random.key(seed)
        ks = jax.random.split(key, 11)
        B, S, D, H, E, R = (2, 128, D_MODEL, D_HIDDEN, NUM_EXPERTS, LORA_RANK)
        sd = 1.0 / np.sqrt(D)
        sh = 1.0 / np.sqrt(H)
        x = jax.random.normal(ks[0], (B, S, D), jnp.float32)
        gate_w = jax.random.normal(ks[1], (E, D), jnp.float32) * sd
        w_up = jax.random.normal(ks[2], (H, D), jnp.float32) * sd
        w_gate = jax.random.normal(ks[3], (H, D), jnp.float32) * sd
        w_down = jax.random.normal(ks[4], (D, H), jnp.float32) * sh
        up_A = jax.random.normal(ks[5], (E, R, D), jnp.float32) * sd
        up_B = jax.random.normal(ks[6], (E, H, R), jnp.float32) * 0.02
        gate_A = jax.random.normal(ks[7], (E, R, D), jnp.float32) * sd
        gate_B = jax.random.normal(ks[8], (E, H, R), jnp.float32) * 0.02
        down_A = jax.random.normal(ks[9], (E, R, H), jnp.float32) * sh
        down_B = jax.random.normal(ks[10], (E, D, R), jnp.float32) * 0.02
        return {'x': x, 'gate_w': gate_w, 'w_up': w_up, 'w_gate': w_gate, 'w_down': w_down, 'up_A': up_A, 'up_B': up_B, 'gate_A': gate_A, 'gate_B': gate_B, 'down_A': down_A, 'down_B': down_B}
    _L0_ffn_in = _L0_ffn_setup()
    _d = {'L0_attn_x': _L0_attn_in['x'], 'L0_attn_wq': _L0_attn_in['wq'], 'L0_attn_wk': _L0_attn_in['wk'], 'L0_attn_wv': _L0_attn_in['wv'], 'L0_attn_wo': _L0_attn_in['wo'], 'L0_ffn_gate_w': _L0_ffn_in['gate_w'], 'L0_ffn_w_up': _L0_ffn_in['w_up'], 'L0_ffn_w_gate': _L0_ffn_in['w_gate'], 'L0_ffn_w_down': _L0_ffn_in['w_down'], 'L0_ffn_up_A': _L0_ffn_in['up_A'], 'L0_ffn_up_B': _L0_ffn_in['up_B'], 'L0_ffn_gate_A': _L0_ffn_in['gate_A'], 'L0_ffn_gate_B': _L0_ffn_in['gate_B'], 'L0_ffn_down_A': _L0_ffn_in['down_A'], 'L0_ffn_down_B': _L0_ffn_in['down_B']}
    _x0 = _d['L0_attn_x']
    _d['L0_attn_x'] = jax.random.normal(jax.random.fold_in(jax.random.key(seed), 1), (2, 1024, 256), dtype=_x0.dtype)
    del _x0
    return _d

def reference(L0_attn_x, L0_attn_wq, L0_attn_wk, L0_attn_wv, L0_attn_wo, L0_ffn_gate_w, L0_ffn_w_up, L0_ffn_w_gate, L0_ffn_w_down, L0_ffn_up_A, L0_ffn_up_B, L0_ffn_gate_A, L0_ffn_gate_B, L0_ffn_down_A, L0_ffn_down_B):

    def _L0_attn_ref(x, wq, wk, wv, wo):
        import jax, jax.numpy as jnp
        import numpy as np
        MIN_TIMESCALE = 1.0
        MAX_TIMESCALE = 10000.0

        def llama_rope(x):
            B, S, N, H = x.shape
            half = H // 2
            fraction = 2.0 * jnp.arange(0, half, dtype=jnp.float32) / H
            timescale = MIN_TIMESCALE * (MAX_TIMESCALE / MIN_TIMESCALE) ** fraction
            position = jnp.arange(S, dtype=jnp.float32)[None, :, None, None]
            sinusoid = position / timescale[None, None, None, :]
            sin, cos = (jnp.sin(sinusoid), jnp.cos(sinusoid))
            xr = x.astype(jnp.float32).reshape(B, S, N, half, 2)
            x1, x2 = (xr[..., 0], xr[..., 1])
            r1 = x1 * cos - x2 * sin
            r2 = x2 * cos + x1 * sin
            out = jnp.stack((r1, r2), axis=-1).reshape(B, S, N, H)
            return out.astype(x.dtype)
        q = jnp.einsum('bsd,dnh->bsnh', x, wq)
        k = jnp.einsum('bsd,dnh->bsnh', x, wk)
        v = jnp.einsum('bsd,dnh->bsnh', x, wv)
        q = llama_rope(q)
        k = llama_rope(k)
        head_dim = q.shape[-1]
        q = q / jnp.sqrt(jnp.asarray(head_dim, q.dtype))
        S = q.shape[1]
        logits = jnp.einsum('bqnh,bknh->bnqk', q, k)
        causal = jnp.tril(jnp.ones((S, S), dtype=bool))
        logits = jnp.where(causal[None, None, :, :], logits, jnp.asarray(-1e+30, logits.dtype))
        probs = jax.nn.softmax(logits.astype(jnp.float32), axis=-1).astype(v.dtype)
        attn = jnp.einsum('bnqk,bknh->bqnh', probs, v)
        return jnp.einsum('bqnh,nhd->bqd', attn, wo)

    def _L0_ffn_ref(x, gate_w, w_up, w_gate, w_down, up_A, up_B, gate_A, gate_B, down_A, down_B):
        import jax, jax.numpy as jnp
        import numpy as np
        NUM_EXPERTS = 8
        TOP_K = 2
        LORA_ALPHA = 2.0
        LORA_RANK = 16
        D_MODEL = 256
        D_HIDDEN = 704
        B, S, D = x.shape
        H = w_up.shape[0]
        gate_logits = jnp.einsum('bsd,ed->bse', x, gate_w)
        topw, sel = jax.lax.top_k(gate_logits, TOP_K)
        topw = jax.nn.softmax(topw.astype(jnp.float32), axis=1).astype(x.dtype)
        xt = x.reshape(-1, D)
        wf = topw.reshape(-1, TOP_K)
        sf = sel.reshape(-1, TOP_K)
        base_up = xt @ w_up.T
        base_gate = xt @ w_gate.T
        mixed_h = jnp.zeros((xt.shape[0], H), x.dtype)
        lora_down = jnp.zeros_like(xt)
        for e in range(NUM_EXPERTS):
            c = jnp.sum(jnp.where(sf == e, wf, 0.0), axis=1)
            lo_up = LORA_ALPHA * (xt @ up_A[e].T @ up_B[e].T)
            lo_gate = LORA_ALPHA * (xt @ gate_A[e].T @ gate_B[e].T)
            h_e = jax.nn.silu(base_up + lo_up) * (base_gate + lo_gate)
            ch = c[:, None] * h_e
            mixed_h = mixed_h + ch
            lora_down = lora_down + LORA_ALPHA * (ch @ down_A[e].T @ down_B[e].T)
        out = mixed_h @ w_down.T + lora_down
        return out.reshape(B, S, D)
    x = L0_attn_x
    x = x + 0.5 * _L0_ffn_ref(_layernorm(x, axis=-1), L0_ffn_gate_w, L0_ffn_w_up, L0_ffn_w_gate, L0_ffn_w_down, L0_ffn_up_A, L0_ffn_up_B, L0_ffn_gate_A, L0_ffn_gate_B, L0_ffn_down_A, L0_ffn_down_B)
    x = x + _L0_attn_ref(_layernorm(x, axis=-1), L0_attn_wq, L0_attn_wk, L0_attn_wv, L0_attn_wo)
    x = x + 0.5 * _L0_ffn_ref(_layernorm(x, axis=-1), L0_ffn_gate_w, L0_ffn_w_up, L0_ffn_w_gate, L0_ffn_w_down, L0_ffn_up_A, L0_ffn_up_B, L0_ffn_gate_A, L0_ffn_gate_B, L0_ffn_down_A, L0_ffn_down_B)
    return x

_drawn_inputs = setup_inputs


def setup_inputs(seed=0):
    import zlib

    import numpy as np

    out = dict(_drawn_inputs(seed))
    spreads = {}
    factors = {'L0_ffn_gate_w': 8.0,
     'L0_ffn_w_up': 8.0,
     'L0_ffn_w_gate': 8.0,
     'L0_ffn_w_down': 7.872,
     'L0_ffn_up_A': 8.0,
     'L0_ffn_up_B': 8.0,
     'L0_ffn_gate_A': 8.0,
     'L0_ffn_gate_B': 8.0,
     'L0_ffn_down_A': 8.0,
     'L0_ffn_down_B': 8.0}
    for name, (base, spread) in spreads.items():
        noise = np.random.default_rng([zlib.crc32(name.encode()), seed]).standard_normal(out[name].shape)
        drawn = base * np.exp(spread * noise) if base else spread * noise
        out[name] = jnp.asarray(drawn.astype(out[name].dtype))
    for name, factor in factors.items():
        out[name] = (out[name] * factor).astype(out[name].dtype)
    return out
```

```python
from contextlib import ExitStack

import numpy as np
import concourse.bass as bass
from concourse import mybir

ALU = mybir.AluOpType
ACT = mybir.ActivationFunctionType
AX = mybir.AxisListType
F32 = mybir.dt.float32
F32R = mybir.dt.float32r
BF16 = mybir.dt.bfloat16
U32 = mybir.dt.uint32
I32 = mybir.dt.int32
ds = bass.ds

P = 128
BATCH, SEQ, D = 2, 1024, 256
TOKENS = BATCH * SEQ
TILES = TOKENS // P
SEQ_TILES = SEQ // P
KT = D // P
CHUNK = 512
CHUNKS = TOKENS // CHUNK
CT = CHUNK // P
HEADS, HD = 16, 128
PAIRS = HEADS // 2
EXPERTS, RANK, HIDDEN = 8, 16, 704
ER = EXPERTS * RANK
FULL = HIDDEN // P
TAIL = HIDDEN - FULL * P
HT = FULL + 1
ALPHA = 2.0
EPS = 1e-5
SCALE = 1.0 / float(np.sqrt(np.float32(HD)))
MASKED = -1e30
HUGE = 3.0e38

BASE_TILES = 2 * FULL + 1
LORA_TILES = 2 * FULL + 2
OFF_A = 0
OFF_ROUTE = OFF_A + KT * 2 * ER
OFF_BASE = OFF_ROUTE + KT * EXPERTS
OFF_LORA = OFF_BASE + KT * BASE_TILES * P
OFF_DOWN_A = OFF_LORA + LORA_TILES * P
OFF_DOWN = OFF_DOWN_A + HT * ER
OFF_DOWN_B = OFF_DOWN + HT * D
FFN_COLS = OFF_DOWN_B + D
PIECES = 10
PIECE = FFN_COLS // PIECES
assert PIECE * PIECES == FFN_COLS
MASK_ROWS = 4 * EXPERTS
EX_M1, EX_CM1, EX_M2, EX_CM2, EX_C1, EX_C2 = range(6)
EX_COLS = 6 * P
RAW = max(PIECE, EX_COLS)

BU, BG, L0, L1, D1, D2, OUT0, OUT1 = range(8)
T_BANK, PV_BANK, MISC_BANK = 4, 6, 7

UNITS = 4
STEPS = UNITS * SEQ_TILES
DRAIN_STEPS = 4
T_LAG, PV_LAG = 2, 3
GROUPS_AT = [0, 1, 2, 3, 4, 6, 8, 10]
UNIT_GROUPS = 12
KINDS = ["v", "k", "q", "o"]
RAW_OF = {"v": 0, "k": 0, "q": 1, "o": 2}


def tile_groups(i):
    first = 1 - i % 2
    out = []
    while first <= i + 1 - i % 2:
        n = min(4, i + 2 - i % 2 - first)
        out.append((first, n))
        first += n
    return out


def build(nc, x_in, ffn_w, expand_w, attn_w, rope_w, out):
    with ExitStack() as ctx:
        def sem(name):
            return ctx.enter_context(nc.semaphore(name))

        def sbuf(stack, name, shape, dt=F32):
            return stack.enter_context(nc.sbuf_tensor(name, shape, dt))

        x_sb = sbuf(ctx, "x_sb", [P, TILES, D])
        xnT_h = sbuf(ctx, "xnT_h", [P, KT, TOKENS], F32R)
        xnT_l = sbuf(ctx, "xnT_l", [P, KT, TOKENS], F32R)
        ident = sbuf(ctx, "ident", [P, P])
        causal = sbuf(ctx, "causal", [P, SEQ], BF16)
        stats = sbuf(ctx, "stats", [P, CT, 6])
        mean_var = sbuf(ctx, "mean_var", [P, CT, 2])
        var_eps = sbuf(ctx, "var_eps", [P, CT])
        rstd = sbuf(ctx, "rstd", [P, CT])
        minus_half = sbuf(ctx, "minus_half", [P, CT])
        ps = ctx.enter_context(nc.psum_tensor("ps", [P, 8, 512], F32))

        with ExitStack() as st:
            w_h = sbuf(st, "w_h", [P, FFN_COLS], F32R)
            w_l = sbuf(st, "w_l", [P, FFN_COLS], F32R)
            expand = sbuf(st, "expand", [P, 6, P], F32R)
            raw = sbuf(st, "raw", [P, 2, RAW])
            xn = sbuf(st, "xn", [P, CT, D])
            cm = sbuf(st, "cm", [P, TILES, MASK_ROWS])
            cm_pad = sbuf(st, "cm_pad", [P, CT, P])
            maskT_h = sbuf(st, "maskT_h", [P, CHUNK], F32R)
            maskT_l = sbuf(st, "maskT_l", [P, CHUNK], F32R)
            spread = sbuf(st, "spread", [P, 6, CHUNK])
            um_h = sbuf(st, "um_h", [P, 4, CHUNK], F32R)
            um_l = sbuf(st, "um_l", [P, 4, CHUNK], F32R)
            base_up = sbuf(st, "base_up", [P, 2, CHUNK])
            base_gate = sbuf(st, "base_gate", [P, 2, CHUNK])
            up_act = sbuf(st, "up_act", [P, 2, CHUNK])
            hid = sbuf(st, "hid", [P, 2, CHUNK])
            hid_h = sbuf(st, "hid_h", [P, 2, 2, CHUNK], F32R)
            hid_l = sbuf(st, "hid_l", [P, 2, 2, CHUNK], F32R)
            mixed = sbuf(st, "mixed", [P, CHUNK])
            mixed_h = sbuf(st, "mixed_h", [P, 2, CHUNK], F32R)
            mixed_l = sbuf(st, "mixed_l", [P, 2, CHUNK], F32R)
            dm_h = sbuf(st, "dm_h", [P, CHUNK], F32R)
            dm_l = sbuf(st, "dm_l", [P, CHUNK], F32R)
            top8 = sbuf(st, "top8", [P, TILES, 8])
            top_at = sbuf(st, "top_at", [P, TILES, 8], U32)
            top_f = sbuf(st, "top_f", [P, SEQ_TILES, 2])
            expert_i = sbuf(st, "expert_i", [P, EXPERTS], I32)
            expert_f = sbuf(st, "expert_f", [P, EXPERTS])
            part = sbuf(st, "part", [P, 3, 2])
            whole = sbuf(st, "whole", [P, 2, 2])
            route = sbuf(st, "route", [P, SEQ_TILES, 2])

        with ExitStack() as st:
            rope = sbuf(st, "rope", [P, 2, SEQ])
            w_raw = [sbuf(st, f"w_raw{i}", [P, 512]) for i in range(3)]
            wa_h = {k: sbuf(st, f"w{k}_h", [P, 2, 256], F32R) for k in KINDS}
            wa_l = {k: sbuf(st, f"w{k}_l", [P, 2, 256], F32R) for k in KINDS}
            qT_h = sbuf(st, "qT_h", [P, 2, SEQ], F32R)
            qT_l = sbuf(st, "qT_l", [P, 2, SEQ], F32R)
            kT_h = sbuf(st, "kT_h", [P, 2, SEQ], F32R)
            kT_l = sbuf(st, "kT_l", [P, 2, SEQ], F32R)
            v_h = sbuf(st, "v_h", [P, BATCH, SEQ_TILES, 256], F32R)
            v_l = sbuf(st, "v_l", [P, BATCH, SEQ_TILES, 256], F32R)
            pT_h = [sbuf(st, f"pT_h{i}", [P, 6 + 2 * i, 256], F32R) for i in range(2)]
            pT_l = [sbuf(st, f"pT_l{i}", [P, 6 + 2 * i, 256], F32R) for i in range(2)]
            probs = [sbuf(st, f"probs{i}", [P, P * (SEQ_TILES - 3 + i)]) for i in range(4)]
            swapped = sbuf(st, "swapped", [P, 512])
            rot = sbuf(st, "rot", [P, 2, 512])
            rot_sin = sbuf(st, "rot_sin", [P, 512])
            oA_h = sbuf(st, "oA_h", [P, SEQ], F32R)
            oA_l = sbuf(st, "oA_l", [P, SEQ], F32R)
            oB_h = sbuf(st, "oB_h", [P, 2, 256], F32R)
            oB_l = sbuf(st, "oB_l", [P, 2, 256], F32R)
            neg_max = sbuf(st, "neg_max", [P, 4])
            row_sum = sbuf(st, "row_sum", [P, 4])
            inv_sum = sbuf(st, "inv_sum", [P, 4])

        x_loaded = [sem(f"x_loaded{c}") for c in range(CHUNKS)]
        consts_made = sem("consts_made")
        raw_loaded = [sem(f"raw_loaded{i}") for i in range(2)]
        w_high = sem("w_high")
        w_ready = sem("w_ready")
        ln_stats = sem("ln_stats")
        ln_aggr = sem("ln_aggr")
        ln_var = sem("ln_var")
        ln_rstd = sem("ln_rstd")
        xn_ready = sem("xn_ready")
        xn_turned = sem("xn_turned")
        xn_high = sem("xn_high")
        xnT_ready = sem("xnT_ready")
        logits_ready = sem("logits_ready")
        route_chain = sem("route_chain")
        route_whole = sem("route_whole")
        route_exp = sem("route_exp")
        cm_padded = sem("cm_padded")
        mask_turned = sem("mask_turned")
        mask_high = sem("mask_high")
        mask_ready = sem("mask_ready")
        low_rank = sem("low_rank")
        spread_done = sem("spread_done")
        spread_act = sem("spread_act")
        spread_dve = sem("spread_dve")
        um_raw = sem("um_raw")
        um_high = sem("um_high")
        um_ready1 = sem("um_ready1")
        um_ready2 = sem("um_ready2")
        base_done = sem("base_done")
        lora_done = sem("lora_done")
        base_up_kept = sem("base_up_kept")
        base_gate_kept = sem("base_gate_kept")
        up_summed = sem("up_summed")
        up_act_done = sem("up_act_done")
        gate_summed = sem("gate_summed")
        hid_done = sem("hid_done")
        hid_high = sem("hid_high")
        hid_ready = sem("hid_ready")
        mixed_done = sem("mixed_done")
        mixed_high = sem("mixed_high")
        mixed_ready = sem("mixed_ready")
        down_a_done = sem("down_a_done")
        dm_parts = sem("dm_parts")
        dm_raw = sem("dm_raw")
        dm_high = sem("dm_high")
        dm_ready = sem("dm_ready")
        out_done = sem("out_done")
        x_updated = sem("x_updated")
        rope_loaded = sem("rope_loaded")
        wa_loaded = {k: sem(f"w{k}_loaded") for k in KINDS}
        wa_high = {k: sem(f"w{k}_high") for k in KINDS}
        wa_ready = {k: sem(f"w{k}_ready") for k in KINDS}
        zeroed = sem("zeroed")
        proj_done = sem("proj_done")
        proj_swapped = sem("proj_swapped")
        proj_cos = sem("proj_cos")
        proj_sin = sem("proj_sin")
        proj_rot = sem("proj_rot")
        proj_high = sem("proj_high")
        proj_ready = sem("proj_ready")
        v_done = sem("v_done")
        v_high = sem("v_high")
        v_ready = sem("v_ready")
        scores_done = sem("scores_done")
        max_done = sem("max_done")
        exp_done = sem("exp_done")
        inv_done = sem("inv_done")
        probs_ready = sem("probs_ready")
        turned = sem("turned")
        pT_high = sem("pT_high")
        pT_ready = sem("pT_ready")
        pv_done = sem("pv_done")
        o_high = sem("o_high")
        o_ready = sem("o_ready")
        y_done = sem("y_done")
        y_added = sem("y_added")
        stored = sem("stored")

        def need(eng, semaphore, count):
            if not isinstance(count, int) or count > 0:
                eng.wait_ge(semaphore, count)

        def low(eng, dst, src, high):
            return eng.tensor_tensor(dst, src, high.bitcast(F32), ALU.subtract)

        def chunk_tiles(c):
            return x_sb[:, ds(CT * c, CT), :]

        def chunk_cols(c):
            return ds(CHUNK * c, CHUNK)

        def w_a(w, kt, gate):
            at = OFF_A + kt * 2 * ER + gate * ER
            return w[:, at:at + ER]

        def w_route(w, kt):
            at = OFF_ROUTE + kt * EXPERTS
            return w[:, at:at + EXPERTS]

        def w_base(w, kt, tile):
            at = OFF_BASE + (kt * BASE_TILES + tile) * P
            return w[:, at:at + P]

        def w_lora(w, tile):
            at = OFF_LORA + tile * P
            return w[:, at:at + P]

        def w_down_a(w, m):
            at = OFF_DOWN_A + m * ER
            return w[:, at:at + ER]

        def w_down(w, m):
            at = OFF_DOWN + m * D
            return w[:, at:at + D]

        def w_down_b(w):
            return w[:, OFF_DOWN_B:OFF_DOWN_B + D]

        def unit_of(t):
            return t // SEQ_TILES, t % SEQ_TILES

        def tile_at(p, t):
            return (p, t) if t >= 0 else (p - 1, t + STEPS)

        def groups_before(p, t):
            u, i = unit_of(t)
            return UNITS * UNIT_GROUPS * p + UNIT_GROUPS * u + GROUPS_AT[i]

        def groups_through(p, t):
            return groups_before(p, t) + len(tile_groups(t % SEQ_TILES))

        def side_work(p, t, last):
            if t >= STEPS:
                return None
            u, i = unit_of(t)
            k = i // 2
            if i % 2 == 0:
                if u == UNITS - 1 and last:
                    return None
                return "proj", (u + 1) % UNITS, 4 * (UNITS * p + u + 1) + k, k
            if u % 2 == 1:
                if u == UNITS - 1 and last:
                    return None
                return "v", (u // 2 + 1) % 2, 4 * (2 * p + u // 2 + 1) + k, k
            return None

        def chunk_of_step(p, t, first):
            q, s = tile_at(p, t - PV_LAG)
            if s % 2 == 0 or (first and t < PV_LAG) or s >= STEPS:
                return None
            u, i = unit_of(s)
            c = i // 2
            return u, c, 16 * q + 4 * u + c, q, s

        def out_of_step(p, t, first):
            q, s = tile_at(p, t - PV_LAG - 1)
            if s % 2 == 0 or (first and t < PV_LAG + 1) or s >= STEPS:
                return None
            u, i = unit_of(s)
            if u % 2 == 0:
                return None
            return u // 2, i // 2, 4 * (2 * q + u // 2) + i // 2

        def score_view(slot, i):
            n = P * (i + 1)
            if n <= 512:
                return ps[:, 2 * slot:2 * slot + 1, 0:n], 1, n
            return ps[:, 2 * slot:2 * slot + 2, 0:n // 2], 2, n // 2

        block = ctx.enter_context(nc.Block())

        @block.sync
        def _(sp):
            def load_ffn(f):
                for n in range(PIECES + 1):
                    if n >= 2:
                        sp.wait_ge(w_ready, PIECES * f + n - 1)
                    src = ffn_w[:, n * PIECE:(n + 1) * PIECE] if n < PIECES else expand_w
                    sp.dma_start(raw[:, n % 2, 0:src.shape[1]], src).then_inc(raw_loaded[n % 2], 16)

            def load_pair(p):
                need(sp, wa_ready["k"], p)
                sp.dma_start(w_raw[0][:], attn_w[p, 0]).then_inc(wa_loaded["v"], 16)
                need(sp, wa_ready["v"], p + 1)
                sp.dma_start(w_raw[0][:], attn_w[p, 1]).then_inc(wa_loaded["k"], 16)
                need(sp, wa_ready["q"], p)
                sp.dma_start(w_raw[1][:], attn_w[p, 2]).then_inc(wa_loaded["q"], 16)
                need(sp, wa_ready["o"], p)
                sp.dma_start(w_raw[2][:], attn_w[p, 3]).then_inc(wa_loaded["o"], 16)

            x_view = x_in.rearrange("(c t p) d -> c p t d", t=CT, p=P)
            out_view = out.rearrange("(c t p) d -> c p t d", t=CT, p=P)
            for c in range(CHUNKS):
                sp.dma_start(chunk_tiles(c), x_view[c]).then_inc(x_loaded[c], 16)
            load_ffn(0)
            sp.wait_ge(out_done, 2 * CHUNKS)
            sp.dma_start(rope[:], rope_w).then_inc(rope_loaded, 16)
            load_pair(0)
            with sp.Fori(1, PAIRS) as p:
                load_pair(p)
            sp.wait_ge(y_added, 8 * PAIRS)
            load_ffn(1)
            with sp.Fori(0, CHUNKS) as c:
                sp.wait_ge(x_updated, 2 * c + (2 * CHUNKS + 2))
                sp.dma_start(out_view[c], chunk_tiles(c)).then_inc(stored, 16)
            sp.wait_ge(stored, 16 * CHUNKS)

        @block.gpsimd
        def _(pool):
            pool.memset(ident[:], 0.0).then_inc(consts_made, 1)
            pool.memset(causal[:], 0.0).then_inc(consts_made, 1)
            pool.memset(minus_half[:], -0.5).then_inc(consts_made, 1)
            pool.wait_ge(consts_made, 3)
            pool.affine_select(out=ident[:], in_=ident[:], compare_op=ALU.not_equal, fill=1.0, base=0,
                               pattern=[[-1, P]], channel_multiplier=1).then_inc(consts_made, 1)
            pool.affine_select(out=causal[:, SEQ - P:], in_=causal[:, SEQ - P:], compare_op=ALU.is_ge,
                               fill=MASKED, base=0, pattern=[[-1, P]], channel_multiplier=1)\
                .then_inc(consts_made, 1)

            def layer_norm(n):
                pool.wait_ge(ln_var, n + 1)
                pool.tensor_tensor(rstd[:], var_eps[:], minus_half[:], ALU.pow).then_inc(ln_rstd, 1)

            def router(f):
                pool.iota(expert_i[:], pattern=[[1, EXPERTS]], base=0, channel_multiplier=0)\
                    .then_inc(route_whole, 1)
                for b in range(BATCH):
                    k = 2 * f + b
                    pool.wait_ge(route_chain, 10 * k + 4)
                    pool.partition_all_reduce(whole[:, 0, :], part[:, 0, :], P, bass.bass_isa.ReduceOp.max)\
                        .then_inc(route_whole, 1)
                    pool.wait_ge(route_chain, 10 * k + 6)
                    pool.partition_all_reduce(whole[:, 1, :], part[:, 1, :], P, bass.bass_isa.ReduceOp.add)\
                        .then_inc(route_whole, 1)

            def ffn_chunk(g, c, f, first):
                for s in range(2):
                    pool.wait_ge(um_high, 4 * g + 3 + s)
                    if s == 0:
                        need(pool, lora_done, 22 * g)
                    low(pool, um_l[:, 2 + s], (up_act, hid)[s][:, 1], um_h[:, 2 + s])\
                        .then_inc(um_ready2, 1)
                for m in range(HT):
                    rows = P if m < FULL else TAIL
                    for j in range(2):
                        pool.wait_ge(hid_high, 12 * g + 2 * m + j + 1)
                        low(pool, hid_l[0:rows, m % 2, j], hid[0:rows, j], hid_h[0:rows, m % 2, j])\
                            .then_inc(hid_ready, 1)
                    pool.wait_ge(mixed_high, 6 * g + m + 1)
                    low(pool, mixed_l[0:rows, m % 2], mixed[0:rows], mixed_h[0:rows, m % 2])\
                        .then_inc(mixed_ready, 1)
                    if m == 0 and f == 0 and not first:
                        layer_norm(c + 3)

            def ffn(f):
                for c in range(CHUNKS):
                    layer_norm(8 * f + c)
                router(f)
                ffn_chunk(4 * f, 0, f, True)
                with pool.Fori(1, CHUNKS) as c:
                    ffn_chunk(c + 4 * f, c, f, False)
                if f == 0:
                    layer_norm(2 * CHUNKS - 1)

            def rope_sin(index, ch):
                pool.wait_ge(proj_swapped, index + 1)
                need(pool, proj_rot, index)
                pool.tensor_tensor(rot_sin[:], swapped[:], rope[:, 1, 512 * ch:512 * ch + 512], ALU.mult)\
                    .then_inc(proj_sin, 1)

            def rope_low(index, u, k):
                pool.wait_ge(proj_high, index + 1)
                h, l = ((kT_h, kT_l), (qT_h, qT_l))[k % 2]
                cols = slice(512 * (k // 2), 512 * (k // 2) + 512)
                low(pool, l[:, u % 2, cols], rot[:, k % 2], h[:, u % 2, cols]).then_inc(proj_ready, 1)

            def attention(p, first, last):
                for t in range(STEPS + (DRAIN_STEPS if last else 0)):
                    q, s = tile_at(p, t - 1)
                    if s < STEPS and not (first and t == 0):
                        n = P * (s % SEQ_TILES + 1)
                        pool.wait_ge(inv_done, STEPS * q + s + 1)
                        pool.nop(nofuse=True)
                        pool.tensor_scalar(probs[s % 4][:, 0:n], probs[s % 4][:, 0:n], inv_sum[:, s % 4:s % 4 + 1], 1.0,
                                           ALU.mult, ALU.mult).then_inc(probs_ready, 1)
                    side = side_work(p, t, last)
                    if side and side[0] == "proj":
                        rope_sin(side[2], side[3] // 2)
                        rope_low(side[2], side[1], side[3])

            ffn(0)
            pool.wait_ge(xn_turned, KT * 2 * CHUNKS)
            for i in range(2):
                pool.memset(pT_h[i][:, 0, 0:P].bitcast(F32), 0.0)
                last_zero = pool.memset(pT_l[i][:, 0, 0:P].bitcast(F32), 0.0)
            last_zero.then_inc(zeroed, 1)
            pool.wait_ge(rope_loaded, 16)
            for k in range(4):
                rope_sin(k, k // 2)
                rope_low(k, 0, k)
            attention(0, True, False)
            with pool.Fori(1, PAIRS - 1) as p:
                attention(p, False, False)
            attention(PAIRS - 1, False, True)
            ffn(1)

        @block.scalar
        def _(act):
            def split_ffn(f, n):
                act.wait_ge(raw_loaded[n % 2], 16 * ((PIECES // 2 + 1 - n % 2) * f + n // 2 + 1))
                dst = w_h[:, n * PIECE:(n + 1) * PIECE] if n < PIECES else expand[:].rearrange("p a b -> p (a b)")
                act.activation(dst, raw[:, n % 2, 0:dst.shape[1]], ACT.Copy).then_inc(w_high, 1)

            def layer_norm_high(n, c):
                for kt in range(KT):
                    act.wait_ge(xn_turned, KT * n + (kt + 1))
                    act.activation(xnT_h[:, kt, chunk_cols(c)], ps[:, OUT0 + kt, :], ACT.Copy)\
                        .then_inc(xn_high, 1)

            def ffn_chunk(g, c, f, first):
                act.wait_ge(mask_turned, g + 1)
                act.activation(maskT_h[:], ps[:, BU, :], ACT.Copy).then_inc(mask_high, 1)
                for e, bank in ((EX_M1, BG), (EX_M2, D1), (EX_C1, BG), (EX_C2, BU)):
                    act.wait_ge(spread_done, 6 * g + e + 1)
                    act.activation(spread[:, e], ps[:, bank, :], ACT.Copy).then_inc(spread_act, 1)
                for s in range(4):
                    act.wait_ge(um_raw, 4 * g + s + 1)
                    act.activation(um_h[:, s], (up_act, hid)[s % 2][:, s // 2], ACT.Copy).then_inc(um_high, 1)
                for m in range(HT):
                    rows = P if m < FULL else TAIL
                    act.wait_ge(base_done, 11 * g + 2 * m + 1)
                    if m >= 2:
                        act.wait_ge(up_summed, 12 * g + 2 * (m - 1))
                    else:
                        need(act, up_summed, 12 * g)
                    act.activation(base_up[0:rows, m % 2], ps[0:rows, BU, :], ACT.Copy).then_inc(base_up_kept, 1)
                    for j in range(2):
                        act.wait_ge(up_summed, 12 * g + 2 * m + j + 1)
                        act.activation(up_act[0:rows, j], up_act[0:rows, j], ACT.Silu).then_inc(up_act_done, 1)
                        if m == 1 and j == 0 and f == 0 and not first:
                            layer_norm_high(c + 3, c - 1)
                        act.wait_ge(hid_done, 12 * g + 2 * m + j + 1)
                        act.activation(hid_h[0:rows, m % 2, j], hid[0:rows, j], ACT.Copy).then_inc(hid_high, 1)
                    act.wait_ge(mixed_done, 6 * g + m + 1)
                    act.activation(mixed_h[0:rows, m % 2], mixed[0:rows], ACT.Copy).then_inc(mixed_high, 1)
                act.wait_ge(dm_raw, g + 1)
                act.activation(dm_h[:], base_gate[:, 0], ACT.Copy).then_inc(dm_high, 1)

            def ffn(f):
                for c in range(CHUNKS):
                    for n in range(3 * c, min(3 * c + 3, PIECES + 1)):
                        split_ffn(f, n)
                    layer_norm_high(8 * f + c, c)
                for b in range(BATCH):
                    act.wait_ge(route_chain, 10 * (2 * f + b) + 5)
                    act.activation(route[:], route[:], ACT.Exp).then_inc(route_exp, 1)
                ffn_chunk(4 * f, 0, f, True)
                with act.Fori(1, CHUNKS) as c:
                    ffn_chunk(c + 4 * f, c, f, False)
                if f == 0:
                    layer_norm_high(2 * CHUNKS - 1, CHUNKS - 1)

            def split_pair(kind, p):
                act.wait_ge(wa_loaded[kind], 16 * (p + 1))
                if kind in "qk":
                    need(act, proj_done, 16 * p)
                elif kind == "v":
                    need(act, v_done, 8 * p)
                else:
                    need(act, y_done, 8 * p)
                act.activation(wa_h[kind][:].rearrange("p a b -> p (a b)"), w_raw[RAW_OF[kind]][:], ACT.Copy)\
                    .then_inc(wa_high[kind], 1)

            def swap_halves(index):
                act.wait_ge(proj_done, index + 1)
                need(act, proj_sin, index)
                act.activation(swapped[0:64], ps[64:128, MISC_BANK, :], ACT.Copy)
                act.activation(swapped[64:128], ps[0:64, MISC_BANK, :], ACT.Copy).then_inc(proj_swapped, 1)

            def rope_high(index, u, k):
                act.wait_ge(proj_rot, index + 1)
                h = (kT_h, qT_h)[k % 2]
                act.activation(h[:, u % 2, 512 * (k // 2):512 * (k // 2) + 512], rot[:, k % 2], ACT.Copy)\
                    .then_inc(proj_high, 1)

            def value_high(index, b, k):
                act.wait_ge(v_done, index + 1)
                act.activation(v_h[:, b, 2 * k:2 * k + 2, :].rearrange("p a b -> p (a b)"), ps[:, MISC_BANK, :],
                               ACT.Copy).then_inc(v_high, 1)

            def attention(p, first, last):
                for t in range(STEPS + (DRAIN_STEPS if last else 0)):
                    u, i = unit_of(t)
                    if t < STEPS:
                        s_view, a, n = score_view(t % 2, i)
                        act.wait_ge(max_done, STEPS * p + t + 1)
                        if not (first and t < 4):
                            act.wait_ge(turned, groups_through(*tile_at(p, t - 4)))
                        act.activation(probs[t % 4][:, 0:a * n].rearrange("p (a n) -> p a n", a=a), s_view, ACT.Exp,
                                       bias=neg_max[:, t % 4:t % 4 + 1], scale=-1.0,
                                       accum_out=row_sum[:, t % 4:t % 4 + 1]).then_inc(exp_done, 1)
                    side = side_work(p, t, last)
                    if side and side[0] == "proj":
                        swap_halves(side[2])
                    elif side:
                        value_high(side[2], side[1], side[3])
                    if not (first and t < T_LAG) and t - T_LAG < STEPS:
                        q, s = tile_at(p, t - T_LAG)
                        i2 = s % SEQ_TILES
                        half = P * (i2 % 2)
                        for n, (slot, count) in enumerate(tile_groups(i2)):
                            act.wait_ge(turned, groups_before(q, s) + n + 1)
                            bank = T_BANK + (GROUPS_AT[i2] + n) % 2
                            act.activation(pT_h[i2 // 2 % 2][:, slot:slot + count, half:half + P],
                                           ps[:, bank, 0:P * count].rearrange("p (a b) -> p a b", a=count),
                                           ACT.Copy).then_inc(pT_high, 1)
                    if side and side[0] == "proj":
                        rope_high(side[2], side[1], side[3])
                    chunk = chunk_of_step(p, t, first)
                    if chunk:
                        u2, c2, index, _, _ = chunk
                        dst = oA_h[:, 256 * c2:256 * c2 + 256] if u2 % 2 == 0 else oB_h[:, c2 % 2]
                        act.wait_ge(pv_done, index + 1)
                        act.activation(dst, ps[:, PV_BANK, 0:256], ACT.Copy).then_inc(o_high, 1)
                    if t == 4 and not first:
                        split_pair("o", p)
                    if t == 17 and not last:
                        split_pair("v", p + 1)
                    if t == 23 and not last:
                        split_pair("k", p + 1)
                        split_pair("q", p + 1)

            ffn(0)
            for kind in KINDS:
                split_pair(kind, 0)
            for k in range(4):
                swap_halves(k)
                rope_high(k, 0, k)
            for k in range(4):
                value_high(k, 0, k)
            attention(0, True, False)
            with act.Fori(1, PAIRS - 1) as p:
                attention(p, False, False)
            attention(PAIRS - 1, False, True)
            ffn(1)

        @block.vector
        def _(dve):
            def split_ffn(f, n):
                dve.wait_ge(w_high, (PIECES + 1) * f + n + 1)
                at = slice(n * PIECE, (n + 1) * PIECE)
                low(dve, w_l[:, at], raw[:, n % 2, 0:PIECE], w_h[:, at]).then_inc(w_ready, 1)

            def layer_norm(n, c):
                for tt in range(CT):
                    ins = dve.bn_stats(stats[:, tt, :], x_sb[:, ds(CT * c + tt, 1), :].rearrange("p a d -> p (a d)"))
                ins.then_inc(ln_stats, 1)
                dve.wait_ge(ln_stats, n + 1)
                dve.nop(nofuse=True)
                for tt in range(CT):
                    ins = dve.bn_aggr(mean_var[:, tt, :], stats[:, tt, :])
                ins.then_inc(ln_aggr, 1)
                dve.wait_ge(ln_aggr, n + 1)
                dve.tensor_scalar(var_eps[:], mean_var[:, :, 1], EPS, None, ALU.add).then_inc(ln_var, 1)
                dve.wait_ge(ln_rstd, n + 1)
                need(dve, xn_turned, KT * n)
                for tt in range(CT):
                    ins = dve.tensor_scalar(xn[:, tt, :], x_sb[:, ds(CT * c + tt, 1), :].rearrange("p a d -> p (a d)"),
                                            mean_var[:, tt, 0:1], rstd[:, tt:tt + 1], ALU.subtract, ALU.mult)
                ins.then_inc(xn_ready, 1)

            def layer_norm_low(n, c):
                for kt in range(KT):
                    dve.wait_ge(xn_high, KT * n + (kt + 1))
                    low(dve, xnT_l[:, kt, chunk_cols(c)], ps[:, OUT0 + kt, :], xnT_h[:, kt, chunk_cols(c)])\
                        .then_inc(xnT_ready, 1)

            def router(f, b):
                k = 2 * f + b
                steps = [10 * k]

                def link(ins):
                    steps[0] += 1
                    ins.then_inc(route_chain, 1)
                    dve.wait_ge(route_chain, steps[0])

                tiles = range(b * SEQ_TILES, (b + 1) * SEQ_TILES)
                mine = slice(b * SEQ_TILES, (b + 1) * SEQ_TILES)
                dve.wait_ge(logits_ready, k + 1)
                for tile in tiles:
                    ins = dve.max(top8[:, tile, :], ps[:, D1 + b, EXPERTS * tile:EXPERTS * tile + EXPERTS])
                link(ins)
                for tile in tiles:
                    ins = dve.max_index(top_at[:, tile, :], top8[:, tile, :],
                                        ps[:, D1 + b, EXPERTS * tile:EXPERTS * tile + EXPERTS])
                link(ins)
                dve.wait_ge(route_whole, 5 * f + 1)
                dve.tensor_copy(expert_f[:], expert_i[:])
                link(dve.tensor_copy(top_f[:], top_at[:, mine, 0:2]))
                link(dve.tensor_reduce(part[:, 0, :], top8[:, mine, 0:2].rearrange("p t j -> p j t"), AX.X, ALU.max))
                dve.wait_ge(route_whole, 5 * f + 2 * b + 2)
                link(dve.tensor_tensor(route[:], top8[:, mine, 0:2],
                                       whole[:, None, 0, :].to_broadcast([P, SEQ_TILES, 2]), ALU.subtract))
                dve.wait_ge(route_exp, k + 1)
                link(dve.tensor_reduce(part[:, 1, :], route[:].rearrange("p t j -> p j t"), AX.X, ALU.add))
                for j in range(2):
                    ins = dve.tensor_tensor(cm[:, mine, EXPERTS * j:EXPERTS * j + EXPERTS],
                                            expert_f[:, None, :].to_broadcast([P, SEQ_TILES, EXPERTS]),
                                            top_f[:, :, j:j + 1].to_broadcast([P, SEQ_TILES, EXPERTS]), ALU.is_equal)
                link(ins)
                dve.wait_ge(route_whole, 5 * f + 2 * b + 3)
                link(dve.reciprocal(part[:, 2, :], whole[:, 1, :]))
                link(dve.tensor_tensor(route[:], route[:], part[:, None, 2, :].to_broadcast([P, SEQ_TILES, 2]), ALU.mult))
                for j in range(2):
                    ins = dve.tensor_tensor(cm[:, mine, EXPERTS * (2 + j):EXPERTS * (3 + j)],
                                            cm[:, mine, EXPERTS * j:EXPERTS * j + EXPERTS],
                                            route[:, :, j:j + 1].to_broadcast([P, SEQ_TILES, EXPERTS]), ALU.mult)
                link(ins)

            def update_x(g, c, f):
                for k in range(2):
                    dve.wait_ge(out_done, 2 * g + (k + 1))
                    tiles = x_sb[:, ds(CT * c + 2 * k, 2), :].rearrange("p a d -> p (a d)")
                    dve.scalar_tensor_tensor(out=tiles, in0=ps[:, OUT0 + k, :], scalar=0.5, in1=tiles,
                                             op0=ALU.mult, op1=ALU.add).then_inc(x_updated, 1)

            def ffn_chunk(g, c, f, first):
                need(dve, mask_turned, g)
                dve.tensor_copy(cm_pad[:, :, 0:MASK_ROWS], cm[:, ds(CT * c, CT), :]).then_inc(cm_padded, 1)
                dve.wait_ge(mask_high, g + 1)
                low(dve, maskT_l[:], ps[:, BU, :], maskT_h[:]).then_inc(mask_ready, 1)
                if not first:
                    update_x(g - 1, c - 1, f)
                for e, bank in ((EX_CM1, BU), (EX_CM2, D2)):
                    dve.wait_ge(spread_done, 6 * g + e + 1)
                    dve.tensor_copy(spread[:, e], ps[:, bank, :]).then_inc(spread_dve, 1)
                dve.wait_ge(low_rank, 2 * g + 2)
                dve.wait_ge(spread_dve, 2 * g + 2)
                dve.wait_ge(spread_act, 4 * g + 2)
                for s, (bank, e) in enumerate(((L0, EX_M1), (L1, EX_CM1), (L0, EX_M2), (L1, EX_CM2))):
                    dst = (up_act, hid)[s % 2][:, s // 2]
                    dve.tensor_tensor(dst, ps[:, bank, :], spread[:, e], ALU.mult).then_inc(um_raw, 1)
                for s in range(2):
                    dve.wait_ge(um_high, 4 * g + s + 1)
                    low(dve, um_l[:, s], (up_act, hid)[s][:, 0], um_h[:, s]).then_inc(um_ready1, 1)
                for m in range(HT):
                    rows = P if m < FULL else TAIL
                    dve.wait_ge(base_done, 11 * g + min(2 * m + 2, 11))
                    dve.wait_ge(spread_act, 4 * g + 4)
                    for j in range(2):
                        if m < FULL:
                            src, c_j = ps[:, BG, :], spread[:, EX_C1 + j]
                        else:
                            src, c_j = ps[TAIL:2 * TAIL, BU, :], spread[TAIL:2 * TAIL, EX_C1 + j]
                        dve.tensor_tensor(base_gate[0:rows, j], src, c_j, ALU.mult).then_inc(base_gate_kept, 1)
                    dve.wait_ge(base_up_kept, 6 * g + m + 1)
                    for j in range(2):
                        if m == 0 and j == 1:
                            dve.wait_ge(um_ready2, 2 * g + 2)
                        if m < FULL:
                            up_src, gate_src, n = ps[:, L0, :], ps[:, L1, :], 22 * g + 4 * m + 2 * j + 1
                        else:
                            up_src, gate_src, n = ps[0:TAIL, L0 + j, :], ps[TAIL:2 * TAIL, L0 + j, :], 22 * g + 21 + j
                        dve.wait_ge(lora_done, n)
                        dve.tensor_tensor(up_act[0:rows, j], up_src, base_up[0:rows, m % 2], ALU.add).then_inc(up_summed, 1)
                        if m < FULL:
                            dve.wait_ge(lora_done, n + 1)
                        dve.wait_ge(base_gate_kept, 12 * g + 2 * m + j + 1)
                        need(dve, hid_ready, 12 * g + 2 * m + j - 1)
                        if m > 0:
                            dve.wait_ge(mixed_done, 6 * g + m)
                        dve.tensor_tensor(hid[0:rows, j], gate_src, base_gate[0:rows, j], ALU.add).then_inc(gate_summed, 1)
                        dve.wait_ge(up_act_done, 12 * g + 2 * m + j + 1)
                        dve.wait_ge(gate_summed, 12 * g + 2 * m + j + 1)
                        dve.tensor_tensor(hid[0:rows, j], up_act[0:rows, j], hid[0:rows, j], ALU.mult).then_inc(hid_done, 1)
                        if m == 1 and j == 0 and f == 0 and not first:
                            layer_norm_low(c + 3, c - 1)
                    need(dve, mixed_ready, 6 * g + m)
                    dve.wait_ge(hid_done, 12 * g + 2 * m + 2)
                    dve.tensor_tensor(mixed[0:rows], hid[0:rows, 0], hid[0:rows, 1], ALU.add).then_inc(mixed_done, 1)
                    if m == 0 and f == 0 and not first:
                        dve.wait_ge(x_updated, 2 * g)
                        dve.nop(nofuse=True)
                        layer_norm(c + 3, c - 1)
                dve.wait_ge(down_a_done, g + 1)
                for j in range(2):
                    ins = dve.tensor_tensor(base_gate[:, j], ps[:, D1 + j, :], spread[:, (EX_M1, EX_M2)[j]], ALU.mult)
                ins.then_inc(dm_parts, 1)
                dve.wait_ge(dm_parts, g + 1)
                dve.tensor_tensor(base_gate[:, 0], base_gate[:, 0], base_gate[:, 1], ALU.add).then_inc(dm_raw, 1)
                dve.wait_ge(dm_high, g + 1)
                low(dve, dm_l[:], base_gate[:, 0], dm_h[:]).then_inc(dm_ready, 1)

            def ffn(f):
                dve.memset(cm_pad[:], 0.0)
                for c in range(CHUNKS):
                    if f == 0:
                        dve.wait_ge(x_loaded[c], 16)
                        if c == 0:
                            dve.wait_ge(consts_made, 5)
                    elif c == 0:
                        dve.wait_ge(y_added, 8 * PAIRS)
                    layer_norm(8 * f + c, c)
                    for n in range(3 * c, min(3 * c + 3, PIECES)):
                        split_ffn(f, n)
                    layer_norm_low(8 * f + c, c)
                for b in range(BATCH):
                    router(f, b)
                ffn_chunk(4 * f, 0, f, True)
                with dve.Fori(1, CHUNKS) as c:
                    ffn_chunk(c + 4 * f, c, f, False)
                update_x(4 * f + 3, CHUNKS - 1, f)
                if f == 0:
                    dve.wait_ge(x_updated, 2 * CHUNKS)
                    layer_norm(2 * CHUNKS - 1, CHUNKS - 1)
                    layer_norm_low(2 * CHUNKS - 1, CHUNKS - 1)

            def split_pair(kind, p):
                dve.wait_ge(wa_high[kind], p + 1)
                low(dve, wa_l[kind][:].rearrange("p a b -> p (a b)"), w_raw[RAW_OF[kind]][:],
                    wa_h[kind][:].rearrange("p a b -> p (a b)")).then_inc(wa_ready[kind], 1)

            def rope_cos(index, k):
                dve.wait_ge(proj_swapped, index + 1)
                need(dve, proj_ready, index - 1)
                dve.tensor_tensor(rot[:, k % 2], ps[:, MISC_BANK, :], rope[:, 0, 512 * (k // 2):512 * (k // 2) + 512],
                                  ALU.mult).then_inc(proj_cos, 1)

            def rope_sum(index, k):
                dve.wait_ge(proj_cos, index + 1)
                dve.wait_ge(proj_sin, index + 1)
                dve.tensor_tensor(rot[:, k % 2], rot[:, k % 2], rot_sin[:], ALU.add).then_inc(proj_rot, 1)

            def value_low(index, b, k):
                dve.wait_ge(v_high, index + 1)
                low(dve, v_l[:, b, 2 * k:2 * k + 2, :].rearrange("p a b -> p (a b)"), ps[:, MISC_BANK, :],
                    v_h[:, b, 2 * k:2 * k + 2, :].rearrange("p a b -> p (a b)")).then_inc(v_ready, 1)

            def attention(p, first, last):
                for t in range(STEPS + (DRAIN_STEPS if last else 0)):
                    u, i = unit_of(t)
                    if not (first and t == 0) and t - 1 < STEPS:
                        q, s = tile_at(p, t - 1)
                        dve.wait_ge(exp_done, STEPS * q + s + 1)
                        dve.reciprocal(inv_sum[:, s % 4:s % 4 + 1], row_sum[:, s % 4:s % 4 + 1]).then_inc(inv_done, 1)
                    if t < STEPS:
                        s_view, a, n = score_view(t % 2, i)
                        dve.wait_ge(scores_done, STEPS * p + t + 1)
                        dve.nop(nofuse=True)
                        dve.tensor_tensor_reduce(out=s_view, in0=s_view,
                                                 in1=causal[:, SEQ - a * n:].rearrange("p (a n) -> p a n", a=a),
                                                 scale=-SCALE, scalar=HUGE, op0=ALU.add, op1=ALU.min,
                                                 accum_out=neg_max[:, t % 4:t % 4 + 1]).then_inc(max_done, 1)
                    side = side_work(p, t, last)
                    if side and side[0] == "proj":
                        rope_cos(side[2], side[3])
                    elif side:
                        value_low(side[2], side[1], side[3])
                    if not (first and t < T_LAG) and t - T_LAG < STEPS:
                        q, s = tile_at(p, t - T_LAG)
                        i2 = s % SEQ_TILES
                        half = P * (i2 % 2)
                        for n, (slot, count) in enumerate(tile_groups(i2)):
                            dve.wait_ge(pT_high, groups_before(q, s) + n + 1)
                            bank = T_BANK + (GROUPS_AT[i2] + n) % 2
                            low(dve, pT_l[i2 // 2 % 2][:, slot:slot + count, half:half + P],
                                ps[:, bank, 0:P * count].rearrange("p (a b) -> p a b", a=count),
                                pT_h[i2 // 2 % 2][:, slot:slot + count, half:half + P]).then_inc(pT_ready, 1)
                    if side and side[0] == "proj":
                        rope_sum(side[2], side[3])
                    chunk = chunk_of_step(p, t, first)
                    if chunk:
                        u2, c2, index, _, _ = chunk
                        h, l = ((oA_h[:, 256 * c2:256 * c2 + 256], oA_l[:, 256 * c2:256 * c2 + 256]) if u2 % 2 == 0
                                else (oB_h[:, c2 % 2], oB_l[:, c2 % 2]))
                        dve.wait_ge(o_high, index + 1)
                        low(dve, l, ps[:, PV_BANK, 0:256], h).then_inc(o_ready, 1)
                    y = out_of_step(p, t, first)
                    if y:
                        b, c, index = y
                        tiles = x_sb[:, SEQ_TILES * b + 2 * c:SEQ_TILES * b + 2 * c + 2, :].rearrange("p a d -> p (a d)")
                        dve.wait_ge(y_done, index + 1)
                        need(dve, y_added, index - 3)
                        dve.tensor_tensor(tiles, ps[:, MISC_BANK, :], tiles, ALU.add).then_inc(y_added, 1)
                    if t == 4 and not first:
                        split_pair("o", p)
                    if t == 17 and not last:
                        split_pair("v", p + 1)
                    if t == 23 and not last:
                        split_pair("k", p + 1)
                        split_pair("q", p + 1)

            ffn(0)
            for kind in KINDS:
                split_pair(kind, 0)
            dve.wait_ge(rope_loaded, 16)
            for k in range(4):
                rope_cos(k, k)
                rope_sum(k, k)
            for k in range(4):
                value_low(k, 0, k)
            attention(0, True, False)
            with dve.Fori(1, PAIRS - 1) as p:
                attention(p, False, False)
            attention(PAIRS - 1, False, True)
            ffn(1)

        @block.tensor
        def _(pe):
            def product(dst, w, x, start, stop, skip=False):
                pe.matmul(dst, w[0], x[0], start=start, stop=False, skip_group_check=skip)
                pe.matmul(dst, w[0], x[1], start=False, stop=False, skip_group_check=skip)
                return pe.matmul(dst, w[1], x[0], start=False, stop=stop, skip_group_check=skip)

            def xnT(kt, cols):
                return xnT_h[:, kt, cols], xnT_l[:, kt, cols]

            def layer_norm(n):
                pe.wait_ge(xn_ready, n + 1)
                for kt in range(KT):
                    need(pe, xnT_ready, KT * n - (KT - 1) + kt)
                    for tt in range(CT):
                        ins = pe.transpose(ps[:, OUT0 + kt, P * tt:P * tt + P], xn[:, tt, P * kt:P * kt + P], ident[:])
                    ins.then_inc(xn_turned, 1)

            def router(f, b):
                pe.wait_ge(xnT_ready, KT * (8 * f + 2 * b + 2))
                pe.wait_ge(w_ready, PIECES * f + 1)
                for tile in range(b * SEQ_TILES, (b + 1) * SEQ_TILES):
                    dst = ps[:, D1 + b, EXPERTS * tile:EXPERTS * tile + EXPERTS]
                    cols = slice(P * tile, P * tile + P)
                    for kt in range(KT):
                        product(dst, xnT(kt, cols), (w_route(w_h, kt), w_route(w_l, kt)), kt == 0, False)
                        ins = pe.matmul(dst, xnT_l[:, kt, cols], w_route(w_l, kt), start=False, stop=(kt == KT - 1))
                ins.then_inc(logits_ready, 1)

            def down_b(g):
                pe.wait_ge(dm_ready, g + 1)
                for tt in range(CT):
                    cols = slice(P * tt, P * tt + P)
                    ins = product(ps[:, OUT0 + tt // 2, D * (tt % 2):D * (tt % 2) + D], (dm_h[:, cols], dm_l[:, cols]),
                                  (w_down_b(w_h), w_down_b(w_l)), False, True, skip=True)
                    if tt % 2 == 1:
                        ins.then_inc(out_done, 1)

            def ffn_chunk(g, c, f, first):
                cols = chunk_cols(c)
                need(pe, up_summed, 12 * g)
                need(pe, gate_summed, 12 * g)
                for gate in range(2):
                    for kt in range(KT):
                        ins = product(ps[:, L0 + gate, :], (w_a(w_h, kt, gate), w_a(w_l, kt, gate)), xnT(kt, cols),
                                      kt == 0, kt == KT - 1)
                    ins.then_inc(low_rank, 1)
                pe.wait_ge(cm_padded, g + 1)
                need(pe, base_up_kept, 6 * g)
                need(pe, base_gate_kept, 12 * g)
                for tt in range(CT):
                    ins = pe.transpose(ps[:, BU, P * tt:P * tt + P], cm_pad[:, tt, :], ident[:])
                ins.then_inc(mask_turned, 1)
                if not first:
                    down_b(g - 1)
                pe.wait_ge(mask_ready, g + 1)
                for e, bank in ((EX_M1, BG), (EX_CM1, BU), (EX_M2, D1), (EX_CM2, D2), (EX_C1, BG), (EX_C2, BU)):
                    if e == EX_C1:
                        pe.wait_ge(spread_act, 4 * g + 1)
                    if e == EX_C2:
                        pe.wait_ge(spread_dve, 2 * g + 1)
                    pe.matmul(ps[:, bank, :], expand[:, e], maskT_h[:], start=True, stop=False)
                    pe.matmul(ps[:, bank, :], expand[:, e], maskT_l[:], start=False, stop=True).then_inc(spread_done, 1)

                def base(bank, tile):
                    for kt in range(KT):
                        ins = product(ps[:, bank, :], (w_base(w_h, kt, tile), w_base(w_l, kt, tile)), xnT(kt, cols),
                                      kt == 0, kt == KT - 1)
                    ins.then_inc(base_done, 1)

                def lora(bank, tile, s, start=True, stop=True):
                    return product(ps[:, bank, :], (w_lora(w_h, tile), w_lora(w_l, tile)), (um_h[:, s], um_l[:, s]), start, stop)

                def down_a(m, j):
                    pe.wait_ge(hid_ready, 12 * g + 2 * m + j + 1)
                    if m == 0 and j == 0:
                        pe.wait_ge(spread_act, 4 * g + 2)
                    elif m == 0:
                        pe.wait_ge(spread_dve, 2 * g + 2)
                    return product(ps[:, D1 + j, :], (w_down_a(w_h, m), w_down_a(w_l, m)),
                                   (hid_h[:, m % 2, j], hid_l[:, m % 2, j]), m == 0, m == HT - 1)

                def down(m):
                    pe.wait_ge(mixed_ready, 6 * g + m + 1)
                    if m == 0:
                        if f == 0:
                            pe.wait_ge(xnT_ready, KT * CHUNKS if first else KT * (c + 4))
                        elif first:
                            pe.wait_ge(xnT_ready, 3 * KT * CHUNKS)
                        else:
                            pe.wait_ge(x_updated, 2 * g)
                    for tt in range(CT):
                        tok = slice(P * tt, P * tt + P)
                        product(ps[:, OUT0 + tt // 2, D * (tt % 2):D * (tt % 2) + D],
                                (mixed_h[:, m % 2, tok], mixed_l[:, m % 2, tok]),
                                (w_down(w_h, m), w_down(w_l, m)), m == 0 and tt % 2 == 0, False, skip=True)

                for m in range(HT):
                    if m == 0:
                        pe.wait_ge(spread_act, 4 * g + 4)
                    else:
                        pe.wait_ge(base_up_kept, 6 * g + m)
                    if m < FULL:
                        base(BU, m)
                        if m > 0:
                            pe.wait_ge(base_gate_kept, 12 * g + 2 * m)
                        base(BG, FULL + m)
                        for j in range(2):
                            if m == 0:
                                pe.wait_ge((um_ready1, um_ready2)[j], 2 * g + 2)
                                if j == 0:
                                    pe.wait_ge(um_raw, 4 * g + 4)
                            if m > 0 or j > 0:
                                pe.wait_ge(up_summed, 12 * g + 2 * m + j)
                            lora(L0, m, 2 * j).then_inc(lora_done, 1)
                            if m > 0 or j > 0:
                                pe.wait_ge(gate_summed, 12 * g + 2 * m + j)
                            lora(L1, FULL + m, 2 * j + 1).then_inc(lora_done, 1)
                            if m == 1 and j == 0 and f == 0 and not first:
                                layer_norm(c + 3)
                            if m > 0:
                                down_a(m - 1, j)
                    else:
                        base(BU, 2 * FULL)
                        for j in range(2):
                            pe.wait_ge((up_summed, gate_summed)[j], 12 * g + 2 * m)
                            lora(L0 + j, 2 * FULL, 2 * j, True, False)
                            lora(L0 + j, 2 * FULL + 1, 2 * j + 1, False, True).then_inc(lora_done, 1)
                            down_a(m - 1, j)
                    if m > 0:
                        down(m - 1)
                down_a(HT - 1, 0)
                down_a(HT - 1, 1).then_inc(down_a_done, 1)
                down(HT - 1)

            def ffn(f):
                if f == 0:
                    pe.wait_ge(consts_made, 5)
                for c in range(CHUNKS):
                    layer_norm(8 * f + c)
                for b in range(BATCH):
                    router(f, b)
                pe.wait_ge(w_ready, PIECES * (f + 1))
                pe.wait_ge(w_high, (PIECES + 1) * (f + 1))
                ffn_chunk(4 * f, 0, f, True)
                with pe.Fori(1, CHUNKS) as c:
                    ffn_chunk(c + 4 * f, c, f, False)
                down_b(4 * f + 3)
                if f == 0:
                    layer_norm(2 * CHUNKS - 1)

            bank_user = [None]

            def misc_bank_free():
                if bank_user[0]:
                    kind, index = bank_user[0]
                    pe.wait_ge({"proj": proj_cos, "v": v_ready, "o": y_added}[kind], index + 1)

            def project(index, u, k):
                kind = "kq"[k % 2]
                h, l = wa_h[kind], wa_l[kind]
                head, b, at = u % 2, u // 2, 512 * (k // 2)
                cols = slice(SEQ * b + at, SEQ * b + at + 512)
                misc_bank_free()
                for kt in range(KT):
                    w = (h[:, kt, HD * head:HD * head + HD], l[:, kt, HD * head:HD * head + HD])
                    ins = product(ps[:, MISC_BANK, :], w, xnT(kt, cols), kt == 0, kt == KT - 1)
                ins.then_inc(proj_done, 1)
                bank_user[0] = "proj", index

            def values(index, b, k):
                misc_bank_free()
                for half in range(2):
                    tok = SEQ * b + P * (2 * k + half)
                    for kt in range(KT):
                        ins = product(ps[:, MISC_BANK, 256 * half:256 * half + 256], xnT(kt, slice(tok, tok + P)),
                                      (wa_h["v"][:, kt, :], wa_l["v"][:, kt, :]), kt == 0, kt == KT - 1)
                ins.then_inc(v_done, 1)
                bank_user[0] = "v", index

            def side(p, t, last):
                work = side_work(p, t, last)
                if not work:
                    return
                kind, what, index, k = work
                if kind == "proj":
                    if t >= STEPS - SEQ_TILES and k < 2:
                        pe.wait_ge(wa_ready["kq"[k % 2]], p + 2)
                    project(index, what, k)
                else:
                    if t >= STEPS - SEQ_TILES and k == 0:
                        pe.wait_ge(wa_ready["v"], p + 2)
                    values(index, what, k)

            def scores(p, t, first):
                u, i = unit_of(t)
                view, a, n = score_view(t % 2, i)
                if not (first and t < 2):
                    pe.wait_ge(exp_done, STEPS * p + t - 1)
                if i % 4 == 0:
                    pe.wait_ge(proj_ready, 4 * (UNITS * p + u) + 2 + i // 2)
                for part_at in range(a):
                    cols = max(n, 256)
                    dst = ps[:, 2 * (t % 2) + part_at, 0:cols]
                    keys = slice(n * part_at, n * part_at + cols)
                    rows = slice(P * i, P * i + P)
                    ins = product(dst, (qT_h[:, u % 2, rows], qT_l[:, u % 2, rows]),
                                  (kT_h[:, u % 2, keys], kT_l[:, u % 2, keys]), True, True)
                ins.then_inc(scores_done, 1)

            def turn(q, s):
                i = s % SEQ_TILES
                pe.wait_ge(probs_ready, STEPS * q + s + 1)
                for n, (slot, count) in enumerate(tile_groups(i)):
                    need(pe, pT_ready, groups_before(q, s) + n - 1)
                    bank = T_BANK + (GROUPS_AT[i] + n) % 2
                    for k in range(count):
                        kt = 2 * (i // 2) + 1 - (slot + k)
                        ins = pe.transpose(ps[:, bank, P * k:P * k + P], probs[s % 4][:, P * kt:P * kt + P], ident[:])
                    ins.then_inc(turned, 1)

            def weigh(u, c, index, q, s, first_unit):
                pe.wait_ge(pT_ready, groups_through(q, s))
                need(pe, o_ready, index)
                if c == 0 and u % 2 == 0:
                    pe.wait_ge(v_ready, 4 * (2 * q + u // 2) + 4)
                if first_unit and c == 0:
                    pe.wait_ge(zeroed, 1)
                head, b = u % 2, u // 2
                slots = 2 * c + 2
                for slot in range(slots):
                    kt = 2 * c + 1 - slot
                    w = tuple(v[:, b, kt, HD * head:HD * head + HD] for v in (v_h, v_l))
                    ins = product(ps[:, PV_BANK, 0:256], w, (pT_h[c % 2][:, slot, :], pT_l[c % 2][:, slot, :]),
                                  slot == 0, slot == slots - 1)
                ins.then_inc(pv_done, 1)

            def project_out(b, c, index, q):
                if c == 0 and b == 0:
                    pe.wait_ge(wa_ready["o"], q + 1)
                pe.wait_ge(o_ready, 16 * q + 8 * b + 4 + c + 1)
                misc_bank_free()
                for half in range(2):
                    at = slice(256 * c + P * half, 256 * c + P * half + P)
                    for head in range(2):
                        o = ((oA_h[:, at], oA_l[:, at]) if head == 0 else
                             tuple(v[:, c % 2, P * half:P * half + P] for v in (oB_h, oB_l)))
                        ins = product(ps[:, MISC_BANK, 256 * half:256 * half + 256], o,
                                      (wa_h["o"][:, head, :], wa_l["o"][:, head, :]), head == 0, head == 1)
                ins.then_inc(y_done, 1)
                bank_user[0] = "o", index

            def attention(p, first, last):
                if not first:
                    bank_user[0] = "o", 8 * p - 3
                for t in range(STEPS + (DRAIN_STEPS if last else 0)):
                    if t < STEPS:
                        scores(p, t, first)
                    side(p, t, last)
                    if not (first and t < T_LAG) and t - T_LAG < STEPS:
                        turn(*tile_at(p, t - T_LAG))
                    chunk = chunk_of_step(p, t, first)
                    if chunk:
                        weigh(*chunk, first and t < SEQ_TILES)
                    y = out_of_step(p, t, first)
                    if y:
                        q, _ = tile_at(p, t - PV_LAG - 1)
                        project_out(*y, q)

            ffn(0)
            pe.wait_ge(xnT_ready, KT * 2 * CHUNKS)
            for kind in "kq":
                pe.wait_ge(wa_ready[kind], 1)
            for k in range(4):
                project(k, 0, k)
            pe.wait_ge(wa_ready["v"], 1)
            for k in range(4):
                values(k, 0, k)
            attention(0, True, False)
            with pe.Fori(1, PAIRS - 1) as p:
                attention(p, False, False)
            attention(PAIRS - 1, False, True)
            ffn(1)


def pack_ffn(gate_w, w_up, w_gate, w_down, up_A, up_B, gate_A, gate_B, down_A, down_B):
    def by_kt(a):
        return a.reshape(KT, P, -1).transpose(1, 0, 2)

    def padded(a):
        full = np.zeros((HT * P, a.shape[1]), a.dtype)
        full[:HIDDEN] = a
        return full.reshape(HT, P, -1).transpose(1, 0, 2)

    cut = FULL * P
    a = np.concatenate([up_A.reshape(ER, D).T, gate_A.reshape(ER, D).T], axis=1)
    up, gate = w_up.T, w_gate.T
    base = np.concatenate([up[:, :cut], gate[:, :cut], up[:, cut:], gate[:, cut:]], axis=1)
    up_b = up_B.transpose(0, 2, 1).reshape(ER, HIDDEN)
    gate_b = gate_B.transpose(0, 2, 1).reshape(ER, HIDDEN)
    none = np.zeros((ER, TAIL), up_b.dtype)
    lora = np.concatenate([up_b[:, :cut], gate_b[:, :cut], up_b[:, cut:], none, none, gate_b[:, cut:]], axis=1)
    parts = [by_kt(a), by_kt(gate_w.T), by_kt(base), lora, padded(down_A.reshape(ER, HIDDEN).T),
             padded(w_down.T), down_B.transpose(0, 2, 1).reshape(ER, D)]
    return np.ascontiguousarray(np.concatenate([v.reshape(P, -1) for v in parts], axis=1))


def expand_matrices():
    m = np.zeros((P, 6, P), np.float32)
    for e in range(EXPERTS):
        ranks = slice(RANK * e, RANK * e + RANK)
        m[e, EX_M1, ranks] = ALPHA
        m[EXPERTS + e, EX_M2, ranks] = ALPHA
        m[2 * EXPERTS + e, EX_CM1, ranks] = ALPHA
        m[3 * EXPERTS + e, EX_CM2, ranks] = ALPHA
        m[2 * EXPERTS + e, EX_C1, :] = 1.0
        m[3 * EXPERTS + e, EX_C2, :] = 1.0
    return m.reshape(P, EX_COLS)


def rope_tables():
    half = HD // 2
    fraction = np.float32(2.0) * np.arange(half, dtype=np.float32) / np.float32(HD)
    timescale = np.float32(10000.0) ** fraction
    angle = np.arange(SEQ, dtype=np.float32)[None, :] / timescale[:, None].astype(np.float32)
    sin, cos = np.sin(angle), np.cos(angle)
    table = np.stack([np.concatenate([cos, cos]), np.concatenate([-sin, sin])], axis=1)
    return np.ascontiguousarray(table.astype(np.float32))


def pack_attention(wq, wk, wv, wo):
    order = np.concatenate([np.arange(0, HD, 2), np.arange(1, HD, 2)])

    def by_pair(w):
        w = w.reshape(KT, P, PAIRS, 2, HD).transpose(2, 1, 0, 3, 4)
        return w.reshape(PAIRS, P, KT * 2 * HD)

    o = wo.reshape(PAIRS, 2, HD, D).transpose(0, 2, 1, 3).reshape(PAIRS, P, 2 * D)
    return np.ascontiguousarray(np.stack([by_pair(wv), by_pair(wk[:, :, order]), by_pair(wq[:, :, order]), o], axis=1))


def kernel(**inputs):
    import concourse.bacc as _bacc
    from concourse.bass_utils import run_bass_kernel_spmd as _run

    given = {k: np.asarray(v) for k, v in inputs.items()}
    ffn = [given[f"L0_ffn_{n}"] for n in ("gate_w", "w_up", "w_gate", "w_down", "up_A", "up_B", "gate_A", "gate_B",
                                           "down_A", "down_B")]
    arrays = {
        "x_in": np.ascontiguousarray(given["L0_attn_x"].reshape(TOKENS, D)),
        "ffn_w": pack_ffn(*ffn),
        "expand_w": expand_matrices(),
        "attn_w": pack_attention(*[given[f"L0_attn_{n}"] for n in ("wq", "wk", "wv", "wo")]),
        "rope_w": rope_tables(),
    }
    nc = _bacc.Bacc("TRN2", target_bir_lowering=False, num_devices=1)
    args = [nc.dram_tensor(n, a.shape, mybir.dt.from_np(a.dtype), kind="ExternalInput").ap() for n, a in arrays.items()]
    out = nc.dram_tensor("out", (TOKENS, D), F32, kind="ExternalOutput").ap()
    build(nc, *args, out)
    got = _run(nc, [arrays], core_ids=[0])
    return got.results[0]["out"].reshape(BATCH, SEQ, D)
```

```python
from contextlib import ExitStack

import numpy as np
import concourse.bass as bass
from concourse import mybir

ALU = mybir.AluOpType
ACT = mybir.ActivationFunctionType
AX = mybir.AxisListType
F32 = mybir.dt.float32
F32R = mybir.dt.float32r
BF16 = mybir.dt.bfloat16
U32 = mybir.dt.uint32
I32 = mybir.dt.int32
ds = bass.ds

P = 128
BATCH, SEQ, D = 2, 1024, 256
TOKENS = BATCH * SEQ
TILES = TOKENS // P
SEQ_TILES = SEQ // P
KT = D // P
CHUNK = 512
CHUNKS = TOKENS // CHUNK
CT = CHUNK // P
HEADS, HD = 16, 128
PAIRS = HEADS // 2
EXPERTS, RANK, HIDDEN = 8, 16, 704
ER = EXPERTS * RANK
FULL = HIDDEN // P
TAIL = HIDDEN - FULL * P
HT = FULL + 1
ALPHA = 2.0
EPS = 1e-5
SCALE = 1.0 / float(np.sqrt(np.float32(HD)))
MASKED = -1e30
HUGE = 3.0e38

BASE_TILES = 2 * FULL + 1
LORA_TILES = 2 * FULL + 2
OFF_A = 0
OFF_ROUTE = OFF_A + KT * 2 * ER
OFF_BASE = OFF_ROUTE + KT * EXPERTS
OFF_LORA = OFF_BASE + KT * BASE_TILES * P
OFF_DOWN_A = OFF_LORA + LORA_TILES * P
OFF_DOWN = OFF_DOWN_A + HT * ER
OFF_DOWN_B = OFF_DOWN + HT * D
FFN_COLS = OFF_DOWN_B + D
PIECES = 5
PIECE = FFN_COLS // PIECES
SPLITS = 2 * PIECES
SPLIT = FFN_COLS // SPLITS
assert SPLIT * SPLITS == FFN_COLS
MASK_ROWS = 4 * EXPERTS
EX_M1, EX_CM1, EX_M2, EX_CM2, EX_C1, EX_C2 = range(6)
EX_COLS = 6 * P

BU, BG, L0, L1, D1, D2, OUT0, OUT1 = range(8)
T_BANK, PV_BANK, MISC_BANK = 4, 6, 7

UNITS = 4
STEPS = UNITS * SEQ_TILES
T_LAG, PV_LAG, OUT_LAG = 2, 5, 8
ROPE_LAG = 2
DRAIN_STEPS = OUT_LAG + 1
GROUPS_AT = [0, 1, 2, 3, 4, 6, 8, 10]
UNIT_GROUPS = 12
KINDS = ["v", "k", "q", "o"]
RAW_OF = {"v": 0, "k": 0, "q": 1, "o": 2}


def tile_groups(i):
    first = 1 - i % 2
    out = []
    while first <= i + 1 - i % 2:
        n = min(4, i + 2 - i % 2 - first)
        out.append((first, n))
        first += n
    return out


def build(nc, x_in, ffn_w, expand_w, attn_w, rope_w, out):
    with ExitStack() as ctx:
        def sem(name):
            return ctx.enter_context(nc.semaphore(name))

        def sbuf(stack, name, shape, dt=F32):
            return stack.enter_context(nc.sbuf_tensor(name, shape, dt))

        x_sb = sbuf(ctx, "x_sb", [P, TILES, D])
        xnT_h = sbuf(ctx, "xnT_h", [P, KT, TOKENS], F32R)
        xnT_l = sbuf(ctx, "xnT_l", [P, KT, TOKENS], F32R)
        ident = sbuf(ctx, "ident", [P, P])
        causal = sbuf(ctx, "causal", [P, SEQ], BF16)
        stats = sbuf(ctx, "stats", [P, 2, CT, 6])
        mean_var = sbuf(ctx, "mean_var", [P, 2, CT, 2])
        var_eps = sbuf(ctx, "var_eps", [P, 2, CT])
        rstd = sbuf(ctx, "rstd", [P, 2, CT])
        minus_half = sbuf(ctx, "minus_half", [P, CT])
        ps = ctx.enter_context(nc.psum_tensor("ps", [P, 8, 512], F32))

        with ExitStack() as st:
            w_in = sbuf(st, "w_in", [P, FFN_COLS])
        with ExitStack() as st:
            w_l = sbuf(st, "w_l", [P, FFN_COLS], F32R)
            expand_raw = sbuf(st, "expand_raw", [P, EX_COLS])
            w_h = sbuf(st, "w_h", [P, FFN_COLS], F32R)
            expand = sbuf(st, "expand", [P, 6, P], F32R)
            xn = sbuf(st, "xn", [P, CT, D])
            cm = sbuf(st, "cm", [P, TILES, MASK_ROWS])
            cm_pad = sbuf(st, "cm_pad", [P, CT, P])
            maskT_h = sbuf(st, "maskT_h", [P, CHUNK], F32R)
            maskT_l = sbuf(st, "maskT_l", [P, CHUNK], F32R)
            spread = sbuf(st, "spread", [P, 6, CHUNK])
            um_h = sbuf(st, "um_h", [P, 4, CHUNK], F32R)
            um_l = sbuf(st, "um_l", [P, 4, CHUNK], F32R)
            base_up = sbuf(st, "base_up", [P, 2, CHUNK])
            base_gate = sbuf(st, "base_gate", [P, 2, CHUNK])
            up_act = sbuf(st, "up_act", [P, 2, CHUNK])
            hid = sbuf(st, "hid", [P, 2, CHUNK])
            hid_h = sbuf(st, "hid_h", [P, 2, 2, CHUNK], F32R)
            hid_l = sbuf(st, "hid_l", [P, 2, 2, CHUNK], F32R)
            mixed = sbuf(st, "mixed", [P, CHUNK])
            mixed_h = sbuf(st, "mixed_h", [P, 2, CHUNK], F32R)
            mixed_l = sbuf(st, "mixed_l", [P, 2, CHUNK], F32R)
            dm_h = sbuf(st, "dm_h", [P, CHUNK], F32R)
            dm_l = sbuf(st, "dm_l", [P, CHUNK], F32R)
            top8 = sbuf(st, "top8", [P, TILES, 8])
            top_at = sbuf(st, "top_at", [P, TILES, 8], U32)
            top_f = sbuf(st, "top_f", [P, TILES, 2])
            expert_i = sbuf(st, "expert_i", [P, EXPERTS], I32)
            expert_f = sbuf(st, "expert_f", [P, EXPERTS])
            part = sbuf(st, "part", [P, 3, 2 * BATCH])
            whole = sbuf(st, "whole", [P, 2, 2 * BATCH])
            route = sbuf(st, "route", [P, TILES, 2])

        with ExitStack() as st:
            rope = sbuf(st, "rope", [P, 2, SEQ])
            w_raw = [sbuf(st, f"w_raw{i}", [P, 512]) for i in range(3)]
            wa_h = {k: sbuf(st, f"w{k}_h", [P, 2, 256], F32R) for k in KINDS}
            wa_l = {k: sbuf(st, f"w{k}_l", [P, 2, 256], F32R) for k in KINDS}
            qT_h = sbuf(st, "qT_h", [P, 2, SEQ], F32R)
            qT_l = sbuf(st, "qT_l", [P, 2, SEQ], F32R)
            kT_h = sbuf(st, "kT_h", [P, 2, SEQ], F32R)
            kT_l = sbuf(st, "kT_l", [P, 2, SEQ], F32R)
            v_h = sbuf(st, "v_h", [P, BATCH, SEQ_TILES, 256], F32R)
            v_l = sbuf(st, "v_l", [P, BATCH, SEQ_TILES, 256], F32R)
            pT_h = [sbuf(st, f"pT_h{i}", [P, 6 + 2 * i, 256], F32R) for i in range(2)]
            pT_l = [sbuf(st, f"pT_l{i}", [P, 6 + 2 * i, 256], F32R) for i in range(2)]
            probs = [sbuf(st, f"probs{i}", [P, P * (SEQ_TILES - 3 + i)]) for i in range(4)]
            swapped = sbuf(st, "swapped", [P, 512])
            rot = sbuf(st, "rot", [P, 2, 512])
            rot_sin = sbuf(st, "rot_sin", [P, 512])
            oA_h = sbuf(st, "oA_h", [P, SEQ], F32R)
            oA_l = sbuf(st, "oA_l", [P, SEQ], F32R)
            oB_h = sbuf(st, "oB_h", [P, 2, 256], F32R)
            oB_l = sbuf(st, "oB_l", [P, 2, 256], F32R)
            neg_max = sbuf(st, "neg_max", [P, 4])
            row_sum = sbuf(st, "row_sum", [P, 4])
            inv_sum = sbuf(st, "inv_sum", [P, 4])

        x_loaded = [sem(f"x_loaded{c}") for c in range(CHUNKS)]
        consts_made = sem("consts_made")
        w_loaded = [sem(f"w_loaded{i}") for i in range(PIECES)]
        expand_loaded = sem("expand_loaded")
        expand_ready = sem("expand_ready")
        w_high = sem("w_high")
        w_ready = sem("w_ready")
        ln_stats = sem("ln_stats")
        ln_aggr = sem("ln_aggr")
        ln_var = sem("ln_var")
        ln_rstd = sem("ln_rstd")
        xn_ready = sem("xn_ready")
        xn_turned = sem("xn_turned")
        xn_high = sem("xn_high")
        xnT_ready = sem("xnT_ready")
        logitsT_done = sem("logitsT_done")
        logitsT_kept = sem("logitsT_kept")
        logits_ready = sem("logits_ready")
        route_chain = sem("route_chain")
        route_whole = sem("route_whole")
        route_exp = sem("route_exp")
        cm_padded = sem("cm_padded")
        mask_turned = sem("mask_turned")
        mask_high = sem("mask_high")
        mask_ready = sem("mask_ready")
        low_rank = sem("low_rank")
        spread_done = sem("spread_done")
        spread_act = sem("spread_act")
        spread_dve = sem("spread_dve")
        um_raw = sem("um_raw")
        um_high = sem("um_high")
        um_ready1 = sem("um_ready1")
        um_ready2 = sem("um_ready2")
        base_done = sem("base_done")
        lora_done = sem("lora_done")
        base_up_kept = sem("base_up_kept")
        base_gate_kept = sem("base_gate_kept")
        up_summed = sem("up_summed")
        up_act_done = sem("up_act_done")
        gate_summed = sem("gate_summed")
        hid_done = sem("hid_done")
        hid_high = sem("hid_high")
        hid_ready = sem("hid_ready")
        mixed_done = sem("mixed_done")
        mixed_high = sem("mixed_high")
        mixed_ready = sem("mixed_ready")
        down_a_done = sem("down_a_done")
        dm_parts = sem("dm_parts")
        dm_raw = sem("dm_raw")
        dm_high = sem("dm_high")
        dm_ready = sem("dm_ready")
        out_done = sem("out_done")
        x_updated = sem("x_updated")
        rope_loaded = sem("rope_loaded")
        wa_loaded = {k: sem(f"w{k}_loaded") for k in KINDS}
        wa_high = {k: sem(f"w{k}_high") for k in KINDS}
        wa_ready = {k: sem(f"w{k}_ready") for k in KINDS}
        zeroed = sem("zeroed")
        proj_done = sem("proj_done")
        proj_swapped = sem("proj_swapped")
        proj_cos = sem("proj_cos")
        proj_sin = sem("proj_sin")
        proj_rot = sem("proj_rot")
        proj_high = sem("proj_high")
        proj_ready = sem("proj_ready")
        v_done = sem("v_done")
        v_high = sem("v_high")
        v_ready = sem("v_ready")
        scores_done = sem("scores_done")
        max_done = sem("max_done")
        exp_done = sem("exp_done")
        inv_done = sem("inv_done")
        probs_ready = sem("probs_ready")
        turned = sem("turned")
        pT_high = sem("pT_high")
        pT_ready = sem("pT_ready")
        pv_done = sem("pv_done")
        o_high = sem("o_high")
        o_ready = sem("o_ready")
        y_done = sem("y_done")
        y_added = sem("y_added")
        stored = sem("stored")

        def need(eng, semaphore, count):
            if not isinstance(count, int) or count > 0:
                eng.wait_ge(semaphore, count)

        def low(eng, dst, src, high):
            return eng.tensor_tensor(dst, src, high.bitcast(F32), ALU.subtract)

        def logitsT(c):
            return (base_up, base_gate)[c // 2][0:EXPERTS, c % 2, :]

        def chunk_tiles(c):
            return x_sb[:, ds(CT * c, CT), :]

        def chunk_cols(c):
            return ds(CHUNK * c, CHUNK)

        def w_a(w, kt, gate):
            at = OFF_A + kt * 2 * ER + gate * ER
            return w[:, at:at + ER]

        def w_route(w, kt):
            at = OFF_ROUTE + kt * EXPERTS
            return w[:, at:at + P]

        def w_base(w, kt, tile):
            at = OFF_BASE + (kt * BASE_TILES + tile) * P
            return w[:, at:at + P]

        def w_lora(w, tile):
            at = OFF_LORA + tile * P
            return w[:, at:at + P]

        def w_down_a(w, m):
            at = OFF_DOWN_A + m * ER
            return w[:, at:at + ER]

        def w_down(w, m):
            at = OFF_DOWN + m * D
            return w[:, at:at + D]

        def w_down_b(w):
            return w[:, OFF_DOWN_B:OFF_DOWN_B + D]

        def unit_of(t):
            return t // SEQ_TILES, t % SEQ_TILES

        def tile_at(p, t):
            return (p, t) if t >= 0 else (p - 1, t + STEPS)

        def groups_before(p, t):
            u, i = unit_of(t)
            return UNITS * UNIT_GROUPS * p + UNIT_GROUPS * u + GROUPS_AT[i]

        def groups_through(p, t):
            return groups_before(p, t) + len(tile_groups(t % SEQ_TILES))

        def side_work(p, t, last):
            if t >= STEPS:
                return None
            u, i = unit_of(t)
            k = i // 2
            if i % 2 == 0:
                if u == UNITS - 1 and last:
                    return None
                return "proj", (u + 1) % UNITS, 4 * (UNITS * p + u + 1) + k, k
            if u % 2 == 1:
                if u == UNITS - 1 and last:
                    return None
                return "v", (u // 2 + 1) % 2, 4 * (2 * p + u // 2 + 1) + k, k
            return None

        def rotation_to_end(p, t, first, last):
            if t < ROPE_LAG:
                work = None if first else side_work(p - 1, t - ROPE_LAG + STEPS, False)
            else:
                work = side_work(p, t - ROPE_LAG, last)
            return work if work and work[0] == "proj" else None

        def tile_of_step(p, t, lag, first):
            q, s = tile_at(p, t - lag)
            return None if (first and t < lag) or t - lag >= STEPS else (q, s)

        def chunk_of_step(p, t, lag, first):
            tile = tile_of_step(p, t, lag, first)
            if not tile or tile[1] % 2 == 0:
                return None
            q, s = tile
            u, i = unit_of(s)
            return u, i // 2, 16 * q + 4 * u + i // 2, q, s

        def out_of_step(p, t, lag, first):
            chunk = chunk_of_step(p, t, lag, first)
            if not chunk or chunk[0] % 2 == 0:
                return None
            u, c, _, q, _ = chunk
            return u // 2, c, 4 * (2 * q + u // 2) + c, q

        def score_view(slot, i):
            n = P * (i + 1)
            if n <= 512:
                return ps[:, 2 * slot:2 * slot + 1, 0:n], 1, n
            return ps[:, 2 * slot:2 * slot + 2, 0:n // 2], 2, n // 2

        block = ctx.enter_context(nc.Block())

        @block.sync
        def _(sp):
            def load_ffn():
                for n in range(PIECES):
                    at = slice(n * PIECE, (n + 1) * PIECE)
                    sp.dma_start(w_in[:, at], ffn_w[:, at]).then_inc(w_loaded[n], 16)
                sp.dma_start(expand_raw[:], expand_w).then_inc(expand_loaded, 16)

            def load_pair(p):
                need(sp, wa_ready["k"], p)
                sp.dma_start(w_raw[0][:], attn_w[p, 0]).then_inc(wa_loaded["v"], 16)
                need(sp, wa_ready["v"], p + 1)
                sp.dma_start(w_raw[0][:], attn_w[p, 1]).then_inc(wa_loaded["k"], 16)
                need(sp, wa_ready["q"], p)
                sp.dma_start(w_raw[1][:], attn_w[p, 2]).then_inc(wa_loaded["q"], 16)
                need(sp, wa_ready["o"], p)
                sp.dma_start(w_raw[2][:], attn_w[p, 3]).then_inc(wa_loaded["o"], 16)

            x_view = x_in.rearrange("(c t p) d -> c p t d", t=CT, p=P)
            out_view = out.rearrange("(c t p) d -> c p t d", t=CT, p=P)
            for c in range(CHUNKS):
                sp.dma_start(chunk_tiles(c), x_view[c]).then_inc(x_loaded[c], 16)
            load_ffn()
            sp.wait_ge(out_done, 2 * CHUNKS)
            sp.dma_start(rope[:], rope_w).then_inc(rope_loaded, 16)
            load_pair(0)
            with sp.Fori(1, PAIRS) as p:
                load_pair(p)
            sp.wait_ge(y_added, 8 * PAIRS)
            load_ffn()
            with sp.Fori(0, CHUNKS) as c:
                sp.wait_ge(x_updated, 2 * c + (2 * CHUNKS + 2))
                sp.dma_start(out_view[c], chunk_tiles(c)).then_inc(stored, 16)
            sp.wait_ge(stored, 16 * CHUNKS)

        @block.gpsimd
        def _(pool):
            pool.memset(ident[:], 0.0).then_inc(consts_made, 1)
            pool.memset(causal[:], 0.0).then_inc(consts_made, 1)
            pool.memset(minus_half[:], -0.5).then_inc(consts_made, 1)
            pool.wait_ge(consts_made, 3)
            pool.affine_select(out=ident[:], in_=ident[:], compare_op=ALU.not_equal, fill=1.0, base=0,
                               pattern=[[-1, P]], channel_multiplier=1).then_inc(consts_made, 1)
            pool.affine_select(out=causal[:, SEQ - P:], in_=causal[:, SEQ - P:], compare_op=ALU.is_ge,
                               fill=MASKED, base=0, pattern=[[-1, P]], channel_multiplier=1)\
                .then_inc(consts_made, 1)

            def layer_norm(n, k=0):
                pool.wait_ge(ln_var, n + 1)
                pool.tensor_tensor(rstd[:, k], var_eps[:, k], minus_half[:], ALU.pow).then_inc(ln_rstd, 1)

            def split_ffn(f, n):
                pool.wait_ge(w_high, SPLITS * f + n + 1)
                at = slice(n * SPLIT, (n + 1) * SPLIT)
                low(pool, w_l[:, at], w_in[:, at], w_h[:, at]).then_inc(w_ready, 1)

            def router(f):
                pool.iota(expert_i[:], pattern=[[1, EXPERTS]], base=0, channel_multiplier=0)\
                    .then_inc(route_whole, 1)
                pool.wait_ge(route_chain, 10 * f + 4)
                pool.partition_all_reduce(whole[:, 0, :], part[:, 0, :], P, bass.bass_isa.ReduceOp.max)\
                    .then_inc(route_whole, 1)
                pool.wait_ge(route_chain, 10 * f + 6)
                pool.partition_all_reduce(whole[:, 1, :], part[:, 1, :], P, bass.bass_isa.ReduceOp.add)\
                    .then_inc(route_whole, 1)

            def ffn_chunk(g, c, f, first):
                for s in range(2):
                    pool.wait_ge(um_high, 4 * g + 3 + s)
                    if s == 0:
                        need(pool, lora_done, 22 * g)
                    low(pool, um_l[:, 2 + s], (up_act, hid)[s][:, 1], um_h[:, 2 + s])\
                        .then_inc(um_ready2, 1)
                for m in range(HT):
                    rows = P if m < FULL else TAIL
                    for j in range(2):
                        pool.wait_ge(hid_high, 12 * g + 2 * m + j + 1)
                        low(pool, hid_l[0:rows, m % 2, j], hid[0:rows, j], hid_h[0:rows, m % 2, j])\
                            .then_inc(hid_ready, 1)
                    pool.wait_ge(mixed_high, 6 * g + m + 1)
                    low(pool, mixed_l[0:rows, m % 2], mixed[0:rows], mixed_h[0:rows, m % 2])\
                        .then_inc(mixed_ready, 1)
                    if m == 0 and f == 0 and not first:
                        layer_norm(c + 3)

            def ffn(f):
                for c in range(CHUNKS):
                    layer_norm(8 * f + c, c % 2)
                    for n in ((), (0, 1), (2, 3), range(4, SPLITS))[c]:
                        split_ffn(f, n)
                router(f)
                ffn_chunk(4 * f, 0, f, True)
                with pool.Fori(1, CHUNKS) as c:
                    ffn_chunk(c + 4 * f, c, f, False)
                if f == 0:
                    layer_norm(2 * CHUNKS - 1)

            def rope_sin(index, ch):
                pool.wait_ge(proj_swapped, index + 1)
                need(pool, proj_rot, index)
                pool.tensor_tensor(rot_sin[:], swapped[:], rope[:, 1, 512 * ch:512 * ch + 512], ALU.mult)\
                    .then_inc(proj_sin, 1)

            def rope_low(index, u, k):
                pool.wait_ge(proj_high, index + 1)
                h, l = ((kT_h, kT_l), (qT_h, qT_l))[k % 2]
                cols = slice(512 * (k // 2), 512 * (k // 2) + 512)
                low(pool, l[:, u % 2, cols], rot[:, k % 2], h[:, u % 2, cols]).then_inc(proj_ready, 1)

            def attention(p, first, last):
                for t in range(STEPS + (DRAIN_STEPS if last else 0)):
                    q, s = tile_at(p, t - 1)
                    if s < STEPS and not (first and t == 0):
                        n = P * (s % SEQ_TILES + 1)
                        pool.wait_ge(inv_done, STEPS * q + s + 1)
                        pool.nop(nofuse=True)
                        pool.tensor_scalar(probs[s % 4][:, 0:n], probs[s % 4][:, 0:n], inv_sum[:, s % 4:s % 4 + 1], 1.0,
                                           ALU.mult, ALU.mult).then_inc(probs_ready, 1)
                    side = side_work(p, t, last)
                    if side and side[0] == "proj":
                        rope_sin(side[2], side[3] // 2)
                    turn = rotation_to_end(p, t, first, last)
                    if turn:
                        rope_low(turn[2], turn[1], turn[3])

            ffn(0)
            pool.wait_ge(xn_turned, KT * 2 * CHUNKS)
            for i in range(2):
                pool.memset(pT_h[i][:, 0, 0:P].bitcast(F32), 0.0)
                last_zero = pool.memset(pT_l[i][:, 0, 0:P].bitcast(F32), 0.0)
            last_zero.then_inc(zeroed, 1)
            pool.wait_ge(rope_loaded, 16)
            for k in range(4):
                rope_sin(k, k // 2)
                rope_low(k, 0, k)
            attention(0, True, False)
            with pool.Fori(1, PAIRS - 1) as p:
                attention(p, False, False)
            attention(PAIRS - 1, False, True)
            ffn(1)

        @block.scalar
        def _(act):
            def split_ffn(f, n):
                act.wait_ge(w_loaded[n // 2], 16 * (f + 1))
                at = slice(n * SPLIT, (n + 1) * SPLIT)
                act.activation(w_h[:, at], w_in[:, at], ACT.Copy).then_inc(w_high, 1)

            def keep_logits(f, c):
                act.wait_ge(logitsT_done, 4 * f + c + 1)
                act.activation(logitsT(c), ps[0:EXPERTS, c, :], ACT.Copy).then_inc(logitsT_kept, 1)

            def layer_norm_high(n, c):
                for kt in range(KT):
                    act.wait_ge(xn_turned, KT * n + (kt + 1))
                    act.activation(xnT_h[:, kt, chunk_cols(c)], ps[:, OUT0 + kt, :], ACT.Copy)\
                        .then_inc(xn_high, 1)

            def ffn_chunk(g, c, f, first):
                act.wait_ge(mask_turned, g + 1)
                act.activation(maskT_h[:], ps[:, BU, :], ACT.Copy).then_inc(mask_high, 1)
                for e, bank in ((EX_M1, BG), (EX_M2, D1), (EX_C1, BG), (EX_C2, BU)):
                    act.wait_ge(spread_done, 6 * g + e + 1)
                    act.activation(spread[:, e], ps[:, bank, :], ACT.Copy).then_inc(spread_act, 1)
                for s in range(4):
                    act.wait_ge(um_raw, 4 * g + s + 1)
                    act.activation(um_h[:, s], (up_act, hid)[s % 2][:, s // 2], ACT.Copy).then_inc(um_high, 1)
                for m in range(HT):
                    rows = P if m < FULL else TAIL
                    act.wait_ge(base_done, 11 * g + 2 * m + 1)
                    if m >= 2:
                        act.wait_ge(up_summed, 12 * g + 2 * (m - 1))
                    else:
                        need(act, up_summed, 12 * g)
                    act.activation(base_up[0:rows, m % 2], ps[0:rows, BU, :], ACT.Copy).then_inc(base_up_kept, 1)
                    for j in range(2):
                        act.wait_ge(up_summed, 12 * g + 2 * m + j + 1)
                        act.activation(up_act[0:rows, j], up_act[0:rows, j], ACT.Silu).then_inc(up_act_done, 1)
                        if f == 0 and not first and (m, j) == (1, 1):
                            layer_norm_high(c + 3, c - 1)
                        act.wait_ge(hid_done, 12 * g + 2 * m + j + 1)
                        act.activation(hid_h[0:rows, m % 2, j], hid[0:rows, j], ACT.Copy).then_inc(hid_high, 1)
                    act.wait_ge(mixed_done, 6 * g + m + 1)
                    act.activation(mixed_h[0:rows, m % 2], mixed[0:rows], ACT.Copy).then_inc(mixed_high, 1)
                act.wait_ge(dm_raw, g + 1)
                act.activation(dm_h[:], base_gate[:, 0], ACT.Copy).then_inc(dm_high, 1)

            def ffn(f):
                for c in range(CHUNKS):
                    for n in range(2 * c, 2 * c + 2):
                        split_ffn(f, n)
                    layer_norm_high(8 * f + c, c)
                    if c > 0:
                        keep_logits(f, c - 1)
                keep_logits(f, CHUNKS - 1)
                for n in range(2 * CHUNKS, SPLITS):
                    split_ffn(f, n)
                act.wait_ge(expand_loaded, 16 * (f + 1))
                act.activation(expand[:].rearrange("p a b -> p (a b)"), expand_raw[:], ACT.Copy).then_inc(expand_ready, 1)
                act.wait_ge(route_chain, 10 * f + 5)
                act.activation(route[:], route[:], ACT.Exp).then_inc(route_exp, 1)
                ffn_chunk(4 * f, 0, f, True)
                with act.Fori(1, CHUNKS) as c:
                    ffn_chunk(c + 4 * f, c, f, False)
                if f == 0:
                    layer_norm_high(2 * CHUNKS - 1, CHUNKS - 1)

            def split_pair(kind, p):
                act.wait_ge(wa_loaded[kind], 16 * (p + 1))
                if kind in "kq":
                    need(act, proj_done, 16 * p - (kind == "k"))
                elif kind == "v":
                    need(act, v_done, 8 * p)
                else:
                    need(act, y_done, 8 * p)
                act.activation(wa_h[kind][:].rearrange("p a b -> p (a b)"), w_raw[RAW_OF[kind]][:], ACT.Copy)\
                    .then_inc(wa_high[kind], 1)

            def swap_halves(index):
                act.wait_ge(proj_cos, index + 1)
                need(act, proj_sin, index)
                act.activation(swapped[0:64], ps[64:128, MISC_BANK, :], ACT.Copy)
                act.activation(swapped[64:128], ps[0:64, MISC_BANK, :], ACT.Copy).then_inc(proj_swapped, 1)

            def rope_high(index, u, k):
                act.wait_ge(proj_rot, index + 1)
                h = (kT_h, qT_h)[k % 2]
                act.activation(h[:, u % 2, 512 * (k // 2):512 * (k // 2) + 512], rot[:, k % 2], ACT.Copy)\
                    .then_inc(proj_high, 1)

            def value_high(index, b, k):
                act.wait_ge(v_done, index + 1)
                act.activation(v_h[:, b, 2 * k:2 * k + 2, :].rearrange("p a b -> p (a b)"), ps[:, MISC_BANK, :],
                               ACT.Copy).then_inc(v_high, 1)

            def attention(p, first, last):
                for t in range(STEPS + (DRAIN_STEPS if last else 0)):
                    tile = tile_of_step(p, t, T_LAG + 1, first)
                    if tile:
                        q, s = tile
                        i = s % SEQ_TILES
                        half = P * (i % 2)
                        for n, (slot, count) in enumerate(tile_groups(i)):
                            act.wait_ge(turned, groups_before(q, s) + n + 1)
                            bank = T_BANK + (GROUPS_AT[i] + n) % 2
                            act.activation(pT_h[i // 2 % 2][:, slot:slot + count, half:half + P],
                                           ps[:, bank, 0:P * count].rearrange("p (a b) -> p a b", a=count),
                                           ACT.Copy).then_inc(pT_high, 1)
                    turn = rotation_to_end(p, t, first, last)
                    if turn:
                        rope_high(turn[2], turn[1], turn[3])
                    chunk = chunk_of_step(p, t, PV_LAG + 1, first)
                    if chunk:
                        u, c, index, _, _ = chunk
                        dst = oA_h[:, 256 * c:256 * c + 256] if u % 2 == 0 else oB_h[:, c % 2]
                        act.wait_ge(pv_done, index + 1)
                        act.activation(dst, ps[:, PV_BANK, 0:256], ACT.Copy).then_inc(o_high, 1)
                    side = side_work(p, t, last)
                    if side and side[0] == "v":
                        value_high(side[2], side[1], side[3])
                    if t < STEPS:
                        view, a, n = score_view(t % 2, t % SEQ_TILES)
                        act.wait_ge(max_done, STEPS * p + t + 1)
                        if not (first and t < 4):
                            act.wait_ge(turned, groups_through(*tile_at(p, t - 4)))
                        act.activation(probs[t % 4][:, 0:a * n].rearrange("p (a n) -> p a n", a=a), view, ACT.Exp,
                                       bias=neg_max[:, t % 4:t % 4 + 1], scale=-1.0,
                                       accum_out=row_sum[:, t % 4:t % 4 + 1]).then_inc(exp_done, 1)
                    if side and side[0] == "proj":
                        swap_halves(side[2])
                    if t == 8 and not first:
                        split_pair("o", p)
                    if t == 17 and not last:
                        split_pair("v", p + 1)
                    if t == 21 and not last:
                        split_pair("k", p + 1)
                    if t == 23 and not last:
                        split_pair("q", p + 1)

            ffn(0)
            for kind in KINDS:
                split_pair(kind, 0)
            for k in range(4):
                swap_halves(k)
                rope_high(k, 0, k)
            for k in range(4):
                value_high(k, 0, k)
            attention(0, True, False)
            with act.Fori(1, PAIRS - 1) as p:
                attention(p, False, False)
            attention(PAIRS - 1, False, True)
            ffn(1)

        @block.vector
        def _(dve):
            def layer_norm_stats(n, c, k=0):
                for tt in range(CT):
                    ins = dve.bn_stats(stats[:, k, tt, :], x_sb[:, ds(CT * c + tt, 1), :].rearrange("p a d -> p (a d)"))
                ins.then_inc(ln_stats, 1)
                dve.wait_ge(ln_stats, n + 1)
                dve.nop(nofuse=True)
                for tt in range(CT):
                    ins = dve.bn_aggr(mean_var[:, k, tt, :], stats[:, k, tt, :])
                ins.then_inc(ln_aggr, 1)
                dve.wait_ge(ln_aggr, n + 1)
                dve.tensor_scalar(var_eps[:, k], mean_var[:, k, :, 1], EPS, None, ALU.add).then_inc(ln_var, 1)

            def layer_norm(n, c, k=0):
                dve.wait_ge(ln_rstd, n + 1)
                need(dve, xn_turned, KT * n)
                for tt in range(CT):
                    ins = dve.tensor_scalar(xn[:, tt, :], x_sb[:, ds(CT * c + tt, 1), :].rearrange("p a d -> p (a d)"),
                                            mean_var[:, k, tt, 0:1], rstd[:, k, tt:tt + 1], ALU.subtract, ALU.mult)
                ins.then_inc(xn_ready, 1)

            def layer_norm_low(n, c):
                for kt in range(KT):
                    dve.wait_ge(xn_high, KT * n + (kt + 1))
                    low(dve, xnT_l[:, kt, chunk_cols(c)], ps[:, OUT0 + kt, :], xnT_h[:, kt, chunk_cols(c)])\
                        .then_inc(xnT_ready, 1)

            def router(f):
                steps = [10 * f]

                def link(ins):
                    steps[0] += 1
                    ins.then_inc(route_chain, 1)
                    dve.wait_ge(route_chain, steps[0])

                def of_batch(b):
                    return slice(b * SEQ_TILES, (b + 1) * SEQ_TILES)

                def logits(tile):
                    return ps[:, D1, EXPERTS * tile:EXPERTS * tile + EXPERTS]

                def spread_over(v, b):
                    return v[:, None, 2 * b:2 * b + 2].to_broadcast([P, SEQ_TILES, 2])

                dve.wait_ge(logits_ready, f + 1)
                for tile in range(TILES):
                    ins = dve.max(top8[:, tile, :], logits(tile))
                link(ins)
                for tile in range(TILES):
                    ins = dve.max_index(top_at[:, tile, :], top8[:, tile, :], logits(tile))
                link(ins)
                dve.wait_ge(route_whole, 3 * f + 1)
                dve.tensor_copy(expert_f[:], expert_i[:])
                link(dve.tensor_copy(top_f[:], top_at[:, :, 0:2]))
                for b in range(BATCH):
                    ins = dve.tensor_reduce(part[:, 0, 2 * b:2 * b + 2],
                                            top8[:, of_batch(b), 0:2].rearrange("p t j -> p j t"), AX.X, ALU.max)
                link(ins)
                dve.wait_ge(route_whole, 3 * f + 2)
                for b in range(BATCH):
                    ins = dve.tensor_tensor(route[:, of_batch(b), :], top8[:, of_batch(b), 0:2],
                                            spread_over(whole[:, 0, :], b), ALU.subtract)
                link(ins)
                dve.wait_ge(route_exp, f + 1)
                for b in range(BATCH):
                    ins = dve.tensor_reduce(part[:, 1, 2 * b:2 * b + 2],
                                            route[:, of_batch(b), :].rearrange("p t j -> p j t"), AX.X, ALU.add)
                link(ins)
                for j in range(2):
                    ins = dve.tensor_tensor(cm[:, :, EXPERTS * j:EXPERTS * j + EXPERTS],
                                            expert_f[:, None, :].to_broadcast([P, TILES, EXPERTS]),
                                            top_f[:, :, j:j + 1].to_broadcast([P, TILES, EXPERTS]), ALU.is_equal)
                link(ins)
                dve.wait_ge(route_whole, 3 * f + 3)
                link(dve.reciprocal(part[:, 2, :], whole[:, 1, :]))
                for b in range(BATCH):
                    ins = dve.tensor_tensor(route[:, of_batch(b), :], route[:, of_batch(b), :],
                                            spread_over(part[:, 2, :], b), ALU.mult)
                link(ins)
                for j in range(2):
                    ins = dve.tensor_tensor(cm[:, :, EXPERTS * (2 + j):EXPERTS * (3 + j)],
                                            cm[:, :, EXPERTS * j:EXPERTS * j + EXPERTS],
                                            route[:, :, j:j + 1].to_broadcast([P, TILES, EXPERTS]), ALU.mult)
                link(ins)

            def update_x(g, c, f):
                for k in range(2):
                    dve.wait_ge(out_done, 2 * g + (k + 1))
                    tiles = x_sb[:, ds(CT * c + 2 * k, 2), :].rearrange("p a d -> p (a d)")
                    dve.scalar_tensor_tensor(out=tiles, in0=ps[:, OUT0 + k, :], scalar=0.5, in1=tiles,
                                             op0=ALU.mult, op1=ALU.add).then_inc(x_updated, 1)

            def ffn_chunk(g, c, f, first):
                need(dve, mask_turned, g)
                dve.tensor_copy(cm_pad[:, :, 0:MASK_ROWS], cm[:, ds(CT * c, CT), :]).then_inc(cm_padded, 1)
                dve.wait_ge(mask_high, g + 1)
                low(dve, maskT_l[:], ps[:, BU, :], maskT_h[:]).then_inc(mask_ready, 1)
                if not first:
                    update_x(g - 1, c - 1, f)
                for e, bank in ((EX_CM1, BU), (EX_CM2, D2)):
                    dve.wait_ge(spread_done, 6 * g + e + 1)
                    dve.tensor_copy(spread[:, e], ps[:, bank, :]).then_inc(spread_dve, 1)
                dve.wait_ge(low_rank, 2 * g + 2)
                dve.wait_ge(spread_dve, 2 * g + 2)
                dve.wait_ge(spread_act, 4 * g + 2)
                for s, (bank, e) in enumerate(((L0, EX_M1), (L1, EX_CM1), (L0, EX_M2), (L1, EX_CM2))):
                    dst = (up_act, hid)[s % 2][:, s // 2]
                    dve.tensor_tensor(dst, ps[:, bank, :], spread[:, e], ALU.mult).then_inc(um_raw, 1)
                for s in range(2):
                    dve.wait_ge(um_high, 4 * g + s + 1)
                    low(dve, um_l[:, s], (up_act, hid)[s][:, 0], um_h[:, s]).then_inc(um_ready1, 1)
                for m in range(HT):
                    rows = P if m < FULL else TAIL
                    dve.wait_ge(base_done, 11 * g + min(2 * m + 2, 11))
                    dve.wait_ge(spread_act, 4 * g + 4)
                    for j in range(2):
                        if m < FULL:
                            src, c_j = ps[:, BG, :], spread[:, EX_C1 + j]
                        else:
                            src, c_j = ps[TAIL:2 * TAIL, BU, :], spread[TAIL:2 * TAIL, EX_C1 + j]
                        dve.tensor_tensor(base_gate[0:rows, j], src, c_j, ALU.mult).then_inc(base_gate_kept, 1)
                    dve.wait_ge(base_up_kept, 6 * g + m + 1)
                    for j in range(2):
                        if m == 0 and j == 1:
                            dve.wait_ge(um_ready2, 2 * g + 2)
                        if m < FULL:
                            up_src, gate_src, n = ps[:, L0, :], ps[:, L1, :], 22 * g + 4 * m + 2 * j + 1
                        else:
                            up_src, gate_src, n = ps[0:TAIL, L0 + j, :], ps[TAIL:2 * TAIL, L0 + j, :], 22 * g + 21 + j
                        dve.wait_ge(lora_done, n)
                        dve.tensor_tensor(up_act[0:rows, j], up_src, base_up[0:rows, m % 2], ALU.add).then_inc(up_summed, 1)
                        if m < FULL:
                            dve.wait_ge(lora_done, n + 1)
                        dve.wait_ge(base_gate_kept, 12 * g + 2 * m + j + 1)
                        need(dve, hid_ready, 12 * g + 2 * m + j - 1)
                        if m > 0:
                            dve.wait_ge(mixed_done, 6 * g + m)
                        dve.tensor_tensor(hid[0:rows, j], gate_src, base_gate[0:rows, j], ALU.add).then_inc(gate_summed, 1)
                        dve.wait_ge(up_act_done, 12 * g + 2 * m + j + 1)
                        dve.wait_ge(gate_summed, 12 * g + 2 * m + j + 1)
                        dve.tensor_tensor(hid[0:rows, j], up_act[0:rows, j], hid[0:rows, j], ALU.mult).then_inc(hid_done, 1)
                        if f == 0 and not first and (m, j) == (0, 0):
                            dve.wait_ge(x_updated, 2 * g)
                            dve.nop(nofuse=True)
                            layer_norm_stats(c + 3, c - 1)
                        if f == 0 and not first and (m, j) == (1, 1):
                            layer_norm_low(c + 3, c - 1)
                    need(dve, mixed_ready, 6 * g + m)
                    dve.wait_ge(hid_done, 12 * g + 2 * m + 2)
                    dve.tensor_tensor(mixed[0:rows], hid[0:rows, 0], hid[0:rows, 1], ALU.add).then_inc(mixed_done, 1)
                    if m == 0 and f == 0 and not first:
                        layer_norm(c + 3, c - 1)
                dve.wait_ge(down_a_done, g + 1)
                for j in range(2):
                    ins = dve.tensor_tensor(base_gate[:, j], ps[:, D1 + j, :], spread[:, (EX_M1, EX_M2)[j]], ALU.mult)
                ins.then_inc(dm_parts, 1)
                dve.wait_ge(dm_parts, g + 1)
                dve.tensor_tensor(base_gate[:, 0], base_gate[:, 0], base_gate[:, 1], ALU.add).then_inc(dm_raw, 1)
                dve.wait_ge(dm_high, g + 1)
                low(dve, dm_l[:], base_gate[:, 0], dm_h[:]).then_inc(dm_ready, 1)

            def ffn(f):
                if f == 1:
                    dve.wait_ge(y_added, 8 * PAIRS)
                dve.memset(cm_pad[:], 0.0)
                for c in range(CHUNKS + 1):
                    if c < CHUNKS:
                        if f == 0:
                            dve.wait_ge(x_loaded[c], 16)
                            if c == 0:
                                dve.wait_ge(consts_made, 5)
                        layer_norm_stats(8 * f + c, c, c % 2)
                    if c > 1:
                        layer_norm_low(8 * f + c - 2, c - 2)
                    if c > 0:
                        layer_norm(8 * f + c - 1, c - 1, (c - 1) % 2)
                layer_norm_low(8 * f + CHUNKS - 1, CHUNKS - 1)
                router(f)
                ffn_chunk(4 * f, 0, f, True)
                with dve.Fori(1, CHUNKS) as c:
                    ffn_chunk(c + 4 * f, c, f, False)
                update_x(4 * f + 3, CHUNKS - 1, f)
                if f == 0:
                    dve.wait_ge(x_updated, 2 * CHUNKS)
                    layer_norm_stats(2 * CHUNKS - 1, CHUNKS - 1)
                    layer_norm(2 * CHUNKS - 1, CHUNKS - 1)
                    layer_norm_low(2 * CHUNKS - 1, CHUNKS - 1)

            def split_pair(kind, p):
                dve.wait_ge(wa_high[kind], p + 1)
                low(dve, wa_l[kind][:].rearrange("p a b -> p (a b)"), w_raw[RAW_OF[kind]][:],
                    wa_h[kind][:].rearrange("p a b -> p (a b)")).then_inc(wa_ready[kind], 1)

            def rope_cos(index, k):
                dve.wait_ge(proj_done, index + 1)
                need(dve, proj_ready, index - 1)
                dve.tensor_tensor(rot[:, k % 2], ps[:, MISC_BANK, :], rope[:, 0, 512 * (k // 2):512 * (k // 2) + 512],
                                  ALU.mult).then_inc(proj_cos, 1)

            def rope_sum(index, k):
                dve.wait_ge(proj_cos, index + 1)
                dve.wait_ge(proj_sin, index + 1)
                dve.tensor_tensor(rot[:, k % 2], rot[:, k % 2], rot_sin[:], ALU.add).then_inc(proj_rot, 1)

            def value_low(index, b, k):
                dve.wait_ge(v_high, index + 1)
                low(dve, v_l[:, b, 2 * k:2 * k + 2, :].rearrange("p a b -> p (a b)"), ps[:, MISC_BANK, :],
                    v_h[:, b, 2 * k:2 * k + 2, :].rearrange("p a b -> p (a b)")).then_inc(v_ready, 1)

            def invert_sum(p, t, first):
                tile = tile_of_step(p, t, 1, first)
                if tile:
                    q, s = tile
                    dve.wait_ge(exp_done, STEPS * q + s + 1)
                    dve.reciprocal(inv_sum[:, s % 4:s % 4 + 1], row_sum[:, s % 4:s % 4 + 1]).then_inc(inv_done, 1)

            def attention(p, first, last):
                for t in range(STEPS + (DRAIN_STEPS if last else 0)):
                    y = out_of_step(p, t, OUT_LAG + 1, first)
                    if y:
                        b, c, index, _ = y
                        tiles = x_sb[:, SEQ_TILES * b + 2 * c:SEQ_TILES * b + 2 * c + 2, :].rearrange("p a d -> p (a d)")
                        dve.wait_ge(y_done, index + 1)
                        need(dve, y_added, index - 3)
                        dve.tensor_tensor(tiles, ps[:, MISC_BANK, :], tiles, ALU.add).then_inc(y_added, 1)
                    turn = rotation_to_end(p, t, first, last)
                    if turn:
                        rope_sum(turn[2], turn[3])
                    if t % 2 == 1:
                        invert_sum(p, t, first)
                    if t < STEPS:
                        view, a, n = score_view(t % 2, t % SEQ_TILES)
                        dve.wait_ge(scores_done, STEPS * p + t + 1)
                        dve.nop(nofuse=True)
                        dve.tensor_tensor_reduce(out=view, in0=view,
                                                 in1=causal[:, SEQ - a * n:].rearrange("p (a n) -> p a n", a=a),
                                                 scale=-SCALE, scalar=HUGE, op0=ALU.add, op1=ALU.min,
                                                 accum_out=neg_max[:, t % 4:t % 4 + 1]).then_inc(max_done, 1)
                    tile = tile_of_step(p, t, T_LAG + 1, first)
                    if tile:
                        q, s = tile
                        i = s % SEQ_TILES
                        half = P * (i % 2)
                        for n, (slot, count) in enumerate(tile_groups(i)):
                            dve.wait_ge(pT_high, groups_before(q, s) + n + 1)
                            bank = T_BANK + (GROUPS_AT[i] + n) % 2
                            low(dve, pT_l[i // 2 % 2][:, slot:slot + count, half:half + P],
                                ps[:, bank, 0:P * count].rearrange("p (a b) -> p a b", a=count),
                                pT_h[i // 2 % 2][:, slot:slot + count, half:half + P]).then_inc(pT_ready, 1)
                    side = side_work(p, t, last)
                    if side and side[0] == "proj":
                        rope_cos(side[2], side[3])
                    elif side:
                        value_low(side[2], side[1], side[3])
                    chunk = chunk_of_step(p, t, PV_LAG + 1, first)
                    if chunk:
                        u, c, index, _, _ = chunk
                        h, l = ((oA_h[:, 256 * c:256 * c + 256], oA_l[:, 256 * c:256 * c + 256]) if u % 2 == 0
                                else (oB_h[:, c % 2], oB_l[:, c % 2]))
                        dve.wait_ge(o_high, index + 1)
                        low(dve, l, ps[:, PV_BANK, 0:256], h).then_inc(o_ready, 1)
                    if t % 2 == 0:
                        invert_sum(p, t, first)
                    if t == 8 and not first:
                        split_pair("o", p)
                    if t == 17 and not last:
                        split_pair("v", p + 1)
                    if t == 21 and not last:
                        split_pair("k", p + 1)
                    if t == 23 and not last:
                        split_pair("q", p + 1)

            ffn(0)
            for kind in KINDS:
                split_pair(kind, 0)
            dve.wait_ge(rope_loaded, 16)
            for k in range(4):
                rope_cos(k, k)
                rope_sum(k, k)
            for k in range(4):
                value_low(k, 0, k)
            attention(0, True, False)
            with dve.Fori(1, PAIRS - 1) as p:
                attention(p, False, False)
            attention(PAIRS - 1, False, True)
            ffn(1)

        @block.tensor
        def _(pe):
            def product(dst, w, x, start, stop, skip=False):
                pe.matmul(dst, w[0], x[0], start=start, stop=False, skip_group_check=skip)
                pe.matmul(dst, w[0], x[1], start=False, stop=False, skip_group_check=skip)
                return pe.matmul(dst, w[1], x[0], start=False, stop=stop, skip_group_check=skip)

            def xnT(kt, cols):
                return xnT_h[:, kt, cols], xnT_l[:, kt, cols]

            def layer_norm(n):
                pe.wait_ge(xn_ready, n + 1)
                for kt in range(KT):
                    need(pe, xnT_ready, KT * n - (KT - 1) + kt)
                    for tt in range(CT):
                        ins = pe.transpose(ps[:, OUT0 + kt, P * tt:P * tt + P], xn[:, tt, P * kt:P * kt + P], ident[:])
                    ins.then_inc(xn_turned, 1)

            def router_logits(f, c):
                pe.wait_ge(w_ready, SPLITS * f + 2)
                pe.wait_ge(xnT_ready, KT * (8 * f + c + 1))
                for kt in range(KT):
                    product(ps[:, c, :], (w_route(w_h, kt), w_route(w_l, kt)), xnT(kt, chunk_cols(c)), kt == 0, False)
                    ins = pe.matmul(ps[:, c, :], w_route(w_l, kt), xnT_l[:, kt, chunk_cols(c)], start=False,
                                    stop=(kt == KT - 1))
                ins.then_inc(logitsT_done, 1)

            def router(f):
                for c in range(CHUNKS):
                    pe.wait_ge(logitsT_kept, 4 * f + c + 1)
                    for tt in range(CT):
                        at = EXPERTS * (CT * c + tt)
                        ins = pe.transpose(ps[:, D1, at:at + EXPERTS], logitsT(c)[:, P * tt:P * tt + P],
                                           ident[0:EXPERTS, 0:EXPERTS])
                ins.then_inc(logits_ready, 1)

            def down_b(g):
                pe.wait_ge(dm_ready, g + 1)
                for tt in range(CT):
                    cols = slice(P * tt, P * tt + P)
                    ins = product(ps[:, OUT0 + tt // 2, D * (tt % 2):D * (tt % 2) + D], (dm_h[:, cols], dm_l[:, cols]),
                                  (w_down_b(w_h), w_down_b(w_l)), False, True, skip=True)
                    if tt % 2 == 1:
                        ins.then_inc(out_done, 1)

            def ffn_chunk(g, c, f, first):
                cols = chunk_cols(c)
                need(pe, up_summed, 12 * g)
                need(pe, gate_summed, 12 * g)
                for gate in range(2):
                    for kt in range(KT):
                        ins = product(ps[:, L0 + gate, :], (w_a(w_h, kt, gate), w_a(w_l, kt, gate)), xnT(kt, cols),
                                      kt == 0, kt == KT - 1)
                    ins.then_inc(low_rank, 1)
                pe.wait_ge(cm_padded, g + 1)
                need(pe, base_up_kept, 6 * g)
                need(pe, base_gate_kept, 12 * g)
                for tt in range(CT):
                    ins = pe.transpose(ps[:, BU, P * tt:P * tt + P], cm_pad[:, tt, :], ident[:])
                ins.then_inc(mask_turned, 1)
                if not first:
                    down_b(g - 1)
                pe.wait_ge(mask_ready, g + 1)
                for e, bank in ((EX_M1, BG), (EX_CM1, BU), (EX_M2, D1), (EX_CM2, D2), (EX_C1, BG), (EX_C2, BU)):
                    if e == EX_C1:
                        pe.wait_ge(spread_act, 4 * g + 1)
                    if e == EX_C2:
                        pe.wait_ge(spread_dve, 2 * g + 1)
                    pe.matmul(ps[:, bank, :], expand[:, e], maskT_h[:], start=True, stop=False)
                    pe.matmul(ps[:, bank, :], expand[:, e], maskT_l[:], start=False, stop=True).then_inc(spread_done, 1)

                def base(bank, tile):
                    for kt in range(KT):
                        ins = product(ps[:, bank, :], (w_base(w_h, kt, tile), w_base(w_l, kt, tile)), xnT(kt, cols),
                                      kt == 0, kt == KT - 1)
                    ins.then_inc(base_done, 1)

                def lora(bank, tile, s, start=True, stop=True):
                    return product(ps[:, bank, :], (w_lora(w_h, tile), w_lora(w_l, tile)), (um_h[:, s], um_l[:, s]), start, stop)

                def down_a(m, j):
                    pe.wait_ge(hid_ready, 12 * g + 2 * m + j + 1)
                    if m == 0 and j == 0:
                        pe.wait_ge(spread_act, 4 * g + 2)
                    elif m == 0:
                        pe.wait_ge(spread_dve, 2 * g + 2)
                    return product(ps[:, D1 + j, :], (w_down_a(w_h, m), w_down_a(w_l, m)),
                                   (hid_h[:, m % 2, j], hid_l[:, m % 2, j]), m == 0, m == HT - 1)

                def down(m):
                    pe.wait_ge(mixed_ready, 6 * g + m + 1)
                    if m == 0:
                        if f == 0:
                            pe.wait_ge(xnT_ready, KT * CHUNKS if first else KT * (c + 4))
                        elif first:
                            pe.wait_ge(xnT_ready, 3 * KT * CHUNKS)
                        else:
                            pe.wait_ge(x_updated, 2 * g)
                    for tt in range(CT):
                        tok = slice(P * tt, P * tt + P)
                        product(ps[:, OUT0 + tt // 2, D * (tt % 2):D * (tt % 2) + D],
                                (mixed_h[:, m % 2, tok], mixed_l[:, m % 2, tok]),
                                (w_down(w_h, m), w_down(w_l, m)), m == 0 and tt % 2 == 0, False, skip=True)

                for m in range(HT):
                    if m == 0:
                        pe.wait_ge(spread_act, 4 * g + 4)
                    else:
                        pe.wait_ge(base_up_kept, 6 * g + m)
                    if m < FULL:
                        base(BU, m)
                        if m > 0:
                            pe.wait_ge(base_gate_kept, 12 * g + 2 * m)
                        base(BG, FULL + m)
                        if m >= 2:
                            down(m - 2)
                        for j in range(2):
                            if m == 0:
                                pe.wait_ge((um_ready1, um_ready2)[j], 2 * g + 2)
                                if j == 0:
                                    pe.wait_ge(um_raw, 4 * g + 4)
                            if m > 0 or j > 0:
                                pe.wait_ge(up_summed, 12 * g + 2 * m + j)
                            lora(L0, m, 2 * j).then_inc(lora_done, 1)
                            if m > 0 or j > 0:
                                pe.wait_ge(gate_summed, 12 * g + 2 * m + j)
                            lora(L1, FULL + m, 2 * j + 1).then_inc(lora_done, 1)
                            if m > 0:
                                down_a(m - 1, j)
                        if m == 1 and f == 0 and not first:
                            layer_norm(c + 3)
                    else:
                        base(BU, 2 * FULL)
                        down(m - 2)
                        for j in range(2):
                            pe.wait_ge((up_summed, gate_summed)[j], 12 * g + 2 * m)
                            lora(L0 + j, 2 * FULL, 2 * j, True, False)
                            lora(L0 + j, 2 * FULL + 1, 2 * j + 1, False, True).then_inc(lora_done, 1)
                            down_a(m - 1, j)
                down(HT - 2)
                down_a(HT - 1, 0)
                down_a(HT - 1, 1).then_inc(down_a_done, 1)
                down(HT - 1)

            def ffn(f):
                if f == 0:
                    pe.wait_ge(consts_made, 5)
                for c in range(CHUNKS):
                    layer_norm(8 * f + c)
                    if c > 0:
                        router_logits(f, c - 1)
                router_logits(f, CHUNKS - 1)
                router(f)
                pe.wait_ge(w_ready, SPLITS * (f + 1))
                pe.wait_ge(expand_ready, f + 1)
                ffn_chunk(4 * f, 0, f, True)
                with pe.Fori(1, CHUNKS) as c:
                    ffn_chunk(c + 4 * f, c, f, False)
                down_b(4 * f + 3)
                if f == 0:
                    layer_norm(2 * CHUNKS - 1)

            bank_user = [None]

            def misc_bank_free():
                if bank_user[0]:
                    kind, index = bank_user[0]
                    pe.wait_ge({"proj": proj_swapped, "v": v_ready, "o": y_added}[kind], index + 1)

            def project(index, u, k):
                kind = "kq"[k % 2]
                h, l = wa_h[kind], wa_l[kind]
                head, b, at = u % 2, u // 2, 512 * (k // 2)
                cols = slice(SEQ * b + at, SEQ * b + at + 512)
                misc_bank_free()
                for kt in range(KT):
                    w = (h[:, kt, HD * head:HD * head + HD], l[:, kt, HD * head:HD * head + HD])
                    ins = product(ps[:, MISC_BANK, :], w, xnT(kt, cols), kt == 0, kt == KT - 1)
                ins.then_inc(proj_done, 1)
                bank_user[0] = "proj", index

            def values(index, b, k):
                misc_bank_free()
                for half in range(2):
                    tok = SEQ * b + P * (2 * k + half)
                    for kt in range(KT):
                        ins = product(ps[:, MISC_BANK, 256 * half:256 * half + 256], xnT(kt, slice(tok, tok + P)),
                                      (wa_h["v"][:, kt, :], wa_l["v"][:, kt, :]), kt == 0, kt == KT - 1)
                ins.then_inc(v_done, 1)
                bank_user[0] = "v", index

            def side(p, t, last):
                work = side_work(p, t, last)
                if not work:
                    return
                kind, what, index, k = work
                if kind == "proj":
                    if t >= STEPS - SEQ_TILES and k < 2:
                        pe.wait_ge(wa_ready["kq"[k % 2]], p + 2)
                    project(index, what, k)
                else:
                    if t >= STEPS - SEQ_TILES and k == 0:
                        pe.wait_ge(wa_ready["v"], p + 2)
                    values(index, what, k)

            def scores(p, t, first):
                u, i = unit_of(t)
                view, a, n = score_view(t % 2, i)
                if not (first and t < 2):
                    pe.wait_ge(exp_done, STEPS * p + t - 1)
                if i % 4 == 0:
                    pe.wait_ge(proj_ready, 4 * (UNITS * p + u) + 2 + i // 2)
                for part_at in range(a):
                    cols = max(n, 256)
                    dst = ps[:, 2 * (t % 2) + part_at, 0:cols]
                    keys = slice(n * part_at, n * part_at + cols)
                    rows = slice(P * i, P * i + P)
                    ins = product(dst, (qT_h[:, u % 2, rows], qT_l[:, u % 2, rows]),
                                  (kT_h[:, u % 2, keys], kT_l[:, u % 2, keys]), True, True)
                ins.then_inc(scores_done, 1)

            def turn(q, s):
                i = s % SEQ_TILES
                pe.wait_ge(probs_ready, STEPS * q + s + 1)
                for n, (slot, count) in enumerate(tile_groups(i)):
                    need(pe, pT_ready, groups_before(q, s) + n - 1)
                    bank = T_BANK + (GROUPS_AT[i] + n) % 2
                    for k in range(count):
                        kt = 2 * (i // 2) + 1 - (slot + k)
                        ins = pe.transpose(ps[:, bank, P * k:P * k + P], probs[s % 4][:, P * kt:P * kt + P], ident[:])
                    ins.then_inc(turned, 1)

            def weigh(u, c, index, q, s, first_unit):
                pe.wait_ge(pT_ready, groups_through(q, s))
                need(pe, o_ready, index)
                if c == 0 and u % 2 == 0:
                    pe.wait_ge(v_ready, 4 * (2 * q + u // 2) + 4)
                if first_unit and c == 0:
                    pe.wait_ge(zeroed, 1)
                head, b = u % 2, u // 2
                slots = 2 * c + 2
                for slot in range(slots):
                    kt = 2 * c + 1 - slot
                    w = tuple(v[:, b, kt, HD * head:HD * head + HD] for v in (v_h, v_l))
                    ins = product(ps[:, PV_BANK, 0:256], w, (pT_h[c % 2][:, slot, :], pT_l[c % 2][:, slot, :]),
                                  slot == 0, slot == slots - 1)
                ins.then_inc(pv_done, 1)

            def project_out(b, c, index, q):
                if c == 0 and b == 0:
                    pe.wait_ge(wa_ready["o"], q + 1)
                pe.wait_ge(o_ready, 16 * q + 8 * b + 4 + c + 1)
                misc_bank_free()
                for half in range(2):
                    at = slice(256 * c + P * half, 256 * c + P * half + P)
                    for head in range(2):
                        o = ((oA_h[:, at], oA_l[:, at]) if head == 0 else
                             tuple(v[:, c % 2, P * half:P * half + P] for v in (oB_h, oB_l)))
                        ins = product(ps[:, MISC_BANK, 256 * half:256 * half + 256], o,
                                      (wa_h["o"][:, head, :], wa_l["o"][:, head, :]), head == 0, head == 1)
                ins.then_inc(y_done, 1)
                bank_user[0] = "o", index

            def attention(p, first, last):
                bank_user[0] = "v", 8 * p + 3
                for t in range(STEPS + (DRAIN_STEPS if last else 0)):
                    if t < STEPS:
                        scores(p, t, first)
                    side(p, t, last)
                    chunk = chunk_of_step(p, t, PV_LAG, first)
                    if chunk:
                        weigh(*chunk, first and t < SEQ_TILES)
                    y = out_of_step(p, t, OUT_LAG, first)
                    if y:
                        project_out(*y)
                    tile = tile_of_step(p, t, T_LAG, first)
                    if tile:
                        turn(*tile)

            ffn(0)
            pe.wait_ge(xnT_ready, KT * 2 * CHUNKS)
            for kind in "kq":
                pe.wait_ge(wa_ready[kind], 1)
            for k in range(4):
                project(k, 0, k)
            pe.wait_ge(wa_ready["v"], 1)
            for k in range(4):
                values(k, 0, k)
            attention(0, True, False)
            with pe.Fori(1, PAIRS - 1) as p:
                attention(p, False, False)
            attention(PAIRS - 1, False, True)
            ffn(1)


def pack_ffn(gate_w, w_up, w_gate, w_down, up_A, up_B, gate_A, gate_B, down_A, down_B):
    def by_kt(a):
        return a.reshape(KT, P, -1).transpose(1, 0, 2)

    def padded(a):
        full = np.zeros((HT * P, a.shape[1]), a.dtype)
        full[:HIDDEN] = a
        return full.reshape(HT, P, -1).transpose(1, 0, 2)

    cut = FULL * P
    a = np.concatenate([up_A.reshape(ER, D).T, gate_A.reshape(ER, D).T], axis=1)
    up, gate = w_up.T, w_gate.T
    base = np.concatenate([up[:, :cut], gate[:, :cut], up[:, cut:], gate[:, cut:]], axis=1)
    up_b = up_B.transpose(0, 2, 1).reshape(ER, HIDDEN)
    gate_b = gate_B.transpose(0, 2, 1).reshape(ER, HIDDEN)
    none = np.zeros((ER, TAIL), up_b.dtype)
    lora = np.concatenate([up_b[:, :cut], gate_b[:, :cut], up_b[:, cut:], none, none, gate_b[:, cut:]], axis=1)
    parts = [by_kt(a), by_kt(gate_w.T), by_kt(base), lora, padded(down_A.reshape(ER, HIDDEN).T),
             padded(w_down.T), down_B.transpose(0, 2, 1).reshape(ER, D)]
    return np.ascontiguousarray(np.concatenate([v.reshape(P, -1) for v in parts], axis=1))


def expand_matrices():
    m = np.zeros((P, 6, P), np.float32)
    for e in range(EXPERTS):
        ranks = slice(RANK * e, RANK * e + RANK)
        m[e, EX_M1, ranks] = ALPHA
        m[EXPERTS + e, EX_M2, ranks] = ALPHA
        m[2 * EXPERTS + e, EX_CM1, ranks] = ALPHA
        m[3 * EXPERTS + e, EX_CM2, ranks] = ALPHA
        m[2 * EXPERTS + e, EX_C1, :] = 1.0
        m[3 * EXPERTS + e, EX_C2, :] = 1.0
    return m.reshape(P, EX_COLS)


def rope_tables():
    half = HD // 2
    fraction = np.float32(2.0) * np.arange(half, dtype=np.float32) / np.float32(HD)
    timescale = np.float32(10000.0) ** fraction
    angle = np.arange(SEQ, dtype=np.float32)[None, :] / timescale[:, None].astype(np.float32)
    sin, cos = np.sin(angle), np.cos(angle)
    table = np.stack([np.concatenate([cos, cos]), np.concatenate([-sin, sin])], axis=1)
    return np.ascontiguousarray(table.astype(np.float32))


def pack_attention(wq, wk, wv, wo):
    order = np.concatenate([np.arange(0, HD, 2), np.arange(1, HD, 2)])

    def by_pair(w):
        w = w.reshape(KT, P, PAIRS, 2, HD).transpose(2, 1, 0, 3, 4)
        return w.reshape(PAIRS, P, KT * 2 * HD)

    o = wo.reshape(PAIRS, 2, HD, D).transpose(0, 2, 1, 3).reshape(PAIRS, P, 2 * D)
    return np.ascontiguousarray(np.stack([by_pair(wv), by_pair(wk[:, :, order]), by_pair(wq[:, :, order]), o], axis=1))


def kernel(**inputs):
    import concourse.bacc as _bacc
    from concourse.bass_utils import run_bass_kernel_spmd as _run

    given = {k: np.asarray(v) for k, v in inputs.items()}
    ffn = [given[f"L0_ffn_{n}"] for n in ("gate_w", "w_up", "w_gate", "w_down", "up_A", "up_B", "gate_A", "gate_B",
                                           "down_A", "down_B")]
    arrays = {
        "x_in": np.ascontiguousarray(given["L0_attn_x"].reshape(TOKENS, D)),
        "ffn_w": pack_ffn(*ffn),
        "expand_w": expand_matrices(),
        "attn_w": pack_attention(*[given[f"L0_attn_{n}"] for n in ("wq", "wk", "wv", "wo")]),
        "rope_w": rope_tables(),
    }
    nc = _bacc.Bacc("TRN2", target_bir_lowering=False, num_devices=1)
    args = [nc.dram_tensor(n, a.shape, mybir.dt.from_np(a.dtype), kind="ExternalInput").ap() for n, a in arrays.items()]
    out = nc.dram_tensor("out", (TOKENS, D), F32, kind="ExternalOutput").ap()
    build(nc, *args, out)
    got = _run(nc, [arrays], core_ids=[0])
    return got.results[0]["out"].reshape(BATCH, SEQ, D)
```

```python
from contextlib import ExitStack

import numpy as np
import concourse.bass as bass
from concourse import mybir

ALU = mybir.AluOpType
ACT = mybir.ActivationFunctionType
AX = mybir.AxisListType
F32 = mybir.dt.float32
F32R = mybir.dt.float32r
BF16 = mybir.dt.bfloat16
U32 = mybir.dt.uint32
I32 = mybir.dt.int32
ds = bass.ds

P = 128
BATCH, SEQ, D = 2, 1024, 256
TOKENS = BATCH * SEQ
TILES = TOKENS // P
SEQ_TILES = SEQ // P
KT = D // P
CHUNK = 512
CHUNKS = TOKENS // CHUNK
CT = CHUNK // P
HEADS, HD = 16, 128
PAIRS = HEADS // 2
EXPERTS, RANK, HIDDEN = 8, 16, 704
ER = EXPERTS * RANK
FULL = HIDDEN // P
TAIL = HIDDEN - FULL * P
HT = FULL + 1
ALPHA = 2.0
EPS = 1e-5
SCALE = 1.0 / float(np.sqrt(np.float32(HD)))
MASKED = -1e30
HUGE = 3.0e38

BASE_TILES = 2 * FULL + 1
LORA_TILES = 2 * FULL + 2
OFF_A = 0
OFF_ROUTE = OFF_A + KT * 2 * ER
OFF_BASE = OFF_ROUTE + KT * EXPERTS
OFF_LORA = OFF_BASE + KT * BASE_TILES * P
OFF_DOWN_A = OFF_LORA + LORA_TILES * P
OFF_DOWN = OFF_DOWN_A + HT * ER
OFF_DOWN_B = OFF_DOWN + HT * D
FFN_COLS = OFF_DOWN_B + D
EARLY_SPLITS = 6
PIECES = 5
PIECE = FFN_COLS // PIECES
SPLITS = 2 * PIECES
SPLIT = FFN_COLS // SPLITS
assert SPLIT * SPLITS == FFN_COLS
assert OFF_LORA + (FULL + 1) * P <= EARLY_SPLITS * SPLIT
MASK_ROWS = 4 * EXPERTS
ROUTE_CHAIN, ROUTE_MAX, ROUTE_SHIFTED, ROUTE_SUMMED = 12, 6, 7, 8
EX_M1, EX_CM1, EX_M2, EX_CM2, EX_C1, EX_C2 = range(6)
EX_COLS = 6 * P

BU, BG, L0, L1, D1, D2, OUT0, OUT1 = range(8)
SPREAD_BANKS = [BU, D1, D2, BU, D1, D2]
LN_BANKS = [(BU, BG), (L0, L1), (D1, D2), (OUT0, OUT1)]
LOGIT_BANKS = [BU, BG, D2, BU]
TURNED_BANKS = [D1, D1, D1, OUT0]
T_BANK, PV_BANK = 4, 6
MISC_BANKS = [1, 3, 7, 3, 7, 7, 7, 7]

UNITS = 4
STEPS = UNITS * SEQ_TILES
T_LAG, PV_LAG, OUT_LAG = 2, 5, 8
ROPE_LAG = 2
PAIR_SPLITS_AT = {"o": 7, "v": 17, "k": 21, "q": 23}
DRAIN_STEPS = OUT_LAG + 1
EARLY_NORMS = 3
STATS_AT, STATS_STEP = [-11, -6, 6], [1, 1, 0]
NORM_AT, TURN_AT = [-1, 2, 7], [2, 3, 8]
DRAIN_SPLIT_AT, DRAIN_SPLITS = 3, 5
GROUPS_AT = [0, 1, 2, 3, 4, 6, 8, 10]
UNIT_GROUPS = 12
KINDS = ["v", "k", "q", "o"]
RAW_OF = {"k": 0, "q": 1, "v": 2, "o": 2}


def tile_groups(i):
    first = 1 - i % 2
    out = []
    while first <= i + 1 - i % 2:
        n = min(4, i + 2 - i % 2 - first)
        out.append((first, n))
        first += n
    return out


def build(nc, x_in, ffn_w, expand_w, attn_w, rope_w, out):
    with ExitStack() as ctx:
        def sem(name):
            return ctx.enter_context(nc.semaphore(name))

        def sbuf(stack, name, shape, dt=F32):
            return stack.enter_context(nc.sbuf_tensor(name, shape, dt))

        x_sb = sbuf(ctx, "x_sb", [P, TILES, D])
        xnT_h = sbuf(ctx, "xnT_h", [P, KT, TOKENS], F32R)
        xnT_l = sbuf(ctx, "xnT_l", [P, KT, TOKENS], F32R)
        ident = sbuf(ctx, "ident", [P, P])
        causal = sbuf(ctx, "causal", [P, SEQ], BF16)
        stats = sbuf(ctx, "stats", [P, 2, CT, 6])
        mean_var = sbuf(ctx, "mean_var", [P, 2, CT, 2])
        var_eps = sbuf(ctx, "var_eps", [P, 2, CT])
        rstd = sbuf(ctx, "rstd", [P, 2, CT])
        minus_half = sbuf(ctx, "minus_half", [P, CT])
        table_scratch = sbuf(ctx, "table_scratch", [P, 1])
        ps = ctx.enter_context(nc.psum_tensor("ps", [P, 8, 512], F32))

        with ExitStack() as st:
            w_in = sbuf(st, "w_in", [P, FFN_COLS])
        with ExitStack() as st:
            w_l = sbuf(st, "w_l", [P, FFN_COLS], F32R)
            expand_raw = sbuf(st, "expand_raw", [P, EX_COLS])
            xn = sbuf(st, "xn", [P, CT, D])
            spread = sbuf(st, "spread", [P, 6, CHUNK])
            w_h = sbuf(st, "w_h", [P, FFN_COLS], F32R)
            expand = sbuf(st, "expand", [P, 6, P], F32R)
            cm = sbuf(st, "cm", [P, TILES, MASK_ROWS])
            cm_pad = sbuf(st, "cm_pad", [P, CT, P])
            maskT_h = sbuf(st, "maskT_h", [P, CHUNK], F32R)
            maskT_l = sbuf(st, "maskT_l", [P, CHUNK], F32R)
            um_h = sbuf(st, "um_h", [P, 4, CHUNK], F32R)
            um_l = sbuf(st, "um_l", [P, 4, CHUNK], F32R)
            base_up = sbuf(st, "base_up", [P, 2, CHUNK])
            base_gate = sbuf(st, "base_gate", [P, 2, CHUNK])
            up_act = sbuf(st, "up_act", [P, 2, CHUNK])
            hid = sbuf(st, "hid", [P, 2, CHUNK])
            hid_h = sbuf(st, "hid_h", [P, 2, 2, CHUNK], F32R)
            hid_l = sbuf(st, "hid_l", [P, 2, 2, CHUNK], F32R)
            mixed = sbuf(st, "mixed", [P, CHUNK])
            mixed_h = sbuf(st, "mixed_h", [P, 2, CHUNK], F32R)
            mixed_l = sbuf(st, "mixed_l", [P, 2, CHUNK], F32R)
            dm_h = sbuf(st, "dm_h", [P, CHUNK], F32R)
            dm_l = sbuf(st, "dm_l", [P, CHUNK], F32R)
            top8 = sbuf(st, "top8", [P, TILES, 8])
            top_at = sbuf(st, "top_at", [P, TILES, 8], U32)
            top_f = sbuf(st, "top_f", [P, TILES, 2])
            expert_i = sbuf(st, "expert_i", [P, EXPERTS], I32)
            expert_f = sbuf(st, "expert_f", [P, EXPERTS])
            part = sbuf(st, "part", [P, 3, 2 * BATCH])
            whole = sbuf(st, "whole", [P, 2, 2 * BATCH])
            route = sbuf(st, "route", [P, TILES, 2])

        with ExitStack() as st:
            rope = sbuf(st, "rope", [P, 2, SEQ])
            w_raw = [sbuf(st, f"w_raw{i}", [P, 512]) for i in range(3)]
            wa_h = {k: sbuf(st, f"w{k}_h", [P, 2, 256], F32R) for k in "vkq"}
            wa_l = {k: sbuf(st, f"w{k}_l", [P, 2, 256], F32R) for k in "vkq"}
            swapped = sbuf(st, "swapped", [P, 512])
            rot = sbuf(st, "rot", [P, 2, 512])
            rot_sin = sbuf(st, "rot_sin", [P, 512])
            qT_h = sbuf(st, "qT_h", [P, 2, SEQ], F32R)
            qT_l = sbuf(st, "qT_l", [P, 2, SEQ], F32R)
            kT_h = sbuf(st, "kT_h", [P, 2, SEQ], F32R)
            kT_l = sbuf(st, "kT_l", [P, 2, SEQ], F32R)
            wa_h["o"] = sbuf(st, "wo_h", [P, 2, 256], F32R)
            wa_l["o"] = sbuf(st, "wo_l", [P, 2, 256], F32R)
            oA_h = sbuf(st, "oA_h", [P, SEQ], F32R)
            oA_l = sbuf(st, "oA_l", [P, SEQ], F32R)
            v_h = sbuf(st, "v_h", [P, BATCH, SEQ_TILES, 256], F32R)
            v_l = sbuf(st, "v_l", [P, BATCH, SEQ_TILES, 256], F32R)
            pT_h = [sbuf(st, f"pT_h{i}", [P, 6 + 2 * i, 256], F32R) for i in range(2)]
            pT_l = [sbuf(st, f"pT_l{i}", [P, 6 + 2 * i, 256], F32R) for i in range(2)]
            probs = [sbuf(st, f"probs{i}", [P, P * (SEQ_TILES - 3 + i)]) for i in range(4)]
            oB_h = sbuf(st, "oB_h", [P, 2, 256], F32R)
            oB_l = sbuf(st, "oB_l", [P, 2, 256], F32R)
            neg_max = sbuf(st, "neg_max", [P, 4])
            row_sum = sbuf(st, "row_sum", [P, 4])
            inv_sum = sbuf(st, "inv_sum", [P, 4])

        x_loaded = [sem(f"x_loaded{c}") for c in range(CHUNKS)]
        consts_made = sem("consts_made")
        w_loaded = [sem(f"w_loaded{i}") for i in range(PIECES)]
        expand_loaded = sem("expand_loaded")
        expand_ready = sem("expand_ready")
        w_high = sem("w_high")
        w_ready = sem("w_ready")
        ln_stats = sem("ln_stats")
        ln_aggr = sem("ln_aggr")
        ln_var = sem("ln_var")
        ln_rstd = sem("ln_rstd")
        xn_ready = sem("xn_ready")
        xn_turned = sem("xn_turned")
        xn_high = sem("xn_high")
        xnT_ready = sem("xnT_ready")
        logitsT_done = sem("logitsT_done")
        logitsT_kept = sem("logitsT_kept")
        logits_ready = sem("logits_ready")
        route_chain = sem("route_chain")
        route_whole = sem("route_whole")
        route_exp = sem("route_exp")
        cm_padded = sem("cm_padded")
        mask_turned = sem("mask_turned")
        mask_high = sem("mask_high")
        mask_ready = sem("mask_ready")
        low_rank = sem("low_rank")
        spread_done = sem("spread_done")
        spread_kept = sem("spread_kept")
        um_raw = sem("um_raw")
        um_high = sem("um_high")
        um_ready = sem("um_ready")
        um_ready_pool = sem("um_ready_pool")
        base_done = sem("base_done")
        lora_done = sem("lora_done")
        base_up_kept = sem("base_up_kept")
        base_gate_kept = sem("base_gate_kept")
        up_summed = sem("up_summed")
        up_act_done = sem("up_act_done")
        gate_summed = sem("gate_summed")
        hid_done = sem("hid_done")
        hid_high = sem("hid_high")
        hid_ready = sem("hid_ready")
        mixed_done = sem("mixed_done")
        mixed_high = sem("mixed_high")
        mixed_ready = sem("mixed_ready")
        mixed_used = sem("mixed_used")
        tail_mixed = sem("tail_mixed")
        tail_ready = sem("tail_ready")
        down_a_done = sem("down_a_done")
        dm_parts = sem("dm_parts")
        dm_raw = sem("dm_raw")
        dm_high = sem("dm_high")
        dm_ready = sem("dm_ready")
        out_done = sem("out_done")
        x_updated = sem("x_updated")
        rope_loaded = sem("rope_loaded")
        wa_loaded = {k: sem(f"w{k}_loaded") for k in KINDS}
        wa_high = {k: sem(f"w{k}_high") for k in KINDS}
        wa_ready = {k: sem(f"w{k}_ready") for k in KINDS}
        zeroed = sem("zeroed")
        proj_done = sem("proj_done")
        proj_swapped = sem("proj_swapped")
        proj_cos = sem("proj_cos")
        proj_sin = sem("proj_sin")
        proj_rot = sem("proj_rot")
        proj_high = sem("proj_high")
        proj_ready = sem("proj_ready")
        v_done = sem("v_done")
        v_high = sem("v_high")
        v_ready = sem("v_ready")
        scores_done = sem("scores_done")
        max_done = sem("max_done")
        exp_done = sem("exp_done")
        inv_done = sem("inv_done")
        probs_ready = sem("probs_ready")
        turned = sem("turned")
        pT_high = sem("pT_high")
        pT_ready = sem("pT_ready")
        pv_done = sem("pv_done")
        o_high = sem("o_high")
        o_ready = sem("o_ready")
        y_done = sem("y_done")
        y_added = sem("y_added")
        stored = sem("stored")

        def need(eng, semaphore, count):
            if not isinstance(count, int) or count > 0:
                eng.wait_ge(semaphore, count)

        def low(eng, dst, src, high):
            return eng.tensor_tensor(dst, src, high.bitcast(F32), ALU.subtract)

        def logitsT(c):
            return (base_up, base_gate)[c // 2][0:EXPERTS, c % 2, :]

        def rope_low_part(eng, index, u, k):
            eng.wait_ge(proj_high, index + 1)
            h, l = ((kT_h, kT_l), (qT_h, qT_l))[k % 2]
            cols = slice(512 * (k // 2), 512 * (k // 2) + 512)
            low(eng, l[:, u % 2, cols], rot[:, k % 2], h[:, u % 2, cols]).then_inc(proj_ready, 1)

        def xn_of(c):
            return spread[:, 0:2].rearrange("p a (b d) -> p (a b) d", d=D) if c % 2 else xn

        xn_last = probs[3][:].rearrange("p (a d) -> p a d", a=CT)

        def chunk_tiles(c):
            return x_sb[:, ds(CT * c, CT), :]

        def chunk_cols(c):
            return ds(CHUNK * c, CHUNK)

        def w_a(w, kt, gate):
            at = OFF_A + kt * 2 * ER + gate * ER
            return w[:, at:at + ER]

        def w_route(w, kt):
            at = OFF_ROUTE + kt * EXPERTS
            return w[:, at:at + P]

        def w_base(w, kt, tile):
            at = OFF_BASE + (kt * BASE_TILES + tile) * P
            return w[:, at:at + P]

        def w_lora(w, tile):
            at = OFF_LORA + tile * P
            return w[:, at:at + P]

        def w_down_a(w, m):
            at = OFF_DOWN_A + m * ER
            return w[:, at:at + ER]

        def w_down(w, m):
            at = OFF_DOWN + m * D
            return w[:, at:at + D]

        def w_down_b(w):
            return w[:, OFF_DOWN_B:OFF_DOWN_B + D]

        def unit_of(t):
            return t // SEQ_TILES, t % SEQ_TILES

        def tile_at(p, t):
            return (p, t) if t >= 0 else (p - 1, t + STEPS)

        def groups_before(p, t):
            u, i = unit_of(t)
            return UNITS * UNIT_GROUPS * p + UNIT_GROUPS * u + GROUPS_AT[i]

        def groups_through(p, t):
            return groups_before(p, t) + len(tile_groups(t % SEQ_TILES))

        def side_work(p, t, first, last):
            if t >= STEPS:
                return None
            u, i = unit_of(t)
            k = i // 2
            if i % 2 == 0:
                if u == UNITS - 1 and last:
                    return None
                return "proj", (u + 1) % UNITS, 4 * (UNITS * p + u + 1) + k, k
            if first and u == 0:
                return "v", 0, k, k
            if u % 2 == 1:
                if u == UNITS - 1 and last:
                    return None
                return "v", (u // 2 + 1) % 2, 4 * (2 * p + u // 2 + 1) + k, k
            return None

        def misc_bank(t):
            return MISC_BANKS[t % SEQ_TILES] if t < STEPS else MISC_BANKS[-1]

        def rotation_to_end(p, t, first, last):
            if t < ROPE_LAG:
                work = None if first else side_work(p - 1, t - ROPE_LAG + STEPS, False, False)
            else:
                work = side_work(p, t - ROPE_LAG, first, last)
            return work if work and work[0] == "proj" else None

        def tile_of_step(p, t, lag, first):
            q, s = tile_at(p, t - lag)
            return None if (first and t < lag) or t - lag >= STEPS else (q, s)

        def chunk_of_step(p, t, lag, first):
            tile = tile_of_step(p, t, lag, first)
            if not tile or tile[1] % 2 == 0:
                return None
            q, s = tile
            u, i = unit_of(s)
            return u, i // 2, 16 * q + 4 * u + i // 2, q, s

        def out_of_step(p, t, lag, first):
            chunk = chunk_of_step(p, t, lag, first)
            if not chunk or chunk[0] % 2 == 0:
                return None
            u, c, _, q, _ = chunk
            return u // 2, c, 4 * (2 * q + u // 2) + c, q

        def score_view(slot, i):
            n = P * (i + 1)
            if n <= 512:
                return ps[:, 2 * slot:2 * slot + 1, 0:n], 1, n
            return ps[:, 2 * slot:2 * slot + 2, 0:n // 2], 2, n // 2

        block = ctx.enter_context(nc.Block())

        @block.sync
        def _(sp):
            def load_ffn():
                for n in range(PIECES):
                    at = slice(n * PIECE, (n + 1) * PIECE)
                    sp.dma_start(w_in[:, at], ffn_w[:, at]).then_inc(w_loaded[n], 16)
                sp.dma_start(expand_raw[:], expand_w).then_inc(expand_loaded, 16)

            def load(p, kind):
                sp.dma_start(w_raw[RAW_OF[kind]][:], attn_w[p, KINDS.index(kind)]).then_inc(wa_loaded[kind], 16)

            def load_pair(p):
                for kind, last, count in (("k", "k", p), ("q", "q", p), ("v", "o", p), ("o", "v", p + 1)):
                    sp.wait_ge(wa_ready[last], count)
                    sp.nop(nofuse=True)
                    load(p, kind)

            x_view = x_in.rearrange("(c t p) d -> c p t d", t=CT, p=P)
            out_view = out.rearrange("(c t p) d -> c p t d", t=CT, p=P)
            for c in range(CHUNKS):
                sp.dma_start(chunk_tiles(c), x_view[c]).then_inc(x_loaded[c], 16)
            load_ffn()
            sp.wait_ge(base_done, BASE_TILES * CHUNKS)
            load(0, "k")
            load(0, "q")
            sp.dma_start(rope[:], rope_w).then_inc(rope_loaded, 16)
            sp.wait_ge(lora_done, 2 * LORA_TILES * CHUNKS - 2 * CHUNKS)
            load(0, "v")
            sp.wait_ge(wa_ready["v"], 1)
            load(0, "o")
            with sp.Fori(1, PAIRS) as p:
                load_pair(p)
            sp.wait_ge(proj_ready, UNITS * 4 * PAIRS)
            sp.wait_ge(v_done, 2 * 4 * PAIRS)
            sp.wait_ge(wa_ready["o"], PAIRS)
            load_ffn()
            with sp.Fori(0, CHUNKS) as c:
                sp.wait_ge(x_updated, 2 * c + (2 * CHUNKS + 2))
                sp.dma_start(out_view[c], chunk_tiles(c)).then_inc(stored, 16)
            sp.wait_ge(stored, 16 * CHUNKS)

        @block.gpsimd
        def _(pool):
            pool.memset(ident[:], 0.0).then_inc(consts_made, 1)
            pool.memset(causal[:], 0.0).then_inc(consts_made, 1)
            pool.memset(minus_half[:], -0.5).then_inc(consts_made, 1)
            pool.wait_ge(consts_made, 3)
            pool.affine_select(out=ident[:], in_=ident[:], compare_op=ALU.not_equal, fill=1.0, base=0,
                               pattern=[[-1, P]], channel_multiplier=1).then_inc(consts_made, 1)
            pool.affine_select(out=causal[:, SEQ - P:], in_=causal[:, SEQ - P:], compare_op=ALU.is_ge,
                               fill=MASKED, base=0, pattern=[[-1, P]], channel_multiplier=1)\
                .then_inc(consts_made, 1)

            def layer_norm(n, k=0):
                pool.wait_ge(ln_var, n + 1)
                pool.tensor_tensor(rstd[:, k], var_eps[:, k], minus_half[:], ALU.pow).then_inc(ln_rstd, 1)

            def split_ffn(f, n):
                pool.wait_ge(w_high, SPLITS * f + n + 1)
                at = slice(n * SPLIT, (n + 1) * SPLIT)
                low(pool, w_l[:, at], w_in[:, at], w_h[:, at]).then_inc(w_ready, 1)

            def router(f):
                pool.wait_ge(route_chain, ROUTE_CHAIN * f + ROUTE_MAX)
                pool.partition_all_reduce(whole[:, 0, :], part[:, 0, :], P, bass.bass_isa.ReduceOp.max)\
                    .then_inc(route_whole, 1)
                pool.wait_ge(route_chain, ROUTE_CHAIN * f + ROUTE_SUMMED)
                pool.partition_all_reduce(whole[:, 1, :], part[:, 1, :], P, bass.bass_isa.ReduceOp.add)\
                    .then_inc(route_whole, 1)

            def ffn_chunk(g, c, f, first):
                pool.wait_ge(um_high, 4 * g + 4)
                need(pool, lora_done, 22 * g)
                low(pool, um_l[:, 3], hid[:, 1], um_h[:, 3]).then_inc(um_ready_pool, 1)
                for m in range(HT):
                    rows = P if m < FULL else TAIL
                    for j in range(2 if m < FULL else 1):
                        if j == 1:
                            pool.wait_ge(hid_done, 12 * g + 2 * m + 2)
                            if m == 0:
                                need(pool, tail_ready, 2 * g)
                            else:
                                pool.wait_ge(mixed_ready, 5 * g + m)
                            pool.tensor_tensor(mixed[:], hid[:, 0], hid[:, 1], ALU.add).then_inc(mixed_done, 1)
                        pool.wait_ge(hid_high, 12 * g + 2 * m + j + 1)
                        low(pool, hid_l[0:rows, m % 2, j], hid[0:rows, j], hid_h[0:rows, m % 2, j])\
                            .then_inc(hid_ready, 1)
                        if f == 0 and not first and (m, j) == (3, 0):
                            layer_norm(c + 3)
                    if m < FULL:
                        pool.wait_ge(mixed_high, 6 * g + m + 1)
                        low(pool, mixed_l[:, m % 2], mixed[:], mixed_h[:, m % 2]).then_inc(mixed_ready, 1)
            def ffn(f):
                if f == 0:
                    for c in range(CHUNKS):
                        layer_norm(c, c % 2)
                        if c == CHUNKS - 2:
                            split_ffn(f, 0)
                else:
                    layer_norm(2 * CHUNKS + EARLY_NORMS, EARLY_NORMS % 2)
                    pool.wait_ge(y_added, 8 * PAIRS)
                pool.iota(expert_i[:], pattern=[[1, EXPERTS]], base=0, channel_multiplier=0).then_inc(route_whole, 1)
                for n in range(1 if f == 0 else DRAIN_SPLITS, EARLY_SPLITS):
                    split_ffn(f, n)
                router(f)
                for n in range(EARLY_SPLITS, SPLITS):
                    split_ffn(f, n)
                ffn_chunk(4 * f, 0, f, True)
                if f == 0:
                    ffn_chunk(1, 1, f, False)
                with pool.Fori(2 - f, CHUNKS) as c:
                    ffn_chunk(c + 4 * f, c, f, False)

            def rope_sin(index, ch):
                pool.wait_ge(proj_swapped, index + 1)
                need(pool, proj_rot, index)
                pool.tensor_tensor(rot_sin[:], swapped[:], rope[:, 1, 512 * ch:512 * ch + 512], ALU.mult)\
                    .then_inc(proj_sin, 1)

            def attention(p, first, last):
                for t in range(STEPS + (DRAIN_STEPS if last else 0)):
                    q, s = tile_at(p, t - 1)
                    if s < STEPS and not (first and t == 0):
                        n = P * (s % SEQ_TILES + 1)
                        pool.wait_ge(inv_done, STEPS * q + s + 1)
                        pool.nop(nofuse=True)
                        pool.tensor_scalar(probs[s % 4][:, 0:n], probs[s % 4][:, 0:n], inv_sum[:, s % 4:s % 4 + 1], 1.0,
                                           ALU.mult, ALU.mult).then_inc(probs_ready, 1)
                    side = side_work(p, t, first, last)
                    if side and side[0] == "proj":
                        rope_sin(side[2], side[3] // 2)
                    turn = rotation_to_end(p, t, first, last)
                    if turn:
                        rope_low_part(pool, turn[2], turn[1], turn[3])
                    if last:
                        for c in range(EARLY_NORMS):
                            if t == STEPS + STATS_AT[c] + CT * STATS_STEP[c] + 1:
                                layer_norm(2 * CHUNKS + c, c % 2)
                        if 0 <= t - STEPS - DRAIN_SPLIT_AT - 1 < DRAIN_SPLITS:
                            split_ffn(1, t - STEPS - DRAIN_SPLIT_AT - 1)

            ffn(0)
            pool.wait_ge(rope_loaded, 16)
            for k in range(4):
                rope_sin(k, k // 2)
                if k == 1:
                    layer_norm(2 * CHUNKS - 1)
            for i in range(2):
                pool.memset(pT_h[i][:, 0, 0:P].bitcast(F32), 0.0)
                last_zero = pool.memset(pT_l[i][:, 0, 0:P].bitcast(F32), 0.0)
            last_zero.then_inc(zeroed, 1)
            attention(0, True, False)
            with pool.Fori(1, PAIRS - 1) as p:
                attention(p, False, False)
            attention(PAIRS - 1, False, True)
            ffn(1)

        @block.scalar
        def _(act):
            def split_ffn(f, n):
                act.wait_ge(w_loaded[n // 2], 16 * (f + 1))
                at = slice(n * SPLIT, (n + 1) * SPLIT)
                act.activation(w_h[:, at], w_in[:, at], ACT.Copy).then_inc(w_high, 1)

            def keep_logits(f, c):
                act.wait_ge(logitsT_done, 4 * f + c + 1)
                act.activation(logitsT(c), ps[0:EXPERTS, LOGIT_BANKS[c], :], ACT.Copy).then_inc(logitsT_kept, 1)

            def layer_norm_high(n, c, banks=(OUT0, OUT1)):
                for kt in range(KT):
                    act.wait_ge(xn_turned, KT * n + (kt + 1))
                    act.activation(xnT_h[:, kt, chunk_cols(c)], ps[:, banks[kt], :], ACT.Copy)\
                        .then_inc(xn_high, 1)

            def ffn_chunk(g, c, f, first, turns=False):
                if turns:
                    layer_norm_high(c + 2, c - 2, (D1, D2))
                act.wait_ge(mask_turned, g + 1)
                act.activation(maskT_h[:], ps[:, BU, :], ACT.Copy).then_inc(mask_high, 1)
                for e in range(EX_C2 + 1):
                    act.wait_ge(spread_done, 6 * g + e + 1)
                    act.activation(spread[:, e], ps[:, SPREAD_BANKS[e], :], ACT.Copy).then_inc(spread_kept, 1)
                    for s in ((), (), (), (0,), (1, 2), (3,))[e]:
                        act.wait_ge(um_raw, 4 * g + s + 1)
                        act.activation(um_h[:, s], (up_act, hid)[s % 2][:, s // 2], ACT.Copy).then_inc(um_high, 1)
                for m in range(HT):
                    rows = P if m < FULL else TAIL
                    act.wait_ge(base_done, 11 * g + (2 * m + 1 if m > 0 else 2))
                    if m >= 2:
                        act.wait_ge(up_summed, 12 * g + 2 * (m - 1))
                    else:
                        need(act, up_summed, 12 * g)
                    act.activation(base_up[0:rows, m % 2], ps[0:rows, BU, :], ACT.Copy).then_inc(base_up_kept, 1)
                    if m > 0:
                        act.wait_ge(mixed_done, 5 * g + m)
                        act.activation(mixed_h[:, (m - 1) % 2], mixed[:], ACT.Copy).then_inc(mixed_high, 1)
                    for j in range(2):
                        act.wait_ge(up_summed, 12 * g + 2 * m + j + 1)
                        act.activation(up_act[0:rows, j], up_act[0:rows, j], ACT.Silu).then_inc(up_act_done, 1)
                        act.wait_ge(hid_done, 12 * g + 2 * m + j + 1)
                        act.activation(hid_h[0:rows, m % 2, j], hid[0:rows, j], ACT.Copy).then_inc(hid_high, 1)
                act.wait_ge(tail_mixed, g + 1)
                act.wait_ge(mixed_used, g + 1)
                act.activation(mixed_h[0:TAIL, FULL % 2], mixed[0:TAIL], ACT.Copy).then_inc(mixed_high, 1)
                act.wait_ge(dm_raw, g + 1)
                act.activation(dm_h[:], base_gate[:, 0], ACT.Copy).then_inc(dm_high, 1)

            def ffn(f):
                if f == 0:
                    for c in range(CHUNKS):
                        layer_norm_high(c, c, LN_BANKS[c])
                        for n in range(2 * c, 2 * c + 2):
                            split_ffn(f, n)
                        if c > 0:
                            keep_logits(f, c - 1)
                else:
                    layer_norm_high(2 * CHUNKS + EARLY_NORMS - 1, EARLY_NORMS - 1, LN_BANKS[EARLY_NORMS - 1])
                    act.wait_ge(y_added, 8 * PAIRS)
                    for c in range(EARLY_NORMS):
                        keep_logits(f, c)
                    for n in range(DRAIN_SPLITS, EARLY_SPLITS):
                        split_ffn(f, n)
                    layer_norm_high(2 * CHUNKS + EARLY_NORMS, EARLY_NORMS, LN_BANKS[EARLY_NORMS])
                keep_logits(f, CHUNKS - 1)
                for n in range(2 * CHUNKS if f == 0 else EARLY_SPLITS, SPLITS):
                    split_ffn(f, n)
                act.wait_ge(expand_loaded, 16 * (f + 1))
                act.activation(expand[:].rearrange("p a b -> p (a b)"), expand_raw[:], ACT.Copy).then_inc(expand_ready, 1)
                act.wait_ge(route_chain, ROUTE_CHAIN * f + ROUTE_SHIFTED)
                act.activation(route[:], route[:], ACT.Exp).then_inc(route_exp, 1)
                act.activation(table_scratch[:], minus_half[:, 0:1], ACT.Silu)
                ffn_chunk(4 * f, 0, f, True)
                if f == 0:
                    ffn_chunk(1, 1, f, False)
                with act.Fori(2 - f, CHUNKS) as c:
                    ffn_chunk(c + 4 * f, c, f, False, f == 0)
                if f == 0:
                    layer_norm_high(2 * CHUNKS - 2, CHUNKS - 2, (D1, D2))

            def split_pair(kind, p):
                act.wait_ge(wa_loaded[kind], 16 * (p + 1))
                if kind in "kq":
                    need(act, proj_done, 16 * p - (kind == "k"))
                elif kind == "v":
                    need(act, v_done, 8 * p)
                else:
                    need(act, y_done, 8 * p)
                act.activation(wa_h[kind][:].rearrange("p a b -> p (a b)"), w_raw[RAW_OF[kind]][:], ACT.Copy)\
                    .then_inc(wa_high[kind], 1)

            def swap_halves(index, bank):
                act.wait_ge(proj_cos, index + 1)
                need(act, proj_sin, index)
                act.activation(swapped[0:64], ps[64:128, bank, :], ACT.Copy)
                act.activation(swapped[64:128], ps[0:64, bank, :], ACT.Copy).then_inc(proj_swapped, 1)

            def rope_high(index, u, k):
                act.wait_ge(proj_rot, index + 1)
                h = (kT_h, qT_h)[k % 2]
                act.activation(h[:, u % 2, 512 * (k // 2):512 * (k // 2) + 512], rot[:, k % 2], ACT.Copy)\
                    .then_inc(proj_high, 1)

            def value_high(index, b, k, bank):
                act.wait_ge(v_done, index + 1)
                act.activation(v_h[:, b, 2 * k:2 * k + 2, :].rearrange("p a b -> p (a b)"), ps[:, bank, :],
                               ACT.Copy).then_inc(v_high, 1)

            def attention(p, first, last):
                for t in range(STEPS + (DRAIN_STEPS if last else 0)):
                    tile = tile_of_step(p, t, T_LAG + 1, first)
                    if tile:
                        q, s = tile
                        i = s % SEQ_TILES
                        half = P * (i % 2)
                        for n, (slot, count) in enumerate(tile_groups(i)):
                            act.wait_ge(turned, groups_before(q, s) + n + 1)
                            bank = T_BANK + (GROUPS_AT[i] + n) % 2
                            act.activation(pT_h[i // 2 % 2][:, slot:slot + count, half:half + P],
                                           ps[:, bank, 0:P * count].rearrange("p (a b) -> p a b", a=count),
                                           ACT.Copy).then_inc(pT_high, 1)
                    turn = rotation_to_end(p, t, first, last)
                    if turn:
                        rope_high(turn[2], turn[1], turn[3])
                    chunk = chunk_of_step(p, t, PV_LAG + 1, first)
                    if chunk:
                        u, c, index, _, _ = chunk
                        dst = oA_h[:, 256 * c:256 * c + 256] if u % 2 == 0 else oB_h[:, c % 2]
                        act.wait_ge(pv_done, index + 1)
                        act.activation(dst, ps[:, PV_BANK, 0:256], ACT.Copy).then_inc(o_high, 1)
                    side = side_work(p, t, first, last)
                    if side and side[0] == "v":
                        value_high(side[2], side[1], side[3], misc_bank(t))
                    if t < STEPS:
                        view, a, n = score_view(t % 2, t % SEQ_TILES)
                        act.wait_ge(max_done, STEPS * p + t + 1)
                        if not (first and t < 4):
                            act.wait_ge(turned, groups_through(*tile_at(p, t - 4)))
                        act.activation(probs[t % 4][:, 0:a * n].rearrange("p (a n) -> p a n", a=a), view, ACT.Exp,
                                       bias=neg_max[:, t % 4:t % 4 + 1], scale=-1.0,
                                       accum_out=row_sum[:, t % 4:t % 4 + 1]).then_inc(exp_done, 1)
                    if first and t < 2:
                        rope_high(2 + t, 0, 2 + t)
                    if first and t == 0:
                        layer_norm_high(2 * CHUNKS - 1, CHUNKS - 1)
                    if side and side[0] == "proj":
                        swap_halves(side[2], misc_bank(t))
                    for kind, at in PAIR_SPLITS_AT.items():
                        if t == at and (kind == "o" or not last):
                            split_pair(kind, p + (kind != "o"))
                    if last:
                        for c in range(EARLY_NORMS):
                            if t == STEPS + TURN_AT[c] + 1:
                                layer_norm_high(2 * CHUNKS + c, c, LN_BANKS[c])
                        if 0 <= t - STEPS - DRAIN_SPLIT_AT < DRAIN_SPLITS:
                            if t == STEPS + DRAIN_SPLIT_AT:
                                act.wait_ge(scores_done, STEPS * PAIRS)
                            split_ffn(1, t - STEPS - DRAIN_SPLIT_AT)

            ffn(0)
            act.activation(table_scratch[:], minus_half[:, 0:1], ACT.Exp)
            act.wait_ge(out_done, 2 * CHUNKS)
            for kind in "kq":
                split_pair(kind, 0)
            swap_halves(0, 0)
            swap_halves(1, 1)
            split_pair("v", 0)
            rope_high(0, 0, 0)
            rope_high(1, 0, 1)
            swap_halves(2, 2)
            swap_halves(3, 3)
            attention(0, True, False)
            with act.Fori(1, PAIRS - 1) as p:
                attention(p, False, False)
            attention(PAIRS - 1, False, True)
            ffn(1)

        @block.vector
        def _(dve):
            def layer_norm_stats(n, c, k=0):
                for tt in range(CT):
                    tile_stats(c, tt, k, tt == CT - 1)
                aggregate(n, k)

            def tile_stats(c, tt, k, is_last):
                ins = dve.bn_stats(stats[:, k, tt, :], x_sb[:, ds(CT * c + tt, 1), :].rearrange("p a d -> p (a d)"))
                if is_last:
                    ins.then_inc(ln_stats, 1)

            def aggregate(n, k):
                dve.wait_ge(ln_stats, n + 1)
                dve.nop(nofuse=True)
                for tt in range(CT):
                    ins = dve.bn_aggr(mean_var[:, k, tt, :], stats[:, k, tt, :])
                ins.then_inc(ln_aggr, 1)
                dve.wait_ge(ln_aggr, n + 1)
                dve.tensor_scalar(var_eps[:, k], mean_var[:, k, :, 1], EPS, None, ALU.add).then_inc(ln_var, 1)

            def layer_norm(n, c, k=0, dst=xn, ahead=0, tiles=range(CT)):
                if tiles[0] == 0:
                    dve.wait_ge(ln_rstd, n + 1)
                    need(dve, xn_turned, KT * (n - ahead))
                for tt in tiles:
                    ins = dve.tensor_scalar(dst[:, tt, :], x_sb[:, ds(CT * c + tt, 1), :].rearrange("p a d -> p (a d)"),
                                            mean_var[:, k, tt, 0:1], rstd[:, k, tt:tt + 1], ALU.subtract, ALU.mult)
                if tiles[-1] == CT - 1:
                    ins.then_inc(xn_ready, 1)

            def layer_norm_low(n, c, banks=(OUT0, OUT1)):
                for kt in range(KT):
                    dve.wait_ge(xn_high, KT * n + (kt + 1))
                    low(dve, xnT_l[:, kt, chunk_cols(c)], ps[:, banks[kt], :], xnT_h[:, kt, chunk_cols(c)])\
                        .then_inc(xnT_ready, 1)

            def router(f):
                steps = [ROUTE_CHAIN * f]

                def link(ins):
                    steps[0] += 1
                    ins.then_inc(route_chain, 1)
                    dve.wait_ge(route_chain, steps[0])

                def of_batch(b):
                    return slice(b * SEQ_TILES, (b + 1) * SEQ_TILES)

                def logits(tile):
                    return ps[:, TURNED_BANKS[tile // CT], EXPERTS * tile:EXPERTS * tile + EXPERTS]

                def spread_over(v, b):
                    return v[:, None, 2 * b:2 * b + 2].to_broadcast([P, SEQ_TILES, 2])

                for n, tiles in enumerate((range(TILES - CT), range(TILES - CT, TILES))):
                    dve.wait_ge(logits_ready, 2 * f + n + 1)
                    for tile in tiles:
                        ins = dve.max(top8[:, tile, :], logits(tile))
                    link(ins)
                    for tile in tiles:
                        ins = dve.max_index(top_at[:, tile, :], top8[:, tile, :], logits(tile))
                    link(ins)
                dve.wait_ge(route_whole, 3 * f + 1)
                dve.tensor_copy(expert_f[:], expert_i[:])
                link(dve.tensor_copy(top_f[:], top_at[:, :, 0:2]))
                for b in range(BATCH):
                    ins = dve.tensor_reduce(part[:, 0, 2 * b:2 * b + 2],
                                            top8[:, of_batch(b), 0:2].rearrange("p t j -> p j t"), AX.X, ALU.max)
                link(ins)
                dve.wait_ge(route_whole, 3 * f + 2)
                for b in range(BATCH):
                    ins = dve.tensor_tensor(route[:, of_batch(b), :], top8[:, of_batch(b), 0:2],
                                            spread_over(whole[:, 0, :], b), ALU.subtract)
                link(ins)
                dve.wait_ge(route_exp, f + 1)
                for b in range(BATCH):
                    ins = dve.tensor_reduce(part[:, 1, 2 * b:2 * b + 2],
                                            route[:, of_batch(b), :].rearrange("p t j -> p j t"), AX.X, ALU.add)
                link(ins)
                for j in range(2):
                    ins = dve.tensor_tensor(cm[:, :, EXPERTS * j:EXPERTS * j + EXPERTS],
                                            expert_f[:, None, :].to_broadcast([P, TILES, EXPERTS]),
                                            top_f[:, :, j:j + 1].to_broadcast([P, TILES, EXPERTS]), ALU.is_equal)
                link(ins)
                dve.wait_ge(route_whole, 3 * f + 3)
                link(dve.reciprocal(part[:, 2, :], whole[:, 1, :]))
                for b in range(BATCH):
                    ins = dve.tensor_tensor(route[:, of_batch(b), :], route[:, of_batch(b), :],
                                            spread_over(part[:, 2, :], b), ALU.mult)
                link(ins)
                for j in range(2):
                    ins = dve.tensor_tensor(cm[:, :, EXPERTS * (2 + j):EXPERTS * (3 + j)],
                                            cm[:, :, EXPERTS * j:EXPERTS * j + EXPERTS],
                                            route[:, :, j:j + 1].to_broadcast([P, TILES, EXPERTS]), ALU.mult)
                link(ins)

            def update_x(g, c, banks=(0, 1)):
                for k in banks:
                    dve.wait_ge(out_done, 2 * g + (k + 1))
                    tiles = x_sb[:, ds(CT * c + 2 * k, 2), :].rearrange("p a d -> p (a d)")
                    dve.scalar_tensor_tensor(out=tiles, in0=ps[:, OUT0 + k, :], scalar=0.5, in1=tiles,
                                             op0=ALU.mult, op1=ALU.add).then_inc(x_updated, 1)

            def norm_before(g, c, m, j):
                if m == 2:
                    if j == 0:
                        dve.wait_ge(x_updated, 2 * g)
                        dve.nop(nofuse=True)
                    for tt in (2 * j, 2 * j + 1):
                        tile_stats(c - 1, tt, 0, tt == CT - 1)
                if (m, j) == (3, 0):
                    aggregate(c + 3, 0)
                if m == 4:
                    layer_norm(c + 3, c - 1, tiles=range(2 * j, 2 * j + 2))

            def ffn_chunk(g, c, f, first, turns=False):
                need(dve, mask_turned, g)
                dve.tensor_copy(cm_pad[:, :, 0:MASK_ROWS], cm[:, ds(CT * c, CT), :]).then_inc(cm_padded, 1)
                if turns:
                    layer_norm_low(c + 2, c - 2, (D1, D2))
                dve.wait_ge(mask_high, g + 1)
                low(dve, maskT_l[:], ps[:, BU, :], maskT_h[:]).then_inc(mask_ready, 1)
                dve.wait_ge(low_rank, 2 * g + 2)
                for s in range(4):
                    dve.wait_ge(spread_kept, 6 * g + s + 1)
                    dst = (up_act, hid)[s % 2][:, s // 2]
                    dve.tensor_tensor(dst, ps[:, L0 + s % 2, :], spread[:, s], ALU.mult).then_inc(um_raw, 1)
                for s in range(3):
                    dve.wait_ge(um_high, 4 * g + s + 1)
                    low(dve, um_l[:, s], (up_act, hid)[s % 2][:, s // 2], um_h[:, s]).then_inc(um_ready, 1)
                def weigh_base_gate(g, m, j):
                    rows = P if m < FULL else TAIL
                    if m < FULL:
                        src, c_j = ps[:, BG, :], spread[:, EX_C1 + j]
                    else:
                        src, c_j = ps[TAIL:2 * TAIL, BU, :], spread[TAIL:2 * TAIL, EX_C1 + j]
                    if m == 0:
                        dve.wait_ge(spread_kept, 6 * g + 5 + j)
                    dve.tensor_tensor(base_gate[0:rows, j], src, c_j, ALU.mult).then_inc(base_gate_kept, 1)

                for m in range(HT):
                    rows = P if m < FULL else TAIL
                    dve.wait_ge(base_done, 11 * g + min(2 * m + 2, 11))
                    weigh_base_gate(g, m, 0)
                    if m > 0:
                        weigh_base_gate(g, m, 1)
                    dve.wait_ge(base_up_kept, 6 * g + m + 1)
                    for j in range(2):
                        if m < FULL:
                            up_src, gate_src, n = ps[:, L0, :], ps[:, L1, :], 22 * g + 4 * m + 2 * j + 1
                        else:
                            up_src, gate_src, n = ps[0:TAIL, L0 + j, :], ps[TAIL:2 * TAIL, L0 + j, :], 22 * g + 21 + j
                        dve.wait_ge(lora_done, n)
                        dve.tensor_tensor(up_act[0:rows, j], up_src, base_up[0:rows, m % 2], ALU.add).then_inc(up_summed, 1)
                        if m < FULL:
                            dve.wait_ge(lora_done, n + 1)
                        dve.wait_ge(base_gate_kept, 12 * g + 2 * m + j + 1)
                        if m == 0 and j == 1:
                            dve.wait_ge(um_ready_pool, g + 1)
                        need(dve, hid_ready, 11 * g if m == 0 else 11 * g + 2 * m + j - 1)
                        if m > 0:
                            dve.wait_ge(mixed_done, 5 * g + m)
                        dve.tensor_tensor(hid[0:rows, j], gate_src, base_gate[0:rows, j], ALU.add).then_inc(gate_summed, 1)
                        if (m, j) == (0, 0):
                            weigh_base_gate(g, 0, 1)
                        dve.wait_ge(up_act_done, 12 * g + 2 * m + j + 1)
                        dve.wait_ge(gate_summed, 12 * g + 2 * m + j + 1)
                        dve.tensor_tensor(hid[0:rows, j], up_act[0:rows, j], hid[0:rows, j], ALU.mult).then_inc(hid_done, 1)
                        if not first and m == 1:
                            update_x(g - 1, c - 1, (j,))
                        if f == 0 and not first:
                            norm_before(g, c, m, j)
                    if m == FULL:
                        dve.wait_ge(mixed_ready, 5 * g + 5)
                        dve.wait_ge(hid_done, 12 * g + 12)
                        dve.tensor_tensor(mixed[0:rows], hid[0:rows, 0], hid[0:rows, 1], ALU.add).then_inc(tail_mixed, 1)
                        dve.wait_ge(hid_high, 12 * g + 12)
                        low(dve, hid_l[0:rows, m % 2, 1], hid[0:rows, 1], hid_h[0:rows, m % 2, 1]).then_inc(tail_ready, 1)
                        dve.wait_ge(mixed_high, 6 * g + 6)
                        low(dve, mixed_l[0:rows, m % 2], mixed[0:rows], mixed_h[0:rows, m % 2]).then_inc(tail_ready, 1)
                dve.wait_ge(down_a_done, g + 1)
                for j in range(2):
                    ins = dve.tensor_tensor(base_gate[:, j], ps[:, D1 + j, :], spread[:, (EX_M1, EX_M2)[j]], ALU.mult)
                ins.then_inc(dm_parts, 1)
                dve.wait_ge(dm_parts, g + 1)
                dve.tensor_tensor(base_gate[:, 0], base_gate[:, 0], base_gate[:, 1], ALU.add).then_inc(dm_raw, 1)
                dve.wait_ge(dm_high, g + 1)
                low(dve, dm_l[:], base_gate[:, 0], dm_h[:]).then_inc(dm_ready, 1)

            def ffn(f):
                if f == 0:
                    dve.memset(cm_pad[:], 0.0)
                    for c in range(CHUNKS + 1):
                        if c < CHUNKS:
                            dve.wait_ge(x_loaded[c], 16)
                            if c == 0:
                                dve.wait_ge(consts_made, 5)
                            layer_norm_stats(c, c, c % 2)
                        if c > 0:
                            layer_norm(c - 1, c - 1, (c - 1) % 2, xn_of(c - 1), min(c - 1, 1))
                        if c > 1:
                            layer_norm_low(c - 2, c - 2, LN_BANKS[c - 2])
                else:
                    dve.wait_ge(y_added, 8 * PAIRS)
                    dve.nop(nofuse=True)
                    last = 2 * CHUNKS + EARLY_NORMS
                    layer_norm_stats(last, EARLY_NORMS, EARLY_NORMS % 2)
                    dve.memset(cm_pad[:], 0.0)
                    layer_norm_low(last - 1, EARLY_NORMS - 1, LN_BANKS[EARLY_NORMS - 1])
                    layer_norm(last, EARLY_NORMS, EARLY_NORMS % 2, xn_of(EARLY_NORMS), 1)
                layer_norm_low(8 * f + CHUNKS - 1, CHUNKS - 1, LN_BANKS[CHUNKS - 1])
                router(f)
                ffn_chunk(4 * f, 0, f, True)
                if f == 0:
                    ffn_chunk(1, 1, f, False)
                with dve.Fori(2 - f, CHUNKS) as c:
                    ffn_chunk(c + 4 * f, c, f, False, f == 0)
                if f == 0:
                    layer_norm_low(2 * CHUNKS - 2, CHUNKS - 2, (D1, D2))
                update_x(4 * f + 3, CHUNKS - 1)

            def split_pair(kind, p):
                dve.wait_ge(wa_high[kind], p + 1)
                low(dve, wa_l[kind][:].rearrange("p a b -> p (a b)"), w_raw[RAW_OF[kind]][:],
                    wa_h[kind][:].rearrange("p a b -> p (a b)")).then_inc(wa_ready[kind], 1)

            def rope_cos(index, k, bank):
                dve.wait_ge(proj_done, index + 1)
                need(dve, proj_ready, index - 1)
                dve.tensor_tensor(rot[:, k % 2], ps[:, bank, :], rope[:, 0, 512 * (k // 2):512 * (k // 2) + 512],
                                  ALU.mult).then_inc(proj_cos, 1)

            def rope_sum(index, k):
                dve.wait_ge(proj_cos, index + 1)
                dve.wait_ge(proj_sin, index + 1)
                dve.tensor_tensor(rot[:, k % 2], rot[:, k % 2], rot_sin[:], ALU.add).then_inc(proj_rot, 1)

            def value_low(index, b, k, bank):
                dve.wait_ge(v_high, index + 1)
                low(dve, v_l[:, b, 2 * k:2 * k + 2, :].rearrange("p a b -> p (a b)"), ps[:, bank, :],
                    v_h[:, b, 2 * k:2 * k + 2, :].rearrange("p a b -> p (a b)")).then_inc(v_ready, 1)

            def invert_sum(p, t, first):
                tile = tile_of_step(p, t, 1, first)
                if tile:
                    q, s = tile
                    dve.wait_ge(exp_done, STEPS * q + s + 1)
                    dve.reciprocal(inv_sum[:, s % 4:s % 4 + 1], row_sum[:, s % 4:s % 4 + 1]).then_inc(inv_done, 1)

            def norm_early(n, c, d):
                k = c % 2
                if d == STATS_AT[c]:
                    dve.wait_ge(y_added, 8 * PAIRS - (6, 4, 2)[c])
                    dve.nop(nofuse=True)
                for tt in range(CT):
                    if d == STATS_AT[c] + tt * STATS_STEP[c]:
                        tile_stats(c, tt, k, tt == CT - 1)
                if d == STATS_AT[c] + CT * STATS_STEP[c]:
                    aggregate(n, k)
                if d == NORM_AT[c]:
                    if c == 0:
                        dve.wait_ge(proj_ready, UNITS * 4 * PAIRS)
                        dve.wait_ge(scores_done, STEPS * PAIRS - SEQ_TILES)
                    elif c == 1:
                        dve.wait_ge(scores_done, STEPS * PAIRS)
                    layer_norm(n, c, k, xn_of(c), min(c, 1))
                if d == TURN_AT[c] + 1:
                    layer_norm_low(n, c, LN_BANKS[c])

            def attention(p, first, last):
                for t in range(STEPS + (DRAIN_STEPS if last else 0)):
                    y = out_of_step(p, t, OUT_LAG + 1, first)
                    if y:
                        b, c, index, _ = y
                        tiles = x_sb[:, SEQ_TILES * b + 2 * c:SEQ_TILES * b + 2 * c + 2, :].rearrange("p a d -> p (a d)")
                        dve.wait_ge(y_done, index + 1)
                        need(dve, y_added, index - 3)
                        dve.tensor_tensor(tiles, ps[:, misc_bank(t - 1), :], tiles, ALU.add).then_inc(y_added, 1)
                    turn = rotation_to_end(p, t, first, last)
                    if turn:
                        rope_sum(turn[2], turn[3])
                    if t % 2 == 1:
                        invert_sum(p, t, first)
                    if t < STEPS:
                        view, a, n = score_view(t % 2, t % SEQ_TILES)
                        dve.wait_ge(scores_done, STEPS * p + t + 1)
                        dve.nop(nofuse=True)
                        dve.tensor_tensor_reduce(out=view, in0=view,
                                                 in1=causal[:, SEQ - a * n:].rearrange("p (a n) -> p a n", a=a),
                                                 scale=-SCALE, scalar=HUGE, op0=ALU.add, op1=ALU.min,
                                                 accum_out=neg_max[:, t % 4:t % 4 + 1]).then_inc(max_done, 1)
                    if first and t < 2:
                        rope_sum(2 + t, 2 + t)
                        rope_low_part(dve, 2 + t, 0, 2 + t)
                    if first and t == 0:
                        layer_norm_low(2 * CHUNKS - 1, CHUNKS - 1)
                    tile = tile_of_step(p, t, T_LAG + 1, first)
                    if tile:
                        q, s = tile
                        i = s % SEQ_TILES
                        half = P * (i % 2)
                        for n, (slot, count) in enumerate(tile_groups(i)):
                            dve.wait_ge(pT_high, groups_before(q, s) + n + 1)
                            bank = T_BANK + (GROUPS_AT[i] + n) % 2
                            low(dve, pT_l[i // 2 % 2][:, slot:slot + count, half:half + P],
                                ps[:, bank, 0:P * count].rearrange("p (a b) -> p a b", a=count),
                                pT_h[i // 2 % 2][:, slot:slot + count, half:half + P]).then_inc(pT_ready, 1)
                    side = side_work(p, t, first, last)
                    if side and side[0] == "proj":
                        rope_cos(side[2], side[3], misc_bank(t))
                    elif side:
                        value_low(side[2], side[1], side[3], misc_bank(t))
                    chunk = chunk_of_step(p, t, PV_LAG + 1, first)
                    if chunk:
                        u, c, index, _, _ = chunk
                        h, l = ((oA_h[:, 256 * c:256 * c + 256], oA_l[:, 256 * c:256 * c + 256]) if u % 2 == 0
                                else (oB_h[:, c % 2], oB_l[:, c % 2]))
                        dve.wait_ge(o_high, index + 1)
                        low(dve, l, ps[:, PV_BANK, 0:256], h).then_inc(o_ready, 1)
                    if t % 2 == 0:
                        invert_sum(p, t, first)
                    for kind, at in PAIR_SPLITS_AT.items():
                        if t == at + 1 and (kind == "o" or not last):
                            split_pair(kind, p + (kind != "o"))
                    if last:
                        for c in range(EARLY_NORMS):
                            norm_early(2 * CHUNKS + c, c, t - STEPS)

            ffn(0)
            for kind in "kq":
                split_pair(kind, 0)
            dve.wait_ge(rope_loaded, 16)
            rope_cos(0, 0, 0)
            rope_cos(1, 1, 1)
            dve.wait_ge(x_updated, 2 * CHUNKS)
            layer_norm_stats(2 * CHUNKS - 1, CHUNKS - 1)
            rope_sum(0, 0)
            rope_low_part(dve, 0, 0, 0)
            rope_sum(1, 1)
            rope_cos(2, 2, 2)
            rope_low_part(dve, 1, 0, 1)
            rope_cos(3, 3, 3)
            split_pair("v", 0)
            layer_norm(2 * CHUNKS - 1, CHUNKS - 1, dst=xn_last)
            attention(0, True, False)
            with dve.Fori(1, PAIRS - 1) as p:
                attention(p, False, False)
            attention(PAIRS - 1, False, True)
            ffn(1)

        @block.tensor
        def _(pe):
            def product(dst, w, x, start, stop, skip=False):
                pe.matmul(dst, w[0], x[0], start=start, stop=False, skip_group_check=skip)
                pe.matmul(dst, w[0], x[1], start=False, stop=False, skip_group_check=skip)
                return pe.matmul(dst, w[1], x[0], start=False, stop=stop, skip_group_check=skip)

            def xnT(kt, cols):
                return xnT_h[:, kt, cols], xnT_l[:, kt, cols]

            def layer_norm(n, src=xn, banks=(OUT0, OUT1)):
                pe.wait_ge(xn_ready, n + 1)
                for kt in range(KT):
                    if banks == (OUT0, OUT1):
                        need(pe, xnT_ready, KT * n - (KT - 1) + kt)
                    for tt in range(CT):
                        ins = pe.transpose(ps[:, banks[kt], P * tt:P * tt + P], src[:, tt, P * kt:P * kt + P], ident[:])
                    ins.then_inc(xn_turned, 1)

            def router_logits(f, c):
                pe.wait_ge(w_ready, SPLITS * f + 1)
                pe.wait_ge(xnT_ready, KT * (8 * f + c + 1))
                if c == 3:
                    pe.wait_ge(logitsT_kept, 4 * f + 1)
                for kt in range(KT):
                    product(ps[:, LOGIT_BANKS[c], :], (w_route(w_h, kt), w_route(w_l, kt)), xnT(kt, chunk_cols(c)), kt == 0, False)
                    ins = pe.matmul(ps[:, LOGIT_BANKS[c], :], w_route(w_l, kt), xnT_l[:, kt, chunk_cols(c)], start=False,
                                    stop=(kt == KT - 1))
                ins.then_inc(logitsT_done, 1)

            def turn_logits(f, chunks):
                for c in chunks:
                    pe.wait_ge(logitsT_kept, 4 * f + c + 1)
                    for tt in range(CT):
                        at = EXPERTS * (CT * c + tt)
                        ins = pe.transpose(ps[:, TURNED_BANKS[c], at:at + EXPERTS], logitsT(c)[:, P * tt:P * tt + P],
                                           ident[0:EXPERTS, 0:EXPERTS])
                ins.then_inc(logits_ready, 1)

            def down_b(g):
                pe.wait_ge(dm_ready, g + 1)
                for tt in range(CT):
                    cols = slice(P * tt, P * tt + P)
                    ins = product(ps[:, OUT0 + tt // 2, D * (tt % 2):D * (tt % 2) + D], (dm_h[:, cols], dm_l[:, cols]),
                                  (w_down_b(w_h), w_down_b(w_l)), False, True, skip=True)
                    if tt % 2 == 1:
                        ins.then_inc(out_done, 1)

            def low_rank_products(g, c, gates=(0, 1)):
                need(pe, up_summed, 12 * g)
                need(pe, gate_summed, 12 * g)
                for gate in gates:
                    for kt in range(KT):
                        ins = product(ps[:, L0 + gate, :], (w_a(w_h, kt, gate), w_a(w_l, kt, gate)),
                                      xnT(kt, chunk_cols(c)), kt == 0, kt == KT - 1)
                    ins.then_inc(low_rank, 1)

            def turn_before(n, g):
                pe.wait_ge(dm_parts, g)
                layer_norm(n, xn, (D1, D2))

            def ffn_chunk(g, c, f, first, turns=False):
                cols = chunk_cols(c)

                def base(bank, tile):
                    for kt in range(KT):
                        ins = product(ps[:, bank, :], (w_base(w_h, kt, tile), w_base(w_l, kt, tile)), xnT(kt, cols),
                                      kt == 0, kt == KT - 1)
                    ins.then_inc(base_done, 1)

                if first:
                    base(BG, FULL)
                else:
                    low_rank_products(g, c, (0,))
                    if turns:
                        turn_before(c + 2, g)
                    low_rank_products(g, c, (1,))
                pe.wait_ge(cm_padded, g + 1)
                need(pe, base_up_kept, 6 * g)
                need(pe, base_gate_kept, 12 * g)
                for tt in range(CT):
                    ins = pe.transpose(ps[:, BU, P * tt:P * tt + P], cm_pad[:, tt, :], ident[:])
                ins.then_inc(mask_turned, 1)
                if not first:
                    base(BG, FULL)
                pe.wait_ge(mask_ready, g + 1)
                for e in range(EX_C2 + 1):
                    bank = SPREAD_BANKS[e]
                    if turns and e == 1:
                        pe.wait_ge(xnT_ready, KT * (c + 3))
                    if e >= 3:
                        pe.wait_ge(spread_kept, 6 * g + e - 2)
                    if e in (EX_M1, EX_M2):
                        pe.matmul(ps[:, bank, :], expand[:, e], maskT_h[:], start=True, stop=True).then_inc(spread_done, 1)
                    else:
                        pe.matmul(ps[:, bank, :], expand[:, e], maskT_h[:], start=True, stop=False)
                        pe.matmul(ps[:, bank, :], expand[:, e], maskT_l[:], start=False, stop=True).then_inc(spread_done, 1)

                def lora(bank, tile, s, start=True, stop=True):
                    return product(ps[:, bank, :], (w_lora(w_h, tile), w_lora(w_l, tile)), (um_h[:, s], um_l[:, s]), start, stop)

                def down_a(m, j):
                    if m == FULL and j == 1:
                        pe.wait_ge(tail_ready, 2 * g + 1)
                    else:
                        pe.wait_ge(hid_ready, 11 * g + 2 * m + j + 1)
                    if m == 0 and j == 0:
                        pe.wait_ge(spread_kept, 6 * g + 6)
                    return product(ps[:, D1 + j, :], (w_down_a(w_h, m), w_down_a(w_l, m)),
                                   (hid_h[:, m % 2, j], hid_l[:, m % 2, j]), m == 0, m == HT - 1)

                def down(m):
                    if m < FULL:
                        pe.wait_ge(mixed_ready, 5 * g + m + 1)
                    else:
                        pe.wait_ge(tail_ready, 2 * g + 2)
                    if m == 0:
                        if first:
                            pe.wait_ge(xnT_ready, (2 * f + 1) * KT * CHUNKS)
                        else:
                            pe.wait_ge(x_updated, 2 * g)
                    for tt in range(CT):
                        tok = slice(P * tt, P * tt + P)
                        ins = product(ps[:, OUT0 + tt // 2, D * (tt % 2):D * (tt % 2) + D],
                                      (mixed_h[:, m % 2, tok], mixed_l[:, m % 2, tok]),
                                      (w_down(w_h, m), w_down(w_l, m)), m == 0 and tt % 2 == 0, False, skip=True)
                    return ins

                for m in range(HT):
                    if m == 0:
                        pe.wait_ge(spread_kept, 6 * g + 4)
                    else:
                        pe.wait_ge(base_up_kept, 6 * g + m)
                    if m < FULL:
                        base(BU, m)
                        if m > 0:
                            pe.wait_ge(base_gate_kept, 12 * g + 2 * m)
                            base(BG, FULL + m)
                        elif not first:
                            down_b(g - 1)
                        if m >= 2:
                            down(m - 2)
                        for j in range(2):
                            if m == 0:
                                pe.wait_ge(um_ready, 3 * g + 2 + j)
                                if j == 0:
                                    pe.wait_ge(um_raw, 4 * g + 4)
                            if first and m == 1 and j == 0:
                                pe.wait_ge(w_ready, SPLITS * (f + 1))
                            if m > 0 or j > 0:
                                pe.wait_ge(up_summed, 12 * g + 2 * m + j)
                            lora(L0, m, 2 * j).then_inc(lora_done, 1)
                            if m == 0 and j == 1:
                                pe.wait_ge(um_ready_pool, g + 1)
                            if m > 0 or j > 0:
                                pe.wait_ge(gate_summed, 12 * g + 2 * m + j)
                            lora(L1, FULL + m, 2 * j + 1).then_inc(lora_done, 1)
                            if m > 0:
                                down_a(m - 1, j)
                    else:
                        base(BU, 2 * FULL)
                        for j in range(2):
                            pe.wait_ge((up_summed, gate_summed)[j], 12 * g + 2 * m)
                            lora(L0 + j, 2 * FULL, 2 * j, True, False)
                            lora(L0 + j, 2 * FULL + 1, 2 * j + 1, False, True).then_inc(lora_done, 1)
                            down_a(m - 1, j)
                down(HT - 3).then_inc(mixed_used, 1)
                down(HT - 2)
                down_a(HT - 1, 0)
                down_a(HT - 1, 1).then_inc(down_a_done, 1)
                down(HT - 1)

            def ffn(f):
                if f == 0:
                    pe.wait_ge(consts_made, 5)
                if f == 0:
                    for c in range(CHUNKS):
                        layer_norm(c, xn_of(c), LN_BANKS[c])
                        if c > 0:
                            router_logits(f, c - 1)
                else:
                    for c in range(EARLY_NORMS):
                        router_logits(f, c)
                    pe.wait_ge(y_added, 8 * PAIRS)
                    layer_norm(2 * CHUNKS + EARLY_NORMS, xn_of(EARLY_NORMS), LN_BANKS[EARLY_NORMS])
                turn_logits(f, range(CHUNKS - 1))
                router_logits(f, CHUNKS - 1)
                low_rank_products(4 * f, 0, (0,))
                turn_logits(f, range(CHUNKS - 1, CHUNKS))
                low_rank_products(4 * f, 0, (1,))
                pe.wait_ge(w_ready, SPLITS * f + EARLY_SPLITS)
                pe.wait_ge(expand_ready, f + 1)
                ffn_chunk(4 * f, 0, f, True)
                if f == 0:
                    ffn_chunk(1, 1, f, False)
                with pe.Fori(2 - f, CHUNKS) as c:
                    ffn_chunk(c + 4 * f, c, f, False, f == 0)
                if f == 0:
                    turn_before(2 * CHUNKS - 2, CHUNKS)
                down_b(4 * f + 3)

            bank_user = {}

            def bank_free(bank):
                if bank in bank_user:
                    kind, index = bank_user[bank]
                    pe.wait_ge({"proj": proj_swapped, "v": v_ready, "o": y_added}[kind], index + 1)
                elif bank == MISC_BANKS[-1]:
                    pe.wait_ge(xnT_ready, KT * 2 * CHUNKS)

            def project(index, u, k, bank):
                kind = "kq"[k % 2]
                h, l = wa_h[kind], wa_l[kind]
                head, b, at = u % 2, u // 2, 512 * (k // 2)
                cols = slice(SEQ * b + at, SEQ * b + at + 512)
                bank_free(bank)
                bank_user[bank] = "proj", index
                for kt in range(KT):
                    w = (h[:, kt, HD * head:HD * head + HD], l[:, kt, HD * head:HD * head + HD])
                    ins = product(ps[:, bank, :], w, xnT(kt, cols), kt == 0, kt == KT - 1)
                ins.then_inc(proj_done, 1)

            def values(index, b, k, bank):
                bank_free(bank)
                for half in range(2):
                    tok = SEQ * b + P * (2 * k + half)
                    for kt in range(KT):
                        ins = product(ps[:, bank, 256 * half:256 * half + 256], xnT(kt, slice(tok, tok + P)),
                                      (wa_h["v"][:, kt, :], wa_l["v"][:, kt, :]), kt == 0, kt == KT - 1)
                ins.then_inc(v_done, 1)
                bank_user[bank] = "v", index

            def side(p, t, first, last):
                work = side_work(p, t, first, last)
                if not work:
                    return
                kind, what, index, k = work
                if kind == "proj":
                    if t >= STEPS - SEQ_TILES and k < 2:
                        pe.wait_ge(wa_ready["kq"[k % 2]], p + 2)
                    project(index, what, k, misc_bank(t))
                else:
                    if first and t < SEQ_TILES and k == 0:
                        pe.wait_ge(wa_ready["v"], 1)
                    if t >= STEPS - SEQ_TILES and k == 0:
                        pe.wait_ge(wa_ready["v"], p + 2)
                    values(index, what, k, misc_bank(t))

            def scores(p, t, first):
                u, i = unit_of(t)
                view, a, n = score_view(t % 2, i)
                if not (first and t < 2):
                    pe.wait_ge(exp_done, STEPS * p + t - 1)
                elif t == 1:
                    pe.wait_ge(proj_swapped, 3)
                if i in (4, 5):
                    bank_free(2 * (t % 2) + 1)
                if i % 4 == 0:
                    pe.wait_ge(proj_ready, 4 * (UNITS * p + u) + 2 + i // 2)
                for part_at in range(a):
                    cols = max(n, 256)
                    dst = ps[:, 2 * (t % 2) + part_at, 0:cols]
                    keys = slice(n * part_at, n * part_at + cols)
                    rows = slice(P * i, P * i + P)
                    ins = product(dst, (qT_h[:, u % 2, rows], qT_l[:, u % 2, rows]),
                                  (kT_h[:, u % 2, keys], kT_l[:, u % 2, keys]), True, True)
                ins.then_inc(scores_done, 1)

            def turn(q, s):
                i = s % SEQ_TILES
                pe.wait_ge(probs_ready, STEPS * q + s + 1)
                for n, (slot, count) in enumerate(tile_groups(i)):
                    need(pe, pT_ready, groups_before(q, s) + n - 1)
                    bank = T_BANK + (GROUPS_AT[i] + n) % 2
                    for k in range(count):
                        kt = 2 * (i // 2) + 1 - (slot + k)
                        ins = pe.transpose(ps[:, bank, P * k:P * k + P], probs[s % 4][:, P * kt:P * kt + P], ident[:])
                    ins.then_inc(turned, 1)

            def weigh(u, c, index, q, s, first_unit):
                pe.wait_ge(pT_ready, groups_through(q, s))
                need(pe, o_ready, index)
                if first_unit:
                    pe.wait_ge(v_ready, c + 1)
                elif c == 0 and u % 2 == 0:
                    pe.wait_ge(v_ready, 4 * (2 * q + u // 2) + 4)
                if first_unit and c == 0:
                    pe.wait_ge(zeroed, 1)
                head, b = u % 2, u // 2
                slots = 2 * c + 2
                for slot in range(slots):
                    kt = 2 * c + 1 - slot
                    w = tuple(v[:, b, kt, HD * head:HD * head + HD] for v in (v_h, v_l))
                    ins = product(ps[:, PV_BANK, 0:256], w, (pT_h[c % 2][:, slot, :], pT_l[c % 2][:, slot, :]),
                                  slot == 0, slot == slots - 1)
                ins.then_inc(pv_done, 1)

            def project_out(b, c, index, q, bank):
                if c == 0 and b == 0:
                    pe.wait_ge(wa_ready["o"], q + 1)
                pe.wait_ge(o_ready, 16 * q + 8 * b + 4 + c + 1)
                bank_free(bank)
                for half in range(2):
                    at = slice(256 * c + P * half, 256 * c + P * half + P)
                    for head in range(2):
                        o = ((oA_h[:, at], oA_l[:, at]) if head == 0 else
                             tuple(v[:, c % 2, P * half:P * half + P] for v in (oB_h, oB_l)))
                        ins = product(ps[:, bank, 256 * half:256 * half + 256], o,
                                      (wa_h["o"][:, head, :], wa_l["o"][:, head, :]), head == 0, head == 1)
                ins.then_inc(y_done, 1)
                bank_user[bank] = "o", index

            def attention(p, first, last):
                if not first:
                    bank_user.update({1: ("proj", 16 * p), 3: ("v", 8 * p + 1), 7: ("v", 8 * p + 3)})
                for t in range(STEPS + (DRAIN_STEPS if last else 0)):
                    if t < STEPS:
                        scores(p, t, first)
                    side(p, t, first, last)
                    if first and t == 0:
                        layer_norm(2 * CHUNKS - 1, xn_last)
                    chunk = chunk_of_step(p, t, PV_LAG, first)
                    if chunk:
                        weigh(*chunk, first and chunk[0] == 0)
                    y = out_of_step(p, t, OUT_LAG, first)
                    if y:
                        project_out(*y, misc_bank(t))
                    tile = tile_of_step(p, t, T_LAG, first)
                    if tile:
                        turn(*tile)
                    for c in range(EARLY_NORMS if last else 0):
                        if t == STEPS + TURN_AT[c]:
                            if c == 0:
                                pe.wait_ge(exp_done, STEPS * PAIRS)
                            if c == 2:
                                pe.wait_ge(pT_ready, UNITS * UNIT_GROUPS * PAIRS)
                            layer_norm(2 * CHUNKS + c, xn_of(c), LN_BANKS[c])

            ffn(0)
            for k in range(4):
                if k < 2:
                    pe.wait_ge(wa_ready["kq"[k]], 1)
                project(k, 0, k, k)
            attention(0, True, False)
            with pe.Fori(1, PAIRS - 1) as p:
                attention(p, False, False)
            attention(PAIRS - 1, False, True)
            ffn(1)


def pack_ffn(gate_w, w_up, w_gate, w_down, up_A, up_B, gate_A, gate_B, down_A, down_B):
    def by_kt(a):
        return a.reshape(KT, P, -1).transpose(1, 0, 2)

    def padded(a):
        full = np.zeros((HT * P, a.shape[1]), a.dtype)
        full[:HIDDEN] = a
        return full.reshape(HT, P, -1).transpose(1, 0, 2)

    cut = FULL * P
    a = np.concatenate([up_A.reshape(ER, D).T, gate_A.reshape(ER, D).T], axis=1)
    up, gate = w_up.T, w_gate.T
    base = np.concatenate([up[:, :cut], gate[:, :cut], up[:, cut:], gate[:, cut:]], axis=1)
    up_b = up_B.transpose(0, 2, 1).reshape(ER, HIDDEN)
    gate_b = gate_B.transpose(0, 2, 1).reshape(ER, HIDDEN)
    none = np.zeros((ER, TAIL), up_b.dtype)
    lora = np.concatenate([up_b[:, :cut], gate_b[:, :cut], up_b[:, cut:], none, none, gate_b[:, cut:]], axis=1)
    parts = [by_kt(a), by_kt(gate_w.T), by_kt(base), lora, padded(down_A.reshape(ER, HIDDEN).T),
             padded(w_down.T), down_B.transpose(0, 2, 1).reshape(ER, D)]
    return np.ascontiguousarray(np.concatenate([v.reshape(P, -1) for v in parts], axis=1))


def expand_matrices():
    m = np.zeros((P, 6, P), np.float32)
    for e in range(EXPERTS):
        ranks = slice(RANK * e, RANK * e + RANK)
        m[e, EX_M1, ranks] = ALPHA
        m[EXPERTS + e, EX_M2, ranks] = ALPHA
        m[2 * EXPERTS + e, EX_CM1, ranks] = ALPHA
        m[3 * EXPERTS + e, EX_CM2, ranks] = ALPHA
        m[2 * EXPERTS + e, EX_C1, :] = 1.0
        m[3 * EXPERTS + e, EX_C2, :] = 1.0
    return m.reshape(P, EX_COLS)


def rope_tables():
    half = HD // 2
    fraction = np.float32(2.0) * np.arange(half, dtype=np.float32) / np.float32(HD)
    timescale = np.float32(10000.0) ** fraction
    angle = np.arange(SEQ, dtype=np.float32)[None, :] / timescale[:, None].astype(np.float32)
    sin, cos = np.sin(angle), np.cos(angle)
    table = np.stack([np.concatenate([cos, cos]), np.concatenate([-sin, sin])], axis=1)
    return np.ascontiguousarray(table.astype(np.float32))


def pack_attention(wq, wk, wv, wo):
    order = np.concatenate([np.arange(0, HD, 2), np.arange(1, HD, 2)])

    def by_pair(w):
        w = w.reshape(KT, P, PAIRS, 2, HD).transpose(2, 1, 0, 3, 4)
        return w.reshape(PAIRS, P, KT * 2 * HD)

    o = wo.reshape(PAIRS, 2, HD, D).transpose(0, 2, 1, 3).reshape(PAIRS, P, 2 * D)
    return np.ascontiguousarray(np.stack([by_pair(wv), by_pair(wk[:, :, order]), by_pair(wq[:, :, order]), o], axis=1))


def kernel(**inputs):
    import concourse.bacc as _bacc
    from concourse.bass_utils import run_bass_kernel_spmd as _run

    given = {k: np.asarray(v) for k, v in inputs.items()}
    ffn = [given[f"L0_ffn_{n}"] for n in ("gate_w", "w_up", "w_gate", "w_down", "up_A", "up_B", "gate_A", "gate_B",
                                           "down_A", "down_B")]
    arrays = {
        "x_in": np.ascontiguousarray(given["L0_attn_x"].reshape(TOKENS, D)),
        "ffn_w": pack_ffn(*ffn),
        "expand_w": expand_matrices(),
        "attn_w": pack_attention(*[given[f"L0_attn_{n}"] for n in ("wq", "wk", "wv", "wo")]),
        "rope_w": rope_tables(),
    }
    nc = _bacc.Bacc("TRN2", target_bir_lowering=False, num_devices=1)
    args = [nc.dram_tensor(n, a.shape, mybir.dt.from_np(a.dtype), kind="ExternalInput").ap() for n, a in arrays.items()]
    out = nc.dram_tensor("out", (TOKENS, D), F32, kind="ExternalOutput").ap()
    build(nc, *args, out)
    got = _run(nc, [arrays], core_ids=[0])
    return got.results[0]["out"].reshape(BATCH, SEQ, D)
```
